# Optimizing a Trainium2 kernel written in Bass

```python
import numpy as np
import jax
import jax.numpy as jnp

def _softmax(x, axis=-1):
    return jax.nn.softmax(x, axis=axis)

def _gelu(x):
    return jax.nn.gelu(x, approximate=True)

def _silu(x):
    return jax.nn.silu(x)

def _sigmoid(x):
    return jax.nn.sigmoid(x)

def _layernorm(x, axis=-1, eps=1e-05):
    m = jnp.mean(x, axis=axis, keepdims=True)
    v = jnp.var(x, axis=axis, keepdims=True)
    return (x - m) / jnp.sqrt(v + eps)

def _scatter_add(tgt, idx, src, axis=0):
    return tgt.at[idx].add(src)

def _segment_sum(src, seg, n):
    return jax.ops.segment_sum(src, seg, n)
kernel_name = 'mk_adaln_d1_jaxref_r8_f4a0f6'

def setup_inputs(seed: int=0):
    np.random.seed(seed)
    _w = jnp.asarray

    def _L0_attn_setup():
        import jax, jax.numpy as jnp
        import numpy as np
        DIM = 256
        HEADS = 16
        DIM_HEAD = 128
        INNER = HEADS * DIM_HEAD

        def rotate_half(x):
            x1, x2 = jnp.split(x, 2, axis=-1)
            return jnp.concatenate((-x2, x1), axis=-1)

        def rotary_pos(n, dim_head, dtype):
            inv_freq = 1.0 / 10000.0 ** (jnp.arange(0, dim_head, 2, dtype=jnp.float32) / dim_head)
            seq = jnp.arange(n, dtype=jnp.float32)
            freqs = jnp.einsum('i,j->ij', seq, inv_freq)
            return jnp.concatenate((freqs, freqs), axis=-1).astype(dtype)

        def apply_rotary(pos, t):
            return t * jnp.cos(pos) + rotate_half(t) * jnp.sin(pos)
        key = jax.random.key(seed)
        ks = jax.random.split(key, 9)
        s = 0.02
        return {'x': jax.random.normal(ks[0], (2, 256, DIM), dtype=jnp.float32), 'Wq': jax.random.normal(ks[1], (DIM, INNER), dtype=jnp.float32) * s, 'bq': jnp.zeros((INNER,), dtype=jnp.float32), 'Wk': jax.random.normal(ks[2], (DIM, INNER), dtype=jnp.float32) * s, 'bk': jnp.zeros((INNER,), dtype=jnp.float32), 'Wv': jax.random.normal(ks[3], (DIM, INNER), dtype=jnp.float32) * s, 'bv': jnp.zeros((INNER,), dtype=jnp.float32), 'Wo': jax.random.normal(ks[4], (INNER, DIM), dtype=jnp.float32) * s, 'bo': jnp.zeros((DIM,), dtype=jnp.float32)}
    _L0_attn_in = _L0_attn_setup()

    def _L0_ffn_setup():
        import jax, jax.numpy as jnp
        import numpy as np
        DIM = 256
        HID = 704
        ZERO_POINT = 128.0

        def _qlinear(x, wq, scale):
            W = (wq.astype(jnp.float32) - ZERO_POINT) * scale[:, None]
            return jnp.einsum('bsd,hd->bsh', x, W)
        key = jax.random.key(seed)
        ks = jax.random.split(key, 7)
        B, S = (4, 256)
        sg = jax.random.uniform(ks[1], (HID,)) * (0.02 / np.sqrt(DIM)) + 0.0001
        su = jax.random.uniform(ks[3], (HID,)) * (0.02 / np.sqrt(DIM)) + 0.0001
        sd = jax.random.uniform(ks[5], (DIM,)) * (0.02 / np.sqrt(HID)) + 0.0001
        return {'x': jax.random.normal(ks[0], (B, S, DIM), dtype=jnp.float32), 'wq_gate': jax.random.randint(ks[2], (HID, DIM), 0, 32, dtype=jnp.int32), 's_gate': sg, 'wq_up': jax.random.randint(ks[4], (HID, DIM), 0, 32, dtype=jnp.int32), 's_up': su, 'wq_down': jax.random.randint(ks[6], (DIM, HID), 0, 32, dtype=jnp.int32), 's_down': sd}
    _L0_ffn_in = _L0_ffn_setup()
    _L0_c = _w((lambda *s: np.random.randn(*s).astype(np.float32) * 0.05)(2, 256))
    _L0_wmod = _w((lambda *s: np.random.randn(*s).astype(np.float32) * 0.05)(256, 6 * 256) * 256 ** (-0.5))
    _d = {'L0_attn_x': _L0_attn_in['x'], 'L0_attn_Wq': _L0_attn_in['Wq'], 'L0_attn_bq': _L0_attn_in['bq'], 'L0_attn_Wk': _L0_attn_in['Wk'], 'L0_attn_bk': _L0_attn_in['bk'], 'L0_attn_Wv': _L0_attn_in['Wv'], 'L0_attn_bv': _L0_attn_in['bv'], 'L0_attn_Wo': _L0_attn_in['Wo'], 'L0_attn_bo': _L0_attn_in['bo'], 'L0_ffn_wq_gate': _L0_ffn_in['wq_gate'], 'L0_ffn_s_gate': _L0_ffn_in['s_gate'], 'L0_ffn_wq_up': _L0_ffn_in['wq_up'], 'L0_ffn_s_up': _L0_ffn_in['s_up'], 'L0_ffn_wq_down': _L0_ffn_in['wq_down'], 'L0_ffn_s_down': _L0_ffn_in['s_down'], 'L0_c': _L0_c, 'L0_wmod': _L0_wmod}
    _x0 = _d['L0_attn_x']
    _d['L0_attn_x'] = jax.random.normal(jax.random.fold_in(jax.random.key(seed), 1), (2, 1024, 256), dtype=_x0.dtype)
    del _x0
    return _d

def reference(L0_attn_x, L0_attn_Wq, L0_attn_bq, L0_attn_Wk, L0_attn_bk, L0_attn_Wv, L0_attn_bv, L0_attn_Wo, L0_attn_bo, L0_ffn_wq_gate, L0_ffn_s_gate, L0_ffn_wq_up, L0_ffn_s_up, L0_ffn_wq_down, L0_ffn_s_down, L0_c, L0_wmod):

    def _L0_attn_ref(x, Wq, bq, Wk, bk, Wv, bv, Wo, bo):
        import jax, jax.numpy as jnp
        import numpy as np
        DIM = 256
        HEADS = 16
        DIM_HEAD = 128
        INNER = HEADS * DIM_HEAD

        def rotate_half(x):
            x1, x2 = jnp.split(x, 2, axis=-1)
            return jnp.concatenate((-x2, x1), axis=-1)

        def rotary_pos(n, dim_head, dtype):
            inv_freq = 1.0 / 10000.0 ** (jnp.arange(0, dim_head, 2, dtype=jnp.float32) / dim_head)
            seq = jnp.arange(n, dtype=jnp.float32)
            freqs = jnp.einsum('i,j->ij', seq, inv_freq)
            return jnp.concatenate((freqs, freqs), axis=-1).astype(dtype)

        def apply_rotary(pos, t):
            return t * jnp.cos(pos) + rotate_half(t) * jnp.sin(pos)
        b, n, _ = x.shape
        scale = DIM_HEAD ** (-0.5)

        def proj(W, bias):
            t = x @ W + bias
            return t.reshape(b, n, HEADS, DIM_HEAD).transpose(0, 2, 1, 3)
        q = proj(Wq, bq) * scale
        k = proj(Wk, bk)
        v = proj(Wv, bv)
        pos = rotary_pos(n, DIM_HEAD, x.dtype)
        q = apply_rotary(pos, q)
        k = apply_rotary(pos, k)
        sim = jnp.einsum('bhid,bhjd->bhij', q, k)
        causal = jnp.triu(jnp.ones((n, n), dtype=bool), k=1)
        sim = jnp.where(causal, -jnp.finfo(sim.dtype).max, sim)
        attn = jax.nn.softmax(sim, axis=-1)
        out = jnp.einsum('bhij,bhjd->bhid', attn, v)
        out = out.transpose(0, 2, 1, 3).reshape(b, n, INNER)
        return out @ Wo + bo

    def _L0_ffn_ref(x, wq_gate, s_gate, wq_up, s_up, wq_down, s_down):
        import jax, jax.numpy as jnp
        import numpy as np
        DIM = 256
        HID = 704
        ZERO_POINT = 128.0

        def _qlinear(x, wq, scale):
            W = (wq.astype(jnp.float32) - ZERO_POINT) * scale[:, None]
            return jnp.einsum('bsd,hd->bsh', x, W)
        gate = _qlinear(x, wq_gate, s_gate)
        gate = jax.nn.silu(gate)
        up = _qlinear(x, wq_up, s_up)
        return _qlinear(gate * up, wq_down, s_down)
    x = L0_attn_x
    mod = (_silu(L0_c) @ L0_wmod).reshape(L0_c.shape[0], 6, 1, -1)
    sa, ca, ga, sb, cb, gb = (mod[:, 0], mod[:, 1], mod[:, 2], mod[:, 3], mod[:, 4], mod[:, 5])
    ga = (2 * (ga >= 0) - 1) * jnp.maximum(jnp.abs(ga), 0.25)
    gb = (2 * (gb >= 0) - 1) * jnp.maximum(jnp.abs(gb), 0.25)
    h = _layernorm(x, axis=-1) * (1 + ca) + sa
    x = x + ga * _L0_attn_ref(h, L0_attn_Wq, L0_attn_bq, L0_attn_Wk, L0_attn_bk, L0_attn_Wv, L0_attn_bv, L0_attn_Wo, L0_attn_bo)
    h = _layernorm(x, axis=-1) * (1 + cb) + sb
    x = x + gb * _L0_ffn_ref(h, L0_ffn_wq_gate, L0_ffn_s_gate, L0_ffn_wq_up, L0_ffn_s_up, L0_ffn_wq_down, L0_ffn_s_down)
    return x

_drawn_inputs = setup_inputs


def setup_inputs(seed=0):
    import zlib

    import numpy as np

    out = dict(_drawn_inputs(seed))
    spreads = {'L0_attn_bq': (0.0, 0.8),
     'L0_attn_bk': (0.0, 0.8),
     'L0_attn_bv': (0.0, 0.346),
     'L0_attn_bo': (0.0, 0.331)}
    factors = {'L0_attn_Wq': 8.0,
     'L0_attn_Wk': 8.0,
     'L0_attn_Wv': 8.0,
     'L0_ffn_s_gate': 8.0,
     'L0_ffn_s_up': 8.0,
     'L0_ffn_s_down': 8.0}
    for name, (base, spread) in spreads.items():
        noise = np.random.default_rng([zlib.crc32(name.encode()), seed]).standard_normal(out[name].shape)
        drawn = base * np.exp(spread * noise) if base else spread * noise
        out[name] = jnp.asarray(drawn.astype(out[name].dtype))
    for name, factor in factors.items():
        out[name] = (out[name] * factor).astype(out[name].dtype)
    return out
```

```python
from contextlib import ExitStack

import numpy as np

import concourse.bass as bass
from concourse import mybir

F32 = mybir.dt.float32
F32R = mybir.dt.float32r
BF16 = mybir.dt.bfloat16
I32 = mybir.dt.int32
ALU = mybir.AluOpType
ACT = mybir.ActivationFunctionType
AX = mybir.AxisListType.X

P = 128
BATCH, SEQ, DIM = 2, 1024, 256
HEADS, DH = 16, 128
INNER = HEADS * DH
HID = 704
TOK = BATCH * SEQ
KT = DIM // P
NQ = SEQ // P
NTT = TOK // P
CH = 512
NCH = TOK // CH
HM = (HID + P - 1) // P
HLAST = HID - (HM - 1) * P
PAIRS = HEADS // 2
UNITS = 2 * BATCH
TILES = UNITS * NQ
EPS = 1e-5
SCALE = DH ** -0.5
ZERO_POINT = 128.0
MASKED = -3.0e38

ROW_BQ, ROW_BK, ROW_BV = 0, HEADS, 2 * HEADS
ROW_C = 3 * HEADS
ROW_SG = ROW_C + BATCH * KT
ROW_SU = ROW_SG + HM
NROWS = ROW_SU + HM

P_AT = [9, 7, 4, 0, 13, 7, 0, 13]
P_BLOCKS = 21

T_GROUPS = [(t + 4) // 4 for t in range(NQ)]
T_FIRST = [sum(T_GROUPS[:t]) for t in range(NQ)]
T_UNIT = sum(T_GROUPS)


class Step:

    def __init__(self, g):
        self.g = g
        self.scores = g if g < TILES else None
        self.turn = g - 2 if 2 <= g < TILES + 2 else None
        self.first, self.pv, self.late = None, None, []


def schedule(last):
    steps = [Step(g) for g in range(TILES + 4)]
    for u in range(UNITS):
        if not (last and u == UNITS - 1):
            for j, (which, c) in enumerate([(1, 0), (0, 0), (1, 1), (0, 1)]):
                steps[NQ * u + 2 * j + u % 2].first = ("qk", u + 1, which, c)
        for c, at in enumerate((6, 10)):
            steps[NQ * u + at].pv = ("pv", u, c)
        for c, at in enumerate((7, 12 if u < UNITS - 1 else 11)):
            steps[NQ * u + at].late += [("wo", u, c, 0), ("wo", u, c, 1)]
    for j in range(4):
        steps[NQ + 2 * j].first = ("v", 1, j)
        if not last:
            steps[TILES + j].first = ("v", 2, j)
    return steps


def in_order(steps):
    out = []
    for s in steps:
        out += [x for x in (s.first, s.pv, *s.late) if x]
    return out


PROLOGUE_PIECES = [("qk", 0, 1, 0), ("qk", 0, 0, 0), ("qk", 0, 1, 1), ("qk", 0, 0, 1)] + [("v", 0, j) for j in range(4)]


class Pass:

    def __init__(self, i, last):
        self.i, self.last = i, last
        self.steps = schedule(last)
        self.order = in_order(self.steps)
        self.full = in_order(schedule(False))
        self.qk = [x for x in self.order if x[0] == "qk"]
        self.v = [x for x in self.order if x[0] == "v"]
        self.pv = [x for x in self.order if x[0] == "pv"]
        self.wo = [x for x in self.order if x[0] == "wo"]

    def pieces(self, x):
        return self.i * len(self.full) + (len(PROLOGUE_PIECES) + self.order.index(x) + 1)

    def bank(self, x):
        return self.order.index(x) % 2

    def before(self, x):
        at = self.order.index(x)
        return self.order[at - 2] if at >= 2 else None

    def qks(self, x):
        return self.i * 16 + (4 + self.qk.index(x))

    def vs(self, x):
        return self.i * 8 + (4 + self.v.index(x))

    def pvs(self, x):
        return self.i * 8 + self.pv.index(x)

    def wos(self, x):
        return self.i * 16 + self.wo.index(x)

    def tiles(self, g):
        return self.i * TILES + g

    def groups(self, g):
        return self.i * (UNITS * T_UNIT) + (g // NQ * T_UNIT + (T_FIRST[g % NQ] if g < TILES else 0))


class Prologue(Pass):
    def __init__(self):
        pass

    def pieces(self, x):
        return PROLOGUE_PIECES.index(x) + 1

    def bank(self, x):
        return PROLOGUE_PIECES.index(x) % 2

    def before(self, x):
        at = PROLOGUE_PIECES.index(x)
        return PROLOGUE_PIECES[at - 2] if at >= 2 else None

    def qks(self, x):
        return PROLOGUE_PIECES.index(x)

    def vs(self, x):
        return PROLOGUE_PIECES.index(x) - 4


def build(nc, x, wq, bq, wk, bk, wv, bv, wo, bo, wq_gate, s_gate, wq_up, s_up, wq_down, s_down, c, wmod,
          cos, sin, out):
    with ExitStack() as ctx:
        def sem(name):
            return ctx.enter_context(nc.semaphore(name))

        base = (nc.sbuf_base + 31) // 32 * 32
        KB = 1024
        A_HTH, A_HTL, A_Y = 0, 16 * KB, 32 * KB
        A_QK, A_V, A_PT = 48 * KB, 80 * KB, 112 * KB
        A_W, A_ROPE, A_RAW, A_P, A_SMALL = 144 * KB, 168 * KB, 184 * KB, 192 * KB, 192 * KB + 512 * P_BLOCKS
        A_WO, A_O = A_W + 12 * KB, A_W + 16 * KB
        small_at = [A_SMALL]

        def at(name, offset, shape, dt):
            return nc.alloc_sbuf_tensor_at(name, shape, dt, offset=base + offset)

        def small(name, shape, dt):
            size = int(np.prod(shape[1:])) * (2 if dt == BF16 else 4)
            t = at(name, small_at[0], shape, dt)
            small_at[0] += (size + 31) // 32 * 32
            return t

        hT_hi = at("hT_hi", A_HTH, [P, KT, TOK], F32R)
        hT_lo = at("hT_lo", A_HTL, [P, KT, TOK], F32R)
        y = at("y", A_Y, [P, NTT, DIM], F32)
        qk_hi = at("qk_hi", A_QK, [P, 2, 2, SEQ], F32R)
        qk_lo = at("qk_lo", A_QK + 16 * KB, [P, 2, 2, SEQ], F32R)
        v_hi = at("v_hi", A_V, [P, BATCH, NQ, 2 * DH], F32R)
        v_lo = at("v_lo", A_V + 16 * KB, [P, BATCH, NQ, 2 * DH], F32R)
        pT_hi = at("pT_hi", A_PT, [P, NQ, CH], F32R)
        pT_lo = at("pT_lo", A_PT + 16 * KB, [P, NQ, CH], F32R)
        w_hi = at("w_hi", A_W, [P, 3, KT, 2 * DH], F32R)
        w_lo = at("w_lo", A_W + 6 * KB, [P, 3, KT, 2 * DH], F32R)
        wo_hi = at("wo_hi", A_WO, [P, 2, DIM], F32R)
        wo_lo = at("wo_lo", A_WO + 2 * KB, [P, 2, DIM], F32R)
        o_hi = at("o_hi", A_O, [P, 2, CH], F32R)
        o_lo = at("o_lo", A_O + 4 * KB, [P, 2, CH], F32R)
        cos_sb = at("cos_sb", A_ROPE, [P, SEQ], F32)
        sin_sb = at("sin_sb", A_ROPE + 4 * KB, [P, SEQ], F32)
        straight = at("straight", A_ROPE + 8 * KB, [P, 2, CH], F32)
        swapped = at("swapped", A_ROPE + 12 * KB, [P, 2, CH], F32)
        w_raw = at("w_raw", A_RAW, [P, 3, KT, 2 * DH], F32)
        wo_raw = at("wo_raw", A_RAW + 6 * KB, [P, 2, DIM], F32)
        probs = at("probs", A_P, [P, P_BLOCKS * P], F32)
        ident = small("ident", [P, P], F32)
        ident_b = small("ident_b", [P, P], BF16)
        mask_b = small("mask_b", [P, P], BF16)
        attn_bias = small("attn_bias", [P, DIM], F32)
        rows = small("rows", [NROWS, P], F32)
        cols = small("cols", [P, NROWS], F32)
        bq_s = small("bq_s", [P, HEADS], F32)
        tanh_c = small("tanh_c", [P, BATCH * KT], F32)
        silu_c = small("silu_c", [P, BATCH * KT], F32)
        mod = small("mod", [P, 8, BATCH], F32)
        bn = small("bn", [P, NTT, 6], F32)
        mv = small("mv", [P, NTT, 2], F32)
        var = small("var", [P, NTT], F32)
        root = small("root", [P, NTT], F32)
        rstd = small("rstd", [P, NTT], F32)
        newton = small("newton", [P, NTT], F32)
        neg_max = small("neg_max", [P, NQ], F32)
        row_sum = small("row_sum", [P, 2, NQ], F32)
        inv_sum = small("inv_sum", [P, 2, NQ], F32)
        assert base + small_at[0] <= nc.sbuf_usable_end, (base + small_at[0], nc.sbuf_usable_end)

        x_in = at("x_in", A_QK, [P, NTT, DIM], F32)
        wmod_a = at("wmod_a", A_QK + 16 * KB, [P, KT, 4, DIM], F32)
        xn = at("xn", A_PT, [P, NTT, DIM], F32)
        h32 = at("h32", A_PT + 16 * KB, [P, 2, CH], F32)
        bv_wide = at("bv_wide", A_PT + 20 * KB, [P, HEADS, P], F32)
        wo_all = at("wo_all", A_V + 16 * KB, [P, HEADS, DIM], F32)
        bo_wide = at("bo_wide", A_PT + 28 * KB, [P, DIM], F32)
        x2 = at("x2", A_QK, [P, NTT, DIM], F32)
        int_gate = at("int_gate", A_QK + 16 * KB, [P, HM, DIM], I32)
        int_up = at("int_up", A_QK + 22 * KB, [P, HM, DIM], I32)
        wmod_g = at("wmod_g", A_QK + 28 * KB, [P, KT, 2, DIM], F32)
        int_down = at("int_down", A_RAW, [P, KT, HID], I32)
        f_gate = at("f_gate", A_V, [P, HM, DIM], F32)
        f_up = at("f_up", A_V + 6 * KB, [P, HM, DIM], F32)
        f_down = at("f_down", A_V + 12 * KB, [P, KT, HID], F32)
        wd_hi = at("wd_hi", A_V + 18 * KB, [P, HM, DIM], F32R)
        wd_lo = at("wd_lo", A_V + 24 * KB, [P, HM, DIM], F32R)
        wg_hi = at("wg_hi", A_PT, [P, 2, KT, HID], F32R)
        wg_lo = at("wg_lo", A_PT + 11 * KB, [P, 2, KT, HID], F32R)
        h2_32 = at("h2_32", A_PT + 22 * KB, [P, 2, CH], F32)
        g_row = at("g_row", A_PT + 26 * KB, [P, 2, BATCH, DIM], F32)
        silu_w = at("silu_w", A_PT + 30 * KB, [P, BATCH * KT, P], F32)
        xn2 = at("xn2", A_ROPE, [P, NTT, DIM], F32)
        gu_hi = at("gu_hi", A_W, [P, HM, CH], F32R)
        gu_lo = at("gu_lo", A_W + 12 * KB, [P, HM, CH], F32R)
        tanh_g = at("tanh_g", A_P, [P, 2, CH], F32)
        lin_g = at("lin_g", A_P + 4 * KB, [P, 2, CH], F32)
        gu = at("gu", A_QK + 16 * KB, [P, 2, CH], F32)
        g_sign = at("g_sign", A_V + 30 * KB, [P, BATCH, DIM], F32)
        half_su = small("half_su", [P, HM], F32)
        half_sg = small("half_sg", [P, HM], F32)
        sd_wide = small("sd_wide", [P, DIM], F32)
        assert base + small_at[0] <= nc.sbuf_usable_end, (base + small_at[0], nc.sbuf_usable_end)

        ps_s = ctx.enter_context(nc.psum_tensor("ps_s", [P, 2, SEQ], F32))
        ps_t = ctx.enter_context(nc.psum_tensor("ps_t", [P, 2, CH], F32))
        ps_r = ctx.enter_context(nc.psum_tensor("ps_r", [P, 2, CH], F32))

        zeroed = sem("zeroed")
        consts_ready = sem("consts_ready")
        rows_ready = sem("rows_ready")
        x_ready = [sem(f"x_ready{n}") for n in range(NCH)]
        wmod_ready = sem("wmod_ready")
        tables_ready = sem("tables_ready")
        w_raw_ready = sem("w_raw_ready")
        wo_raw_ready = sem("wo_raw_ready")
        wo_all_ready = sem("wo_all_ready")
        cols_turned = sem("cols_turned")
        cols_ready = sem("cols_ready")
        tanh_ready = sem("tanh_ready")
        silu_ready = sem("silu_ready")
        mod_made = sem("mod_made")
        mod_ready = sem("mod_ready")
        var_ready = sem("var_ready")
        root_ready = sem("root_ready")
        xn_ready = sem("xn_ready")
        xn_turned = sem("xn_turned")
        h32_ready = sem("h32_ready")
        hhi_ready = sem("hhi_ready")
        hT_ready = sem("hT_ready")
        bv_wide_ready = sem("bv_wide_ready")
        attn_bias_made = sem("attn_bias_made")
        attn_bias_ready = sem("attn_bias_ready")
        pool_chain = sem("pool_chain")
        dve_chain = sem("dve_chain")
        gain_ready = sem("gain_ready")

        w_hi_ready = sem("w_hi_ready")
        w_ready = sem("w_ready")
        wo_hi_ready = sem("wo_hi_ready")
        wo_ready = sem("wo_ready")
        scores_ready = sem("scores_ready")
        max_ready = sem("max_ready")
        exp_ready = sem("exp_ready")
        turned = sem("turned")
        pT_hi_ready = sem("pT_hi_ready")
        pT_ready = sem("pT_ready")
        piece_made = sem("piece_made")
        y_added = sem("y_added")
        straight_ready = sem("straight_ready")
        swapped_ready = [sem(f"swapped_ready{n}") for n in range(2)]
        rotated = sem("rotated")
        qk_sum = sem("qk_sum")
        qk_hi_ready = sem("qk_hi_ready")
        qk_ready = sem("qk_ready")
        v_hi_ready = sem("v_hi_ready")
        v_ready = sem("v_ready")
        o_hi_ready = sem("o_hi_ready")
        o_ready = sem("o_ready")
        inv_ready = sem("inv_ready")

        ints_ready = sem("ints_ready")
        down_ready = sem("down_ready")
        x2_in_ready = sem("x2_in_ready")
        wmod_g_ready = sem("wmod_g_ready")
        silu_w_ready = sem("silu_w_ready")
        g_made = sem("g_made")
        g_ready = sem("g_ready")
        y_done = sem("y_done")
        x2_ready = sem("x2_ready")
        var2_ready = sem("var2_ready")
        root2_ready = sem("root2_ready")
        xn2_ready = sem("xn2_ready")
        xn2_turned = sem("xn2_turned")
        h2_32_ready = sem("h2_32_ready")
        h2_hi_ready = sem("h2_hi_ready")
        h2_ready = sem("h2_ready")
        wf_ready = sem("wf_ready")
        wf_turned = sem("wf_turned")
        wf_hi_ready = sem("wf_hi_ready")
        wf_lo_ready = sem("wf_lo_ready")
        gate_made = sem("gate_made")
        up_made = sem("up_made")
        lin_ready = sem("lin_ready")
        tanh_g_ready = sem("tanh_g_ready")
        silu_g_ready = sem("silu_g_ready")
        gu_ready = sem("gu_ready")
        gu_hi_ready = sem("gu_hi_ready")
        gu_split = sem("gu_split")
        down_made = sem("down_made")
        out_ready = sem("out_ready")
        stored = sem("stored")

        block = ctx.enter_context(nc.Block())

        x_t = x.rearrange("b (t p) d -> p (b t) d", p=P)
        out_t = out.rearrange("b (t p) d -> p (b t) d", p=P)
        wmod_t = wmod.rearrange("(k p) (j d) -> p k j d", p=P, d=DIM)
        w_t = [w.rearrange("(k p) n -> p k n", p=P) for w in (wq, wk, wv)]
        wo_t = wo.rearrange("(h p) n -> p h n", p=P)
        LAST = PAIRS - 1
        GROUPS4 = TOK // CH * KT

        def unit_batch(u):
            return u // 2 % BATCH

        def qk_at(parity, which, first, size):
            return (qk_hi[:, parity, which, first:first + size], qk_lo[:, parity, which, first:first + size])

        @block.sync
        def _(sp):
            sp.wait_ge(zeroed, 1)
            for src, r0, n in ((bq, ROW_BQ, HEADS), (bk, ROW_BK, HEADS), (bv, ROW_BV, HEADS)):
                sp.dma_start(rows[r0:r0 + n, :], src.rearrange("(h d) -> h d", d=DH)).then_inc(rows_ready, 16)
            sp.dma_start(rows[ROW_C:ROW_SG, :], c.rearrange("b (k p) -> (b k) p", p=P)).then_inc(rows_ready, 16)
            for src, r0 in ((s_gate, ROW_SG), (s_up, ROW_SU)):
                sp.dma_start(rows[r0:r0 + HM - 1, :], src[0:(HM - 1) * P].rearrange("(m p) -> m p", p=P))\
                    .then_inc(rows_ready, 16)
                sp.dma_start(rows[r0 + HM - 1:r0 + HM, 0:HLAST],
                             src[(HM - 1) * P:HID].rearrange("(a p) -> a p", a=1)).then_inc(rows_ready, 16)
            for n in range(NCH):
                sp.dma_start(x_in[:, 4 * n:4 * n + 4, :], x_t[:, 4 * n:4 * n + 4, :]).then_inc(x_ready[n], 16)
                if n == 1:
                    for j, part in enumerate((0, 1, 3, 4)):
                        sp.dma_start(wmod_a[:, :, j, :], wmod_t[:, :, part, :]).then_inc(wmod_ready, 16)
                    for j in range(3):
                        sp.dma_start(w_raw[:, j, :, :], w_t[j][:, :, 0:2 * DH]).then_inc(w_raw_ready, 16)
            sp.dma_start(cos_sb[:, :], cos).then_inc(tables_ready, 16)
            sp.dma_start(sin_sb[:, :], sin).then_inc(tables_ready, 16)
            sp.dma_start(wo_raw[:, :, :], wo_t[:, 0:2, :]).then_inc(wo_raw_ready, 16)
            sp.dma_start(wo_all[:, :, :], wo_t).then_inc(wo_all_ready, 16)
            sp.dma_start(bo_wide[:, :], bo.rearrange("(a n) -> a n", a=1).broadcast_to([P, DIM]))\
                .then_inc(wo_all_ready, 16)

            def swap_halves(n, q):
                sp.wait_ge(straight_ready, n + 1)
                half = DH // 2
                for a, b in ((0, half), (half, 0)):
                    sp.dma_start(swapped[a:a + half, q, :], straight[b:b + half, q, :])\
                        .then_inc(swapped_ready[q], 16)

            def one_pass(ps):
                for s in ps.steps:
                    if s.g == 0 and not ps.last:
                        sp.wait_ge(w_ready, ps.i * 3 + 3)
                        for j in range(3):
                            sp.dma_start(w_raw[:, j, :, :], w_t[j][:, :, bass.ds(ps.i * 256 + 256, 256)])\
                                .then_inc(w_raw_ready, 16)
                    if s.g == 5 and not ps.last:
                        sp.wait_ge(wo_ready, ps.i + 1)
                        sp.dma_start(wo_raw[:, :, :], wo_t[:, bass.ds(ps.i * 2 + 2, 2), :]).then_inc(wo_raw_ready, 16)
                    if s.first and s.first[0] == "qk":
                        swap_halves(ps.qks(s.first), ps.qk.index(s.first) % 2)

            pro = Prologue()
            for piece in PROLOGUE_PIECES[0:4]:
                swap_halves(pro.qks(piece), pro.qks(piece) % 2)
            with sp.Fori(0, LAST) as i:
                one_pass(Pass(i, False))
            one_pass(Pass(LAST, True))

            sp.wait_ge(scores_ready, PAIRS * TILES)
            sp.dma_start(wmod_g[:, :, 0, :], wmod_t[:, :, 2, :]).then_inc(wmod_g_ready, 16)
            sp.dma_start(wmod_g[:, :, 1, :], wmod_t[:, :, 5, :]).then_inc(wmod_g_ready, 16)
            for n in range(NCH):
                sp.dma_start(x2[:, 4 * n:4 * n + 4, :], x_t[:, 4 * n:4 * n + 4, :]).then_inc(x2_in_ready, 16)
            for dst, src in ((int_gate, wq_gate), (int_up, wq_up)):
                sp.dma_start(dst[:, 0:HM - 1, :], src[0:(HM - 1) * P, :].rearrange("(m p) d -> p m d", p=P))\
                    .then_inc(ints_ready, 16)
                sp.dma_start(dst[0:HLAST, HM - 1, :], src[(HM - 1) * P:HID, :]).then_inc(ints_ready, 16)
            sp.wait_ge(wo_ready, PAIRS)
            sp.dma_start(int_down[:, :, :], wq_down.rearrange("(k p) h -> p k h", p=P)).then_inc(down_ready, 16)
            sp.dma_start(sd_wide[:, :], s_down.rearrange("(a n) -> a n", a=1).broadcast_to([P, DIM]))\
                .then_inc(down_ready, 16)
            for n in range(NTT // 2):
                sp.wait_ge(out_ready, n + 1)
                sp.dma_start(out_t[:, 2 * n:2 * n + 2, :], y[:, 2 * n:2 * n + 2, :]).then_inc(stored, 16)
            sp.wait_ge(stored, 16 * (NTT // 2))

        @block.gpsimd
        def _(pool):
            pool.memset(rows[:, :], 0.0).then_inc(zeroed, 1)
            pool.memset(ident[:, :], 0.0).then_inc(pool_chain, 1)
            pool.memset(mask_b[:, :], 0.0).then_inc(pool_chain, 1)
            pool.wait_ge(pool_chain, 2)
            pool.affine_select(out=ident[:, :], in_=ident[:, :], compare_op=ALU.not_equal, fill=1.0, base=0,
                               pattern=[[-1, P]], channel_multiplier=1).then_inc(pool_chain, 1)
            pool.affine_select(out=mask_b[:, :], in_=mask_b[:, :], compare_op=ALU.is_ge, fill=MASKED, base=0,
                               pattern=[[-1, P]], channel_multiplier=1).then_inc(consts_ready, 1)
            pool.wait_ge(pool_chain, 3)
            pool.tensor_copy(ident_b[:, :], ident[:, :]).then_inc(consts_ready, 1)
            pool.memset(y[:, :, :], 0.0).then_inc(y_added, 1)

            def w_low(n, j):
                pool.wait_ge(w_hi_ready, n + 1)
                pool.tensor_tensor(w_lo[:, j, :, :], w_raw[:, j, :, :], w_hi[:, j, :, :].bitcast(F32),
                                   ALU.subtract).then_inc(w_ready, 1)

            def wo_low(i):
                pool.wait_ge(wo_hi_ready, i + 1)
                pool.tensor_tensor(wo_lo[:, :, :], wo_raw[:, :, :], wo_hi[:, :, :].bitcast(F32),
                                   ALU.subtract).then_inc(wo_ready, 1)

            def rotate(n, q, chunk):
                pool.wait_ge(swapped_ready[q], n // 2 * 32 + 32)
                cs = slice(chunk * CH, chunk * CH + CH)
                pool.tensor_tensor(swapped[:, q, :], swapped[:, q, :], sin_sb[:, cs], ALU.mult)
                pool.tensor_tensor(straight[:, q, :], straight[:, q, :], cos_sb[:, cs], ALU.mult).then_inc(rotated, 1)

            def qk_low(n, q, unit, which, chunk):
                pool.wait_ge(qk_hi_ready, n + 1)
                hi, lo = qk_at(unit % 2, which, chunk * CH, CH)
                pool.tensor_tensor(lo, straight[:, q, :], hi.bitcast(F32), ALU.subtract).then_inc(qk_ready, 1)

            pool.wait_ge(cols_ready, 1)
            pool.tensor_copy(bv_wide[:, :, :], cols[:, ROW_BV:ROW_BV + HEADS, None].broadcast_to([P, HEADS, P]))\
                .then_inc(bv_wide_ready, 1)
            for n, j in enumerate((1, 0, 2)):
                w_low(n, j)
            for n in range(GROUPS4):
                pool.wait_ge(hhi_ready, n + 1)
                part = (slice(None), n % KT, slice(n // KT * CH, n // KT * CH + CH))
                pool.tensor_tensor(hT_lo[part], h32[:, n % 2, :], hT_hi[part].bitcast(F32), ALU.subtract)\
                    .then_inc(hT_ready, 1)
            pool.wait_ge(tables_ready, 32)
            for n, piece in enumerate(PROLOGUE_PIECES[0:4]):
                rotate(n, n % 2, piece[3])
                qk_low(n, n % 2, *piece[1:])

            def one_pass(ps):
                wait_low = None
                for s in ps.steps:
                    if s.g == 1:
                        wo_low(ps.i)
                    if s.first and s.first[0] == "qk":
                        n, q = ps.qks(s.first), ps.qk.index(s.first) % 2
                        rotate(n, q, s.first[3])
                        if wait_low:
                            qk_low(*wait_low)
                        wait_low = (n, q, *s.first[1:])
                    if s.g == TILES:
                        if wait_low:
                            qk_low(*wait_low)
                        wait_low = None
                    if s.g == 3 * NQ - 1 and not ps.last:
                        for m, j in enumerate((1, 0, 2)):
                            w_low(ps.i * 3 + 3 + m, j)

            with pool.Fori(0, LAST) as i:
                one_pass(Pass(i, False))
            one_pass(Pass(LAST, True))

            pool.wait_ge(turned, PAIRS * UNITS * T_UNIT)
            pool.wait_ge(o_hi_ready, PAIRS * 8)
            pool.tensor_copy(silu_w[:, :, :], silu_c[:, :, None].broadcast_to([P, BATCH * KT, P]))\
                .then_inc(silu_w_ready, 1)
            pool.wait_ge(ints_ready, 64)
            for dst, src in ((f_gate, int_gate), (f_up, int_up)):
                pool.tensor_scalar(dst[:, 0:HM - 1, :], src[:, 0:HM - 1, :], -ZERO_POINT, None, ALU.add)
                pool.tensor_scalar(dst[0:HLAST, HM - 1, :], src[0:HLAST, HM - 1, :], -ZERO_POINT, None, ALU.add)\
                    .then_inc(wf_ready, 1)
            pool.wait_ge(down_ready, 32)
            pool.tensor_scalar(f_down[:, :, :], int_down[:, :, :], -ZERO_POINT, None, ALU.add).then_inc(wf_ready, 1)
            for n in range(GROUPS4):
                pool.wait_ge(h2_hi_ready, n + 1)
                part = (slice(None), n % KT, slice(n // KT * CH, n // KT * CH + CH))
                pool.tensor_tensor(hT_lo[part], h2_32[:, n % 2, :], hT_hi[part].bitcast(F32), ALU.subtract)\
                    .then_inc(h2_ready, 1)
            for n in range(NCH * HM):
                size = P if n % HM < HM - 1 else HLAST
                pool.wait_ge(gu_hi_ready, n + 1)
                pool.tensor_tensor(gu_lo[0:size, n % HM, :], gu[0:size, n % 2, :],
                                   gu_hi[0:size, n % HM, :].bitcast(F32), ALU.subtract).then_inc(gu_split, 1)

        @block.scalar
        def _(act):
            def w_high(j):
                nc.scalar.activation(w_hi[:, j, :, :], w_raw[:, j, :, :], ACT.Copy).then_inc(w_hi_ready, 1)

            def qk_out(ps, piece, n, q, head):
                which = piece[2]
                act.wait_ge(piece_made, ps.pieces(piece))
                if not (isinstance(n, int) and n < 2):
                    act.wait_ge(qk_ready, n - 1)
                act.nop(nofuse=True)
                bias = (bq_s if which == 0 else cols[:, ROW_BK:ROW_BK + HEADS])[:, bass.ds(head, 1)]
                nc.scalar.activation(straight[:, q, :], ps_r[:, ps.bank(piece), :], ACT.Identity, bias=bias,
                                     scale=SCALE if which == 0 else 1.0).then_inc(straight_ready, 1)

            def qk_high(n, q, unit, which, chunk):
                act.wait_ge(qk_sum, n + 1)
                hi, _ = qk_at(unit % 2, which, chunk * CH, CH)
                nc.scalar.activation(hi, straight[:, q, :], ACT.Copy).then_inc(qk_hi_ready, 1)

            def v_high(ps, piece):
                _, b, j = piece
                act.wait_ge(piece_made, ps.pieces(piece))
                nc.scalar.activation(v_hi[:, b % BATCH, 2 * j:2 * j + 2, :],
                                     ps_r[:, ps.bank(piece), :].rearrange("p (t n) -> p t n", t=2),
                                     ACT.Copy).then_inc(v_hi_ready, 1)

            act.wait_ge(cols_turned, 1)
            nc.scalar.activation(cols[:, :], ps_r[:, 0, 0:NROWS], ACT.Copy).then_inc(cols_ready, 1)
            act.wait_ge(cols_ready, 1)
            nc.scalar.activation(tanh_c[:, :], cols[:, ROW_C:ROW_SG], ACT.Tanh, scale=0.5).then_inc(tanh_ready, 1)
            act.wait_ge(w_raw_ready, 48)
            for j in (1, 0, 2):
                w_high(j)
            act.wait_ge(mod_made, 1)
            nc.scalar.activation(mod[:, :, :], ps_r[:, 1, 0:8 * BATCH].rearrange("p (j b) -> p j b", b=BATCH),
                                 ACT.Copy).then_inc(mod_ready, 1)
            act.wait_ge(var_ready, 1)
            nc.scalar.activation(root[:, :], var[:, :], ACT.Sqrt).then_inc(root_ready, 1)
            act.wait_ge(gain_ready, 2)
            for n in range(GROUPS4):
                k, b = n % KT, n // KT // 2
                act.wait_ge(xn_turned, n + 1)
                if n >= 2:
                    act.wait_ge(hT_ready, n - 1)
                src, shift, gain = ps_t[:, n % 2, :], mod[:, k, b:b + 1], mod[:, KT + k, b:b + 1]
                nc.scalar.activation(h32[:, n % 2, :], src, ACT.Identity, bias=shift, scale=gain).then_inc(h32_ready, 1)
                nc.scalar.activation(hT_hi[:, k, n // KT * CH:n // KT * CH + CH], src, ACT.Identity, bias=shift,
                                     scale=gain).then_inc(hhi_ready, 1)
            pro = Prologue()
            for n, piece in enumerate(PROLOGUE_PIECES[0:4]):
                qk_out(pro, piece, n, n % 2, 0)
                if n:
                    qk_high(n - 1, (n - 1) % 2, *PROLOGUE_PIECES[n - 1][1:])
            qk_high(3, 1, *PROLOGUE_PIECES[3][1:])
            for piece in PROLOGUE_PIECES[4:]:
                v_high(pro, piece)

            def turn_out(ps, g):
                t = g % NQ
                for j in range(T_GROUPS[t]):
                    k0, k1 = 4 * j, min(4 * j + 4, t + 1)
                    slot = k0 + (4 if t < 4 else 0)
                    act.wait_ge(turned, ps.groups(g) + (j + 1))
                    nc.scalar.activation(
                        pT_hi[:, slot:slot + k1 - k0, t % 4 * P:t % 4 * P + P],
                        ps_t[:, (T_FIRST[t] + j) % 2, 0:(k1 - k0) * P].rearrange("p (k q) -> p k q", q=P),
                        ACT.Copy).then_inc(pT_hi_ready, 1)

            def one_pass(ps):
                highs = {}
                for s in ps.steps:
                    if s.g == 1:
                        act.wait_ge(wo_raw_ready, ps.i * 16 + 16)
                        act.wait_ge(piece_made, ps.i * len(ps.full) + len(PROLOGUE_PIECES))
                        nc.scalar.activation(wo_hi[:, :, :], wo_raw[:, :, :], ACT.Copy).then_inc(wo_hi_ready, 1)
                    if s.first and s.first[0] == "qk":
                        n, q, unit = ps.qks(s.first), ps.qk.index(s.first) % 2, s.first[1]
                        qk_out(ps, s.first, n, q, ps.i * 2 + (unit % 2 if unit < UNITS else 2))
                        highs[s.g + 2] = (n, q, *s.first[1:])
                    if s.first and s.first[0] == "v":
                        v_high(ps, s.first)
                    if s.scores is not None:
                        t = s.g % NQ
                        act.wait_ge(max_ready, ps.tiles(s.g) + 1)
                        if s.g >= 3:
                            act.wait_ge(turned, ps.groups(s.g - 2))
                        nc.scalar.activation(probs[:, P_AT[t] * P:(P_AT[t] + t + 1) * P],
                                             ps_s[:, s.g % 2, 0:(t + 1) * P], ACT.Exp, bias=neg_max[:, t:t + 1],
                                             accum_out=row_sum[:, s.g // NQ % 2, t:t + 1]).then_inc(exp_ready, 1)
                    if s.pv:
                        act.wait_ge(piece_made, ps.pieces(s.pv))
                        nc.scalar.activation(o_hi[:, s.pv[2], :], ps_r[:, ps.bank(s.pv), :], ACT.Copy)\
                            .then_inc(o_hi_ready, 1)
                    if s.turn is not None:
                        turn_out(ps, s.turn)
                    if s.g in highs:
                        qk_high(*highs[s.g])
                    if s.g == 3 * NQ - 1 and not ps.last:
                        act.wait_ge(w_raw_ready, ps.i * 48 + 96)
                        act.wait_ge(piece_made, ps.pieces(("qk", 3, 0, 1)))
                        for j in (1, 0, 2):
                            w_high(j)

            with act.Fori(0, LAST) as i:
                one_pass(Pass(i, False))
            one_pass(Pass(LAST, True))

            for n in range(3 * HM):
                which, m = divmod(n, HM)
                size = P if m < HM - 1 else HLAST
                act.wait_ge(wf_turned, n + 1)
                if which < 2:
                    dst = wg_hi[:, which, :, m * P:m * P + size]
                    src = ps_t[:, n % 2, 0:KT * size].rearrange("p (k h) -> p k h", k=KT)
                else:
                    dst, src = wd_hi[0:size, m, :], ps_t[0:size, n % 2, 0:DIM]
                nc.scalar.activation(dst, src, ACT.Copy).then_inc(wf_hi_ready, 1)
            act.wait_ge(var2_ready, 1)
            nc.scalar.activation(root[:, :], var[:, :], ACT.Sqrt).then_inc(root2_ready, 1)
            for n in range(GROUPS4):
                k, b = n % KT, n // KT // 2
                act.wait_ge(xn2_turned, n + 1)
                if n >= 2:
                    act.wait_ge(h2_ready, n - 1)
                src, shift, gain = ps_t[:, n % 2, :], mod[:, 2 * KT + k, b:b + 1], mod[:, 3 * KT + k, b:b + 1]
                nc.scalar.activation(h2_32[:, n % 2, :], src, ACT.Identity, bias=shift, scale=gain)\
                    .then_inc(h2_32_ready, 1)
                nc.scalar.activation(hT_hi[:, k, n // KT * CH:n // KT * CH + CH], src, ACT.Identity, bias=shift,
                                     scale=gain).then_inc(h2_hi_ready, 1)

            def gu_high(n):
                m = n % HM
                size = P if m < HM - 1 else HLAST
                act.wait_ge(gu_ready, n + 1)
                if n >= HM:
                    act.wait_ge(down_made, n // HM * 2)
                nc.scalar.activation(gu_hi[0:size, m, :], gu[0:size, n % 2, :], ACT.Copy).then_inc(gu_hi_ready, 1)

            for n in range(NCH * HM):
                m = n % HM
                size = P if m < HM - 1 else HLAST
                act.wait_ge(gate_made, n + 1)
                if n >= 2:
                    act.wait_ge(gu_ready, n - 1)
                src = ps_s[0:size, n % 2, 0:CH]
                nc.scalar.activation(tanh_g[0:size, n % 2, :], src, ACT.Tanh, scale=half_sg[0:size, m:m + 1])\
                    .then_inc(tanh_g_ready, 1)
                nc.scalar.activation(lin_g[0:size, n % 2, :], src, ACT.Copy,
                                     scale=cols[0:size, ROW_SG + m:ROW_SG + m + 1]).then_inc(lin_ready, 1)
                if n >= 1:
                    gu_high(n - 1)
            gu_high(NCH * HM - 1)

        @block.vector
        def _(dve):
            linked = [0]

            def link(ins):
                linked[0] += 1
                ins.then_inc(dve_chain, 1)
                dve.wait_ge(dve_chain, linked[0])

            def norm(src, dst, tile_ready, var_sem, root_sem, done):
                for t in range(NTT):
                    if t % 4 == 0:
                        tile_ready(t // 4)
                    last = nc.vector.bn_stats(bn[:, t, :], src[:, t, :])
                link(last)
                for t in range(NTT):
                    last = nc.vector.bn_aggr(mv[:, t, :], bn[:, t, :])
                link(last)
                nc.vector.tensor_scalar(var[:, :], mv[:, :, 1], EPS, None, ALU.add).then_inc(var_sem, 1)
                dve.wait_ge(root_sem, 1)
                link(nc.vector.reciprocal(rstd[:, :], root[:, :]))
                link(nc.vector.tensor_tensor(newton[:, :], rstd[:, :], rstd[:, :], ALU.mult))
                link(nc.vector.tensor_tensor(newton[:, :], newton[:, :], var[:, :], ALU.mult))
                link(nc.vector.tensor_scalar(newton[:, :], newton[:, :], -0.5, 1.5, ALU.mult, ALU.add))
                link(nc.vector.tensor_tensor(rstd[:, :], rstd[:, :], newton[:, :], ALU.mult))
                for t in range(NTT):
                    ins = nc.vector.tensor_scalar(dst[:, t, :], src[:, t, :], mv[:, t, 0:1], rstd[:, t:t + 1],
                                                  ALU.subtract, ALU.mult)
                    if t % 4 == 3:
                        ins.then_inc(done, 1)

            dve.wait_ge(tanh_ready, 1)
            link(nc.vector.scalar_tensor_tensor(silu_c[:, :], tanh_c[:, :], 1.0, cols[:, ROW_C:ROW_SG], ALU.add, ALU.mult))
            nc.vector.tensor_scalar(silu_c[:, :], silu_c[:, :], 0.5, None, ALU.mult).then_inc(silu_ready, 1)
            nc.vector.tensor_scalar(bq_s[:, :], cols[:, ROW_BQ:ROW_BQ + HEADS], SCALE, None, ALU.mult)
            nc.vector.tensor_scalar(half_sg[:, :], cols[:, ROW_SG:ROW_SG + HM], 0.5, None, ALU.mult)
            nc.vector.tensor_scalar(half_su[:, :], cols[:, ROW_SU:ROW_SU + HM], 0.5, None, ALU.mult)
            dve.wait_ge(mod_ready, 1)
            for j in (1, 3):
                nc.vector.tensor_scalar(mod[:, KT * j:KT * j + KT, :], mod[:, KT * j:KT * j + KT, :], 1.0, None,
                                        ALU.add).then_inc(gain_ready, 1)
            norm(x_in, xn, lambda n: dve.wait_ge(x_ready[n], 16), var_ready, root_ready, xn_ready)
            dve.wait_ge(wo_all_ready, 32)
            dve.wait_ge(attn_bias_made, 1)
            nc.vector.tensor_tensor(attn_bias[:, :], ps_s[:, 0, 0:DIM], bo_wide[:, :], ALU.add)\
                .then_inc(attn_bias_ready, 1)

            def qk_add(n, q):
                dve.wait_ge(rotated, n + 1)
                nc.vector.tensor_tensor(straight[:, q, :], straight[:, q, :], swapped[:, q, :], ALU.add)\
                    .then_inc(qk_sum, 1)

            def v_low(ps, piece):
                _, b, j = piece
                dve.wait_ge(v_hi_ready, ps.vs(piece) + 1)
                part = (slice(None), b % BATCH, slice(2 * j, 2 * j + 2), slice(None))
                nc.vector.tensor_tensor(v_lo[part], ps_r[:, ps.bank(piece), :].rearrange("p (t n) -> p t n", t=2),
                                        v_hi[part].bitcast(F32), ALU.subtract).then_inc(v_ready, 1)

            pro = Prologue()
            for n in range(4):
                qk_add(n, n % 2)
            for piece in PROLOGUE_PIECES[4:]:
                v_low(pro, piece)

            def turn_low(ps, g):
                t = g % NQ
                for j in range(T_GROUPS[t]):
                    k0, k1 = 4 * j, min(4 * j + 4, t + 1)
                    slot = k0 + (4 if t < 4 else 0)
                    part = (slice(None), slice(slot, slot + k1 - k0), slice(t % 4 * P, t % 4 * P + P))
                    dve.wait_ge(pT_hi_ready, ps.groups(g) + (j + 1))
                    nc.vector.tensor_tensor(
                        pT_lo[part], ps_t[:, (T_FIRST[t] + j) % 2, 0:(k1 - k0) * P].rearrange("p (k q) -> p k q", q=P),
                        pT_hi[part].bitcast(F32), ALU.subtract).then_inc(pT_ready, 1)

            def wo_add(ps, piece):
                _, u, chunk, j = piece
                if j == 0:
                    nc.vector.reciprocal(inv_sum[:, u % 2, 4 * chunk:4 * chunk + 4],
                                         row_sum[:, u % 2, 4 * chunk:4 * chunk + 4]).then_inc(inv_ready, 1)
                    dve.wait_ge(inv_ready, ps.i * 8 + (ps.wo.index(piece) // 2 + 1))
                dve.wait_ge(piece_made, ps.pieces(piece))
                for s in range(2):
                    t = 4 * chunk + 2 * j + s
                    tt = unit_batch(u) * NQ + t
                    ins = nc.vector.scalar_tensor_tensor(
                        y[:, tt, :], ps_r[:, ps.bank(piece), s * DIM:s * DIM + DIM], inv_sum[:, u % 2, t:t + 1],
                        y[:, tt, :], ALU.mult, ALU.add)
                ins.then_inc(y_added, 1)

            def one_pass(ps):
                adds = {}
                for s in ps.steps:
                    if s.scores is not None:
                        t = s.g % NQ
                        dve.wait_ge(scores_ready, ps.tiles(s.g) + 1)
                        nc.vector.tensor_reduce(neg_max[:, t:t + 1], ps_s[:, s.g % 2, 0:(t + 1) * P], AX, ALU.max,
                                                negate=True).then_inc(max_ready, 1)
                    if s.first and s.first[0] == "v":
                        v_low(ps, s.first)
                    if s.first and s.first[0] == "qk":
                        adds[s.g + 2] = (ps.qks(s.first), ps.qk.index(s.first) % 2)
                    if s.g in adds:
                        qk_add(*adds[s.g])
                    if s.pv:
                        _, _, chunk = s.pv
                        dve.wait_ge(o_hi_ready, ps.pvs(s.pv) + 1)
                        nc.vector.tensor_tensor(o_lo[:, chunk, :], ps_r[:, ps.bank(s.pv), :],
                                                o_hi[:, chunk, :].bitcast(F32), ALU.subtract).then_inc(o_ready, 1)
                    if s.turn is not None:
                        turn_low(ps, s.turn)
                    for piece in s.late:
                        wo_add(ps, piece)

            dve.wait_ge(y_added, 1)
            with dve.Fori(0, LAST) as i:
                one_pass(Pass(i, False))
            one_pass(Pass(LAST, True))

            dve.wait_ge(down_ready, 32)
            for j in range(2):
                dve.wait_ge(g_made, j + 1)
                src = ps_r[:, j, :].rearrange("p (b n) -> p b n", b=BATCH)
                link(nc.vector.tensor_scalar(g_sign[:, :, :], src, 0.0, 2.0, ALU.is_ge, ALU.mult))
                link(nc.vector.tensor_scalar(g_row[:, j, :, :], src, -1.0, 0.25, ALU.mult, ALU.max))
                link(nc.vector.tensor_tensor(g_row[:, j, :, :], src, g_row[:, j, :, :], ALU.max))
                link(nc.vector.scalar_tensor_tensor(g_row[:, j, :, :], g_sign[:, :, :], -1.0, g_row[:, j, :, :],
                                                    ALU.add, ALU.mult))
            link(nc.vector.tensor_tensor(g_row[:, 1, :, :], g_row[:, 1, :, :],
                                         sd_wide[:, None, :].broadcast_to([P, BATCH, DIM]), ALU.mult))
            nc.vector.engine_nop().then_inc(g_ready, 1)
            dve.wait_ge(x2_in_ready, 16 * NCH)
            for n in range(NCH):
                part = (slice(None), slice(4 * n, 4 * n + 4), slice(None))
                link(nc.vector.tensor_tensor(y[part], y[part], attn_bias[:, None, :].broadcast_to([P, 4, DIM]), ALU.add))
                link(nc.vector.tensor_tensor(y[part], y[part],
                                             g_row[:, 0, n // 2, None, :].broadcast_to([P, 4, DIM]), ALU.mult))
                link(nc.vector.tensor_tensor(x2[part], x2[part], y[part], ALU.add))
            for n in range(3 * HM):
                which, m = divmod(n, HM)
                size = P if m < HM - 1 else HLAST
                dve.wait_ge(wf_hi_ready, n + 1)
                if which < 2:
                    part = (slice(None), which, slice(None), slice(m * P, m * P + size))
                    nc.vector.tensor_tensor(wg_lo[part], ps_t[:, n % 2, 0:KT * size].rearrange("p (k h) -> p k h", k=KT),
                                            wg_hi[part].bitcast(F32), ALU.subtract).then_inc(wf_lo_ready, 1)
                else:
                    nc.vector.tensor_tensor(wd_lo[0:size, m, :], ps_t[0:size, n % 2, 0:DIM],
                                            wd_hi[0:size, m, :].bitcast(F32), ALU.subtract).then_inc(wf_lo_ready, 1)

            norm(x2, xn2, lambda n: None, var2_ready, root2_ready, xn2_ready)

            def finish(n):
                dve.wait_ge(down_made, n + 1)
                part = (slice(None), slice(2 * n, 2 * n + 2), slice(None))
                link(nc.vector.tensor_tensor(y[part], ps_r[:, n % 2, :].rearrange("p (t n) -> p t n", t=2),
                                             g_row[:, 1, n // 4, None, :].broadcast_to([P, 2, DIM]), ALU.mult))
                nc.vector.tensor_tensor(y[part], y[part], x2[part], ALU.add).then_inc(out_ready, 1)

            for n in range(NCH * HM):
                m = n % HM
                size = P if m < HM - 1 else HLAST
                dve.wait_ge(lin_ready, n + 1)
                link(nc.vector.scalar_tensor_tensor(lin_g[0:size, n % 2, :], tanh_g[0:size, n % 2, :], 1.0,
                                                    lin_g[0:size, n % 2, :], ALU.add, ALU.mult))
                dve.wait_ge(up_made, n + 1)
                if n >= 2:
                    dve.wait_ge(gu_split, n - 1)
                nc.vector.scalar_tensor_tensor(gu[0:size, n % 2, :], ps_s[0:size, n % 2, CH:2 * CH],
                                               half_su[0:size, m:m + 1], lin_g[0:size, n % 2, :], ALU.mult, ALU.mult)\
                    .then_inc(gu_ready, 1)
                if n >= HM and m == 3:
                    for j in range(2):
                        finish(n // HM * 2 - 2 + j)
            for j in range(2):
                finish(NCH * 2 - 2 + j)

        @block.tensor
        def _(pe):
            def three(out, stationary, moving, first, last):
                (shi, slo), (mhi, mlo) = stationary, moving
                nc.tensor.matmul(out, shi, mhi, start=first, stop=False)
                nc.tensor.matmul(out, shi, mlo, start=False, stop=False)
                return nc.tensor.matmul(out, slo, mhi, start=False, stop=last)

            def wait_bank(ps, piece):
                old = ps.before(piece)
                if old is None:
                    if not isinstance(ps, Prologue):
                        pe.wait_ge(y_added, ps.i * 16 + 1)
                elif old[0] == "qk":
                    pe.wait_ge(straight_ready, ps.qks(old) + 1)
                elif old[0] == "v":
                    pe.wait_ge(v_ready, ps.vs(old) + 1)
                elif old[0] == "pv":
                    pe.wait_ge(o_ready, ps.pvs(old) + 1)
                else:
                    pe.wait_ge(y_added, ps.wos(old) + 2)

            def w_at(j, k, first, size):
                return w_hi[:, j, k, first:first + size], w_lo[:, j, k, first:first + size]

            def h_at(k, first, size):
                return hT_hi[:, k, first:first + size], hT_lo[:, k, first:first + size]

            def make(ps, piece):
                wait_bank(ps, piece)
                dst = ps_r[:, ps.bank(piece), :]
                if piece[0] == "qk":
                    _, u, which, chunk = piece
                    for k in range(KT):
                        ins = three(dst, w_at(which, k, u % 2 * DH, DH),
                                    h_at(k, unit_batch(u) * SEQ + chunk * CH, CH), k == 0, k == KT - 1)
                elif piece[0] == "v":
                    _, b, j = piece
                    for s in range(2):
                        for k in range(KT):
                            ins = three(dst[:, s * 2 * DH:s * 2 * DH + 2 * DH],
                                        h_at(k, b % BATCH * SEQ + (2 * j + s) * P, P), w_at(2, k, 0, 2 * DH),
                                        k == 0, k == KT - 1)
                elif piece[0] == "pv":
                    _, u, chunk = piece
                    b, d0 = unit_batch(u), u % 2 * DH
                    pe.wait_ge(pT_ready, ps.groups(NQ * u + 4 * chunk + 4))
                    n_keys = 4 * chunk + 4
                    for k in range(n_keys):
                        q0 = max(0, k - 4 * chunk) * P
                        slot = k + (4 if chunk == 0 else 0)
                        ins = three(dst[:, q0:CH], (v_hi[:, b, k, d0:d0 + DH], v_lo[:, b, k, d0:d0 + DH]),
                                    (pT_hi[:, slot, q0:CH], pT_lo[:, slot, q0:CH]), k == 0, k == n_keys - 1)
                else:
                    _, u, chunk, j = piece
                    pe.wait_ge(o_ready, ps.i * 8 + (ps.pv.index(("pv", u, chunk)) + 1))
                    if u == 0:
                        pe.wait_ge(wo_ready, ps.i + 1)
                    for s in range(2):
                        q0 = (2 * j + s) * P
                        ins = three(dst[:, s * DIM:s * DIM + DIM],
                                    (o_hi[:, chunk, q0:q0 + P], o_lo[:, chunk, q0:q0 + P]),
                                    (wo_hi[:, u % 2, :], wo_lo[:, u % 2, :]), True, True)
                ins.then_inc(piece_made, 1)

            def scores(ps, g):
                u, t = divmod(g, NQ)
                if g >= 2:
                    pe.wait_ge(exp_ready, ps.tiles(g - 2) + 1)
                if t % 4 == 0:
                    pe.wait_ge(qk_ready, ps.i * 16 + (4 * u + 2 * (t // 4) + 2))
                q = qk_at(u % 2, 0, t * P, P)
                for k0 in range(0, (t + 1) * P, CH):
                    size = min(CH, (t + 1) * P - k0)
                    dst = ps_s[:, g % 2, k0:k0 + size]
                    diagonal = k0 + size == (t + 1) * P
                    ins = three(dst, q, qk_at(u % 2, 1, k0, size), True, not diagonal)
                ins = nc.tensor.matmul(ps_s[:, g % 2, t * P:t * P + P], ident_b[:, :], mask_b[:, :], start=False, stop=True)
                ins.then_inc(scores_ready, 1)

            def turn(ps, g):
                t = g % NQ
                pe.wait_ge(exp_ready, ps.tiles(g) + 1)
                for j in range(T_GROUPS[t]):
                    bank = (T_FIRST[t] + j) % 2
                    if g // NQ * T_UNIT + T_FIRST[t] + j >= 2:
                        pe.wait_ge(pT_ready, ps.groups(g) + (j - 1))
                    for k in range(4 * j, min(4 * j + 4, t + 1)):
                        ins = nc.tensor.transpose(ps_t[:, bank, (k - 4 * j) * P:(k - 4 * j) * P + P],
                                                  probs[:, (P_AT[t] + k) * P:(P_AT[t] + k) * P + P], ident[:, :])
                    ins.then_inc(turned, 1)

            pe.wait_ge(consts_ready, 2)
            pe.wait_ge(rows_ready, 16 * 8)
            nc.tensor.transpose(ps_r[:, 0, 0:NROWS], rows[:, :], ident[0:NROWS, 0:NROWS]).then_inc(cols_turned, 1)
            pe.wait_ge(silu_ready, 1)
            pe.wait_ge(wmod_ready, 64)
            for j in range(4):
                for k in range(KT):
                    for kk in range(KT):
                        at_ = (KT * j + k) * BATCH
                        ins = nc.tensor.matmul(ps_r[:, 1, at_:at_ + BATCH], wmod_a[:, kk, j, k * P:k * P + P],
                                               silu_c[:, kk:BATCH * KT:KT], start=kk == 0, stop=kk == KT - 1)
            ins.then_inc(mod_made, 1)

            def turn_tokens(src, ready, n, done):
                k, chunk = n % KT, n // KT
                pe.wait_ge(ready, chunk + 1)
                for t in range(4):
                    ins = nc.tensor.transpose(ps_t[:, n % 2, t * P:t * P + P],
                                              src[:, 4 * chunk + t, k * P:k * P + P], ident[:, :])
                ins.then_inc(done, 1)

            for n in range(GROUPS4):
                if n >= 2:
                    pe.wait_ge(hhi_ready, n - 1)
                turn_tokens(xn, xn_ready, n, xn_turned)
            pe.wait_ge(bv_wide_ready, 1)
            pe.wait_ge(wo_all_ready, 32)
            for h in range(HEADS):
                ins = nc.tensor.matmul(ps_s[:, 0, 0:DIM], bv_wide[:, h, :], wo_all[:, h, :], start=h == 0,
                                       stop=h == HEADS - 1)
            ins.then_inc(attn_bias_made, 1)
            pe.wait_ge(cols_ready, 1)
            pe.wait_ge(mod_ready, 1)
            pe.wait_ge(hT_ready, GROUPS4)
            pe.wait_ge(w_ready, 3)
            pro = Prologue()
            for piece in PROLOGUE_PIECES:
                make(pro, piece)
            pe.wait_ge(v_ready, 4)
            pe.wait_ge(attn_bias_ready, 1)

            def one_pass(ps):
                for s in ps.steps:
                    if s.scores is not None:
                        scores(ps, s.g)
                    if s.g == 3 * NQ + 1 and not ps.last:
                        pe.wait_ge(w_ready, ps.i * 3 + 6)
                    if s.first:
                        make(ps, s.first)
                    if s.pv:
                        if s.pv in (("pv", 0, 0), ("pv", 2, 0)):
                            pe.wait_ge(v_ready, ps.i * 8 + (4 if s.pv[1] == 0 else 8))
                        make(ps, s.pv)
                    if s.turn is not None:
                        turn(ps, s.turn)
                    for piece in s.late:
                        make(ps, piece)

            with pe.Fori(0, LAST) as i:
                one_pass(Pass(i, False))
            one_pass(Pass(LAST, True))

            pe.wait_ge(y_added, PAIRS * 16 + 1)
            pe.wait_ge(silu_w_ready, 1)
            pe.wait_ge(wmod_g_ready, 32)
            for j in range(2):
                for b in range(BATCH):
                    for k in range(KT):
                        ins = nc.tensor.matmul(ps_r[:, j, b * DIM:b * DIM + DIM], silu_w[:, b * KT + k, :],
                                               wmod_g[:, k, j, :], start=k == 0, stop=k == KT - 1)
                ins.then_inc(g_made, 1)
            pe.wait_ge(pT_ready, PAIRS * UNITS * T_UNIT)
            for n in range(3 * HM):
                which, m = divmod(n, HM)
                size = P if m < HM - 1 else HLAST
                pe.wait_ge(wf_ready, which + 1)
                if n >= 2:
                    pe.wait_ge(wf_lo_ready, n - 1)
                for k in range(KT):
                    if which < 2:
                        src = (f_gate, f_up)[which][0:size, m, k * P:k * P + P]
                        ins = nc.tensor.transpose(ps_t[:, n % 2, k * size:k * size + size], src, ident[0:size, 0:size])
                    else:
                        ins = nc.tensor.transpose(ps_t[0:size, n % 2, k * P:k * P + P],
                                                  f_down[:, k, m * P:m * P + size], ident[:, :])
                ins.then_inc(wf_turned, 1)
            for n in range(GROUPS4):
                if n < 2:
                    pe.wait_ge(wf_lo_ready, 3 * HM - 1 + n)
                else:
                    pe.wait_ge(h2_hi_ready, n - 1)
                turn_tokens(xn2, xn2_ready, n, xn2_turned)
            pe.wait_ge(wf_lo_ready, 3 * HM)

            def down(n):
                pe.wait_ge(gu_split, n * HM + HM)
                for j in range(2):
                    if n == 0 and j == 0:
                        pe.wait_ge(g_ready, 1)
                    if n > 0:
                        pe.wait_ge(out_ready, 2 * n - 1 + j)
                    for s in range(2):
                        t = 2 * j + s
                        for m in range(HM):
                            size = P if m < HM - 1 else HLAST
                            ins = three(ps_r[:, j, s * DIM:s * DIM + DIM],
                                        (gu_hi[0:size, m, t * P:t * P + P], gu_lo[0:size, m, t * P:t * P + P]),
                                        (wd_hi[0:size, m, :], wd_lo[0:size, m, :]), m == 0, m == HM - 1)
                    ins.then_inc(down_made, 1)

            for n in range(NCH * HM):
                chunk, m = divmod(n, HM)
                size = P if m < HM - 1 else HLAST
                if m == 0:
                    pe.wait_ge(h2_ready, chunk * KT + KT)
                if n >= 2:
                    pe.wait_ge(gu_ready, n - 1)
                for which, done in enumerate((gate_made, up_made)):
                    for k in range(KT):
                        ins = three(ps_s[0:size, n % 2, which * CH:which * CH + CH],
                                    (wg_hi[:, which, k, m * P:m * P + size], wg_lo[:, which, k, m * P:m * P + size]),
                                    h_at(k, chunk * CH, CH), k == 0, k == KT - 1)
                    ins.then_inc(done, 1)
                if chunk > 0 and m == 1:
                    down(chunk - 1)
            down(NCH - 1)


def rotary_tables():
    inv_freq = np.float32(1.0) / (10000.0 ** (np.arange(0, DH, 2) / DH)).astype(np.float32)
    freqs = np.arange(SEQ, dtype=np.float32)[None, :] * inv_freq[:, None]
    cos = np.cos(freqs.astype(np.float64)).astype(np.float32)
    sin = np.sin(freqs.astype(np.float64)).astype(np.float32)
    return np.concatenate([cos, cos]), np.concatenate([-sin, sin])


INPUTS = ["L0_attn_x", "L0_attn_Wq", "L0_attn_bq", "L0_attn_Wk", "L0_attn_bk", "L0_attn_Wv", "L0_attn_bv",
          "L0_attn_Wo", "L0_attn_bo", "L0_ffn_wq_gate", "L0_ffn_s_gate", "L0_ffn_wq_up", "L0_ffn_s_up",
          "L0_ffn_wq_down", "L0_ffn_s_down", "L0_c", "L0_wmod"]


def kernel(**inputs):
    import concourse.bacc as bacc
    from concourse.bass_utils import run_bass_kernel_spmd

    nc = bacc.Bacc("TRN2", target_bir_lowering=False, num_devices=1)
    arrays, args = {}, []
    cos, sin = rotary_tables()
    for name, a in [(n, inputs[n]) for n in INPUTS] + [("rotary_cos", cos), ("rotary_sin", sin)]:
        a = np.ascontiguousarray(a)
        arrays[f"in_{name}"] = a
        args.append(nc.dram_tensor(f"in_{name}", a.shape, mybir.dt.from_np(a.dtype), kind="ExternalInput").ap())
    out = nc.dram_tensor("out_0", (BATCH, SEQ, DIM), F32, kind="ExternalOutput").ap()
    build(nc, *args, out)
    got = run_bass_kernel_spmd(nc, [arrays], core_ids=[0])
    return got.results[0]["out_0"]
```

```python
from contextlib import ExitStack

import numpy as np

import concourse.bass as bass
from concourse import mybir

F32 = mybir.dt.float32
F32R = mybir.dt.float32r
BF16 = mybir.dt.bfloat16
I32 = mybir.dt.int32
ALU = mybir.AluOpType
ACT = mybir.ActivationFunctionType
AX = mybir.AxisListType.X

P = 128
BATCH, SEQ, DIM = 2, 1024, 256
HEADS, DH = 16, 128
INNER = HEADS * DH
HID = 704
TOK = BATCH * SEQ
KT = DIM // P
NQ = SEQ // P
NTT = TOK // P
CH = 512
NCH = TOK // CH
HM = (HID + P - 1) // P
HLAST = HID - (HM - 1) * P
PAIRS = HEADS // 2
UNITS = 2 * BATCH
TILES = UNITS * NQ
EPS = 1e-5
SCALE = DH ** -0.5
ZERO_POINT = 128.0
MASKED = -3.0e38

ROW_BQ, ROW_BK, ROW_BV = 0, HEADS, 2 * HEADS
ROW_C = 3 * HEADS
ROW_SG = ROW_C + BATCH * KT
ROW_SU = ROW_SG + HM
NROWS = ROW_SU + HM

ORDER = [0, 7, 1, 6, 2, 5, 3, 4]
P_AT = [0, 1, 9, 11, 0, 3, 9, 13]
P_BLOCKS = 18

T_GROUPS = [(t + 4) // 4 for t in ORDER]
T_FIRST = [sum(T_GROUPS[:s]) for s in range(NQ)]
T_UNIT = sum(T_GROUPS)

ALL_UNITS = PAIRS * UNITS
WQ, WK, WV, WO = range(4)


TENSOR_PLAN = """make:K0+ make:Q0+ scores:0 turn:6.0- turn:7.0- scores:1 scores:2 turn:7.1- make:P0- turn:0.0
        make:P1- scores:3 turn:1.0 make:W00- make:K1+ scores:4 turn:1.1 make:W01- turn:2.0 make:Q1+
        make:W10- scores:5 turn:3.0 make:W11- turn:3.1 make:V0 turn:4.0 scores:6 make:V1 turn:5.0 scores:7
        turn:5.1"""
SCALAR_PLAN = """out:K0+ exp:7- turn:6.0- exp:0 split:V out:Q0+ turn:7.0- turn:7.1- high:P0- turn:0.0 exp:1 exp:2
        high:P1- high:K0+ high:Q0+ turn:1.0 out:K1+ turn:1.1 split:K exp:3 turn:2.0 exp:4 out:Q1+ turn:3.0
        split:Q exp:5 turn:3.1 turn:4.0 high:V0 high:K1+ high:V1 turn:5.0 exp:6 split:O turn:5.1 high:Q1+"""
VECTOR_PLAN = """max:0 turn:6.0- turn:7.0- turn:7.1- max:1 low:P0- add:K0+ max:2 turn:0.0 add:Q0+ low:P1- max:3
        sum:W00- turn:1.0 max:4 sum:W01- turn:1.1 turn:2.0 sum:W10- max:5 turn:3.0 sum:W11- add:K1+ turn:3.1
        turn:4.0 max:6 low:V0 add:Q1+ low:V1 max:7 turn:5.0 turn:5.1"""
POOL_PLAN = """rotate:K0+ split:V rotate:Q0+ low:K0+ low:Q0+ rotate:K1+ split:K split:Q rotate:Q1+ low:K1+ low:Q1+
        split:O"""


def unit_plan(plan, u):
    out = []
    for token in plan.split():
        what, name = token.rstrip("+-").split(":")
        v = u + {"+": 1, "-": -1}.get(token[-1], 0)
        if what == "split":
            which = "QKVO".index(name)
            n = v // UNITS + (which != WO)
            if v % UNITS == (0 if which == WO else 2) and n < PAIRS and v < ALL_UNITS:
                out.append((what, which, n))
        elif name[0] in "KQ":
            if 1 <= v < ALL_UNITS:
                out.append((what, v, ("qk", v, int(name[0] == "K"), int(name[1]))))
        elif name[0] == "V":
            piece = ("v", 2 * (v // UNITS) + 1 + v % UNITS // 2, v % 2 * 2 + int(name[1]))
            if v >= 0 and piece[1] < 2 * PAIRS:
                out.append((what, v, piece))
        elif v == -1 and name[0] == "P":
            out.append((what, v, ("v", 0, 2 + int(name[1]))))
        elif 0 <= v < ALL_UNITS:
            if name[0] == "P":
                out.append((what, v, ("pv", v, int(name[1]))))
            elif name[0] == "W":
                out.append((what, v, ("wo", v, int(name[1]), int(name[2]))))
            else:
                out.append((what, v, tuple(int(x) for x in name.split("."))))
    return out


FIRST_QK = [("qk", 0, 1, 0), ("qk", 0, 0, 0), ("qk", 0, 1, 1), ("qk", 0, 0, 1)]
FIRST_V = [("v", 0, 0), ("v", 0, 1)]
BEFORE_LOOP = FIRST_QK + FIRST_V + [piece for what, _, piece in unit_plan(TENSOR_PLAN, 0) if what == "make"]
PIECES = FIRST_QK + FIRST_V + [piece for u in range(ALL_UNITS + 1) for what, _, piece in unit_plan(TENSOR_PLAN, u)
                               if what == "make"]
PIECE_AT = {piece: n for n, piece in enumerate(PIECES)}
RANK = {piece: sum(other[0] == piece[0] for other in PIECES[:n]) for piece, n in PIECE_AT.items()}
PER_PASS = {"qk": 4 * UNITS, "v": 2 * UNITS, "pv": 2 * UNITS, "wo": 4 * UNITS}
PIECES_PER_PASS = sum(PER_PASS.values())


class Span:

    def __init__(self, first, last, i=None):
        self.i = i
        self.units = range(first, last) if i is None else range(first + UNITS, last + UNITS)

    def work(self, plan):
        return [x for u in self.units for x in unit_plan(plan, u)]

    def count(self, n, per_round):
        return n if self.i is None else self.i * per_round + (n - per_round)

    def pieces(self, piece):
        return self.count(PIECE_AT[piece] + 1, PIECES_PER_PASS)

    def rank(self, piece, more=0):
        return self.count(RANK[piece] + more, PER_PASS[piece[0]])

    def bank(self, piece):
        return PIECE_AT[piece] % 2

    def before(self, piece):
        n = PIECE_AT[piece]
        return PIECES[n - 2] if n >= 2 else None

    def tiles(self, u, step):
        return self.count(u * NQ + step, TILES)

    def passes(self, n):
        return self.count(n, 1)

    def groups(self, u, step, more=0):
        return self.count(u * T_UNIT + T_FIRST[step] + more, UNITS * T_UNIT)


def unit_batch(u):
    return u // 2 % BATCH


def build(nc, x, wq, bq, wk, bk, wv, bv, wo, bo, wq_gate, s_gate, wq_up, s_up, wq_down, s_down, c, wmod,
          cos, sin, out):
    with ExitStack() as ctx:
        def sem(name):
            return ctx.enter_context(nc.semaphore(name))

        base = (nc.sbuf_base + 31) // 32 * 32
        KB = 1024
        A_HTH, A_HTL, A_Y = 0, 16 * KB, 32 * KB
        A_QK, A_V, A_PT = 48 * KB, 80 * KB, 112 * KB
        A_W, A_ROPE, A_RAW, A_P, A_SMALL = 148 * KB, 172 * KB, 188 * KB, 194 * KB, 194 * KB + 512 * P_BLOCKS
        A_WO, A_O = A_W + 12 * KB, A_W + 16 * KB
        small_at = [A_SMALL]

        def at(name, offset, shape, dt):
            return nc.alloc_sbuf_tensor_at(name, shape, dt, offset=base + offset)

        def small(name, shape, dt):
            size = int(np.prod(shape[1:])) * (2 if dt == BF16 else 4)
            t = at(name, small_at[0], shape, dt)
            small_at[0] += (size + 31) // 32 * 32
            return t

        hT_hi = at("hT_hi", A_HTH, [P, KT, TOK], F32R)
        hT_lo = at("hT_lo", A_HTL, [P, KT, TOK], F32R)
        y = at("y", A_Y, [P, NTT, DIM], F32)
        qk_hi = at("qk_hi", A_QK, [P, 2, 2, SEQ], F32R)
        qk_lo = at("qk_lo", A_QK + 16 * KB, [P, 2, 2, SEQ], F32R)
        v_hi = at("v_hi", A_V, [P, BATCH, NQ, 2 * DH], F32R)
        v_lo = at("v_lo", A_V + 16 * KB, [P, BATCH, NQ, 2 * DH], F32R)
        pT_hi = at("pT_hi", A_PT, [P, NQ + 1, CH], F32R)
        pT_lo = at("pT_lo", A_PT + 18 * KB, [P, NQ + 1, CH], F32R)
        w_hi = at("w_hi", A_W, [P, 3, KT, 2 * DH], F32R)
        w_lo = at("w_lo", A_W + 6 * KB, [P, 3, KT, 2 * DH], F32R)
        wo_hi = at("wo_hi", A_WO, [P, 2, DIM], F32R)
        wo_lo = at("wo_lo", A_WO + 2 * KB, [P, 2, DIM], F32R)
        o_hi = at("o_hi", A_O, [P, 2, CH], F32R)
        o_lo = at("o_lo", A_O + 4 * KB, [P, 2, CH], F32R)
        cos_sb = at("cos_sb", A_ROPE, [P, SEQ], F32)
        sin_sb = at("sin_sb", A_ROPE + 4 * KB, [P, SEQ], F32)
        straight = at("straight", A_ROPE + 8 * KB, [P, 2, CH], F32)
        swapped = at("swapped", A_ROPE + 12 * KB, [P, 2, CH], F32)
        w_raw = at("w_raw", A_RAW, [P, 3, KT, 2 * DH], F32)
        wo_raw = at("wo_raw", A_RAW + 4 * KB, [P, 2, DIM], F32)
        probs = at("probs", A_P, [P, P_BLOCKS * P], F32)
        ident = small("ident", [P, P], F32)
        ident_b = small("ident_b", [P, P], BF16)
        mask_b = small("mask_b", [P, P], BF16)
        attn_bias = small("attn_bias", [P, DIM], F32)
        rows = small("rows", [NROWS, P], F32)
        cols = small("cols", [P, NROWS], F32)
        bq_s = small("bq_s", [P, HEADS], F32)
        tanh_c = small("tanh_c", [P, BATCH * KT], F32)
        silu_c = small("silu_c", [P, BATCH * KT], F32)
        mod = small("mod", [P, 8, BATCH], F32)
        bn = small("bn", [P, NTT, 6], F32)
        mv = small("mv", [P, NTT, 2], F32)
        var = small("var", [P, NTT], F32)
        root = small("root", [P, NTT], F32)
        rstd = small("rstd", [P, NTT], F32)
        newton = small("newton", [P, NTT], F32)
        neg_max = small("neg_max", [P, NQ], F32)
        row_sum = small("row_sum", [P, 2, NQ], F32)
        inv_sum = small("inv_sum", [P, 2, NQ], F32)
        assert base + small_at[0] <= nc.sbuf_usable_end, (base + small_at[0], nc.sbuf_usable_end)

        x_in = at("x_in", A_QK, [P, NTT, DIM], F32)
        wmod_a = at("wmod_a", A_QK + 16 * KB, [P, KT, 4, DIM], F32)
        xn = at("xn", A_PT, [P, NTT, DIM], F32)
        h32 = at("h32", A_PT + 16 * KB, [P, 2, CH], F32)
        bv_wide = at("bv_wide", A_PT + 20 * KB, [P, HEADS, P], F32)
        wo_all = at("wo_all", A_V + 16 * KB, [P, HEADS, DIM], F32)
        bo_wide = at("bo_wide", A_PT + 28 * KB, [P, DIM], F32)
        x2 = at("x2", A_QK, [P, NTT, DIM], F32)
        int_gate = at("int_gate", A_QK + 16 * KB, [P, HM, DIM], I32)
        int_up = at("int_up", A_QK + 22 * KB, [P, HM, DIM], I32)
        wmod_g = at("wmod_g", A_QK + 28 * KB, [P, KT, 2, DIM], F32)
        int_down = at("int_down", A_RAW, [P, KT, HID], I32)
        f_gate = at("f_gate", A_V, [P, HM, DIM], F32)
        f_up = at("f_up", A_V + 6 * KB, [P, HM, DIM], F32)
        f_down = at("f_down", A_V + 12 * KB, [P, KT, HID], F32)
        wd_hi = at("wd_hi", A_V + 18 * KB, [P, HM, DIM], F32R)
        wd_lo = at("wd_lo", A_V + 24 * KB, [P, HM, DIM], F32R)
        wg_hi = at("wg_hi", A_PT, [P, 2, KT, HID], F32R)
        wg_lo = at("wg_lo", A_PT + 11 * KB, [P, 2, KT, HID], F32R)
        h2_32 = at("h2_32", A_PT + 22 * KB, [P, 2, CH], F32)
        g_row = at("g_row", A_PT + 26 * KB, [P, 2, BATCH, DIM], F32)
        silu_w = at("silu_w", A_PT + 30 * KB, [P, BATCH * KT, P], F32)
        xn2 = at("xn2", A_ROPE, [P, NTT, DIM], F32)
        gu_hi = at("gu_hi", A_W, [P, HM, CH], F32R)
        gu_lo = at("gu_lo", A_W + 12 * KB, [P, HM, CH], F32R)
        tanh_g = at("tanh_g", A_P, [P, 2, CH], F32)
        lin_g = at("lin_g", A_P + 4 * KB, [P, 2, CH], F32)
        gu = at("gu", A_QK + 16 * KB, [P, 2, CH], F32)
        g_sign = at("g_sign", A_V + 30 * KB, [P, BATCH, DIM], F32)
        half_su = small("half_su", [P, HM], F32)
        half_sg = small("half_sg", [P, HM], F32)
        sd_wide = at("sd_wide", A_P + 8 * KB, [P, DIM], F32)
        assert base + small_at[0] <= nc.sbuf_usable_end, (base + small_at[0], nc.sbuf_usable_end)

        ps_s = ctx.enter_context(nc.psum_tensor("ps_s", [P, 2, SEQ], F32))
        ps_t = ctx.enter_context(nc.psum_tensor("ps_t", [P, 2, CH], F32))
        ps_r = ctx.enter_context(nc.psum_tensor("ps_r", [P, 2, CH], F32))

        zeroed = sem("zeroed")
        consts_ready = sem("consts_ready")
        rows_ready = sem("rows_ready")
        x_ready = [sem(f"x_ready{n}") for n in range(NCH)]
        wmod_ready = sem("wmod_ready")
        tables_ready = sem("tables_ready")
        raw_ready = [sem(f"raw_{x}_ready") for x in ("wq", "wk", "wv", "wo")]
        wo_all_ready = sem("wo_all_ready")
        cols_turned = sem("cols_turned")
        cols_ready = sem("cols_ready")
        tanh_ready = sem("tanh_ready")
        silu_ready = sem("silu_ready")
        mod_made = sem("mod_made")
        mod_ready = sem("mod_ready")
        var_ready = sem("var_ready")
        root_ready = sem("root_ready")
        xn_ready = sem("xn_ready")
        xn_turned = sem("xn_turned")
        h32_ready = sem("h32_ready")
        hhi_ready = sem("hhi_ready")
        hT_ready = sem("hT_ready")
        bv_wide_ready = sem("bv_wide_ready")
        attn_bias_made = sem("attn_bias_made")
        attn_bias_ready = sem("attn_bias_ready")
        pool_chain = sem("pool_chain")
        dve_chain = sem("dve_chain")
        gain_ready = sem("gain_ready")

        w_hi_ready = [sem(f"{x}_hi_ready") for x in ("wq", "wk", "wv", "wo")]
        w_ready = [sem(f"{x}_ready") for x in ("wq", "wk", "wv", "wo")]
        scores_ready = sem("scores_ready")
        max_ready = sem("max_ready")
        exp_ready = sem("exp_ready")
        turned = sem("turned")
        pT_hi_ready = sem("pT_hi_ready")
        pT_ready = sem("pT_ready")
        piece_made = sem("piece_made")
        y_added = sem("y_added")
        straight_ready = sem("straight_ready")
        swapped_ready = [sem(f"swapped_ready{n}") for n in range(2)]
        rotated = sem("rotated")
        qk_sum = sem("qk_sum")
        qk_hi_ready = sem("qk_hi_ready")
        qk_ready = sem("qk_ready")
        v_hi_ready = sem("v_hi_ready")
        v_ready = sem("v_ready")
        o_hi_ready = sem("o_hi_ready")
        o_ready = sem("o_ready")
        inv_ready = sem("inv_ready")

        ints_ready = sem("ints_ready")
        down_ready = sem("down_ready")
        x2_in_ready = sem("x2_in_ready")
        wmod_g_ready = sem("wmod_g_ready")
        silu_w_ready = sem("silu_w_ready")
        g_made = sem("g_made")
        g_ready = sem("g_ready")
        y_done = sem("y_done")
        x2_ready = sem("x2_ready")
        var2_ready = sem("var2_ready")
        root2_ready = sem("root2_ready")
        xn2_ready = sem("xn2_ready")
        xn2_turned = sem("xn2_turned")
        h2_32_ready = sem("h2_32_ready")
        h2_hi_ready = sem("h2_hi_ready")
        h2_ready = sem("h2_ready")
        wf_ready = sem("wf_ready")
        wf_turned = sem("wf_turned")
        wf_hi_ready = sem("wf_hi_ready")
        wf_lo_ready = sem("wf_lo_ready")
        gate_made = sem("gate_made")
        up_made = sem("up_made")
        lin_ready = sem("lin_ready")
        tanh_g_ready = sem("tanh_g_ready")
        silu_g_ready = sem("silu_g_ready")
        gu_ready = sem("gu_ready")
        gu_hi_ready = sem("gu_hi_ready")
        gu_split = sem("gu_split")
        down_made = sem("down_made")
        out_ready = sem("out_ready")
        stored = sem("stored")

        block = ctx.enter_context(nc.Block())

        x_t = x.rearrange("b (t p) d -> p (b t) d", p=P)
        out_t = out.rearrange("b (t p) d -> p (b t) d", p=P)
        wmod_t = wmod.rearrange("(k p) (j d) -> p k j d", p=P, d=DIM)
        w_t = [w.rearrange("(k p) n -> p k n", p=P) for w in (wq, wk, wv)]
        wo_t = wo.rearrange("(h p) n -> p h n", p=P)
        LAST = PAIRS - 1
        GROUPS4 = TOK // CH * KT

        w_buffers = [(w_raw[:, j, :, :], w_hi[:, j, :, :], w_lo[:, j, :, :]) for j in range(3)]
        w_buffers.append((wo_raw[:, :, :], wo_hi[:, :, :], wo_lo[:, :, :]))

        def turned_at(t, k0, k1):
            if t < 4:
                return lambda pT: pT.rearrange("p s q -> p (s q)")[:, t * P:t * P + (t + 1) * 3 * P]\
                    .rearrange("p (k q) -> p k q", q=3 * P)[:, :, 0:P]
            return lambda pT: pT[:, 9 - k1:9 - k0, (t - 4) * P:(t - 4) * P + P]

        def groups_of(t):
            return [(k0, min(k0 + 4, t + 1)) for k0 in range(0, t + 1, 4)]

        def qk_at(parity, which, first, size):
            return (qk_hi[:, parity, which, first:first + size], qk_lo[:, parity, which, first:first + size])

        @block.sync
        def _(sp):
            def load_w(j, n):
                if j == WO:
                    src = wo_t[:, bass.ds(n * 2, 2), :]
                else:
                    src = w_t[j][:, :, bass.ds(n * 2 * DH, 2 * DH)]
                sp.dma_start(w_buffers[j][0], src).then_inc(raw_ready[j], 16)

            sp.wait_ge(zeroed, 1)
            for src, r0, n in ((bq, ROW_BQ, HEADS), (bk, ROW_BK, HEADS), (bv, ROW_BV, HEADS)):
                sp.dma_start(rows[r0:r0 + n, :], src.rearrange("(h d) -> h d", d=DH)).then_inc(rows_ready, 16)
            sp.dma_start(rows[ROW_C:ROW_SG, :], c.rearrange("b (k p) -> (b k) p", p=P)).then_inc(rows_ready, 16)
            for src, r0 in ((s_gate, ROW_SG), (s_up, ROW_SU)):
                sp.dma_start(rows[r0:r0 + HM - 1, :], src[0:(HM - 1) * P].rearrange("(m p) -> m p", p=P))\
                    .then_inc(rows_ready, 16)
                sp.dma_start(rows[r0 + HM - 1:r0 + HM, 0:HLAST],
                             src[(HM - 1) * P:HID].rearrange("(a p) -> a p", a=1)).then_inc(rows_ready, 16)
            for n in range(NCH):
                sp.dma_start(x_in[:, 4 * n:4 * n + 4, :], x_t[:, 4 * n:4 * n + 4, :]).then_inc(x_ready[n], 16)
                if n == 1:
                    for j, part in enumerate((0, 1, 3, 4)):
                        sp.dma_start(wmod_a[:, :, j, :], wmod_t[:, :, part, :]).then_inc(wmod_ready, 16)
                    for j in (WK, WQ, WV):
                        load_w(j, 0)
            sp.dma_start(cos_sb[:, :], cos).then_inc(tables_ready, 16)
            sp.dma_start(sin_sb[:, :], sin).then_inc(tables_ready, 16)
            sp.dma_start(wo_all[:, :, :], wo_t).then_inc(wo_all_ready, 16)
            sp.dma_start(bo_wide[:, :], bo.rearrange("(a n) -> a n", a=1).broadcast_to([P, DIM]))\
                .then_inc(wo_all_ready, 16)

            def swap_halves(ps, piece):
                q = RANK[piece] % 2
                sp.wait_ge(straight_ready, ps.rank(piece, 1))
                half = DH // 2
                for a, b in ((0, half), (half, 0)):
                    sp.dma_start(swapped[a:a + half, q, :], straight[b:b + half, q, :])\
                        .then_inc(swapped_ready[q], 16)

            def run(ps):
                for u in ps.units:
                    n = u // UNITS + 1
                    qk = [piece for what, _, piece in unit_plan(TENSOR_PLAN, u) if what == "make" and piece[0] == "qk"]
                    for piece in qk:
                        swap_halves(ps, piece)
                    if n < PAIRS and u % UNITS == 1:
                        for j, shared in ((WK, WK), (WQ, WQ), (WV, WO)):
                            sp.wait_ge(w_ready[shared], ps.passes(n))
                            load_w(j, ps.passes(n))
                    if n < PAIRS and u % UNITS == 2:
                        sp.wait_ge(w_ready[WV], ps.passes(n + 1))
                        load_w(WO, ps.passes(n))

            for piece in FIRST_QK:
                swap_halves(Span(0, 0), piece)
            sp.wait_ge(w_ready[WV], 1)
            load_w(WO, 0)
            run(Span(0, 1))
            with sp.Fori(0, LAST) as i:
                run(Span(1, 1 + UNITS, i))
            run(Span(1 + LAST * UNITS, ALL_UNITS + 1))

            sp.wait_ge(scores_ready, PAIRS * TILES)
            sp.dma_start(wmod_g[:, :, 0, :], wmod_t[:, :, 2, :]).then_inc(wmod_g_ready, 16)
            sp.dma_start(wmod_g[:, :, 1, :], wmod_t[:, :, 5, :]).then_inc(wmod_g_ready, 16)
            for n in range(NCH):
                sp.dma_start(x2[:, 4 * n:4 * n + 4, :], x_t[:, 4 * n:4 * n + 4, :]).then_inc(x2_in_ready, 16)
            for dst, src in ((int_gate, wq_gate), (int_up, wq_up)):
                sp.dma_start(dst[:, 0:HM - 1, :], src[0:(HM - 1) * P, :].rearrange("(m p) d -> p m d", p=P))\
                    .then_inc(ints_ready, 16)
                sp.dma_start(dst[0:HLAST, HM - 1, :], src[(HM - 1) * P:HID, :]).then_inc(ints_ready, 16)
            for j in range(4):
                sp.wait_ge(w_ready[j], PAIRS)
            sp.dma_start(int_down[:, :, :], wq_down.rearrange("(k p) h -> p k h", p=P)).then_inc(down_ready, 16)
            sp.wait_ge(turned, PAIRS * UNITS * T_UNIT)
            sp.dma_start(sd_wide[:, :], s_down.rearrange("(a n) -> a n", a=1).broadcast_to([P, DIM]))\
                .then_inc(down_ready, 16)
            for n in range(NTT // 2):
                sp.wait_ge(out_ready, n + 1)
                sp.dma_start(out_t[:, 2 * n:2 * n + 2, :], y[:, 2 * n:2 * n + 2, :]).then_inc(stored, 16)
            sp.wait_ge(stored, 16 * (NTT // 2))

        @block.gpsimd
        def _(pool):
            pool.memset(rows[:, :], 0.0).then_inc(zeroed, 1)
            pool.memset(ident[:, :], 0.0).then_inc(pool_chain, 1)
            pool.memset(mask_b[:, :], 0.0).then_inc(pool_chain, 1)
            pool.wait_ge(pool_chain, 2)
            pool.affine_select(out=ident[:, :], in_=ident[:, :], compare_op=ALU.not_equal, fill=1.0, base=0,
                               pattern=[[-1, P]], channel_multiplier=1).then_inc(pool_chain, 1)
            pool.affine_select(out=mask_b[:, :], in_=mask_b[:, :], compare_op=ALU.is_ge, fill=MASKED, base=0,
                               pattern=[[-1, P]], channel_multiplier=1).then_inc(consts_ready, 1)
            pool.wait_ge(pool_chain, 3)
            pool.tensor_copy(ident_b[:, :], ident[:, :]).then_inc(consts_ready, 1)
            pool.memset(y[:, :, :], 0.0).then_inc(y_added, 1)

            def w_low(j, n):
                raw, hi, lo = w_buffers[j]
                pool.wait_ge(w_hi_ready[j], n + 1)
                pool.tensor_tensor(lo, raw, hi.bitcast(F32), ALU.subtract).then_inc(w_ready[j], 1)

            def rotate(ps, piece):
                q, chunk = RANK[piece] % 2, piece[3]
                pool.wait_ge(swapped_ready[q], ps.count(RANK[piece] // 2 * 32 + 32, PER_PASS["qk"] // 2 * 32))
                cs = slice(chunk * CH, chunk * CH + CH)
                pool.tensor_tensor(swapped[:, q, :], swapped[:, q, :], sin_sb[:, cs], ALU.mult)
                pool.tensor_tensor(straight[:, q, :], straight[:, q, :], cos_sb[:, cs], ALU.mult).then_inc(rotated, 1)

            def qk_low(ps, piece):
                _, unit, which, chunk = piece
                pool.wait_ge(qk_hi_ready, ps.rank(piece, 1))
                hi, lo = qk_at(unit % 2, which, chunk * CH, CH)
                pool.tensor_tensor(lo, straight[:, RANK[piece] % 2, :], hi.bitcast(F32), ALU.subtract)\
                    .then_inc(qk_ready, 1)

            pool.wait_ge(cols_ready, 1)
            pool.tensor_copy(bv_wide[:, :, :], cols[:, ROW_BV:ROW_BV + HEADS, None].broadcast_to([P, HEADS, P]))\
                .then_inc(bv_wide_ready, 1)
            for j in (WK, WQ, WV):
                w_low(j, 0)
            for n in range(GROUPS4):
                pool.wait_ge(hhi_ready, n + 1)
                part = (slice(None), n % KT, slice(n // KT * CH, n // KT * CH + CH))
                pool.tensor_tensor(hT_lo[part], h32[:, n % 2, :], hT_hi[part].bitcast(F32), ALU.subtract)\
                    .then_inc(hT_ready, 1)
            pool.wait_ge(tables_ready, 32)
            for piece in FIRST_QK:
                rotate(Span(0, 0), piece)
                qk_low(Span(0, 0), piece)

            def run(ps):
                for what, x, piece in ps.work(POOL_PLAN):
                    if what == "rotate":
                        rotate(ps, piece)
                    elif what == "low":
                        qk_low(ps, piece)
                    else:
                        w_low(x, ps.passes(piece))

            run(Span(0, 1))
            with pool.Fori(0, LAST) as i:
                run(Span(1, 1 + UNITS, i))
            run(Span(1 + LAST * UNITS, ALL_UNITS + 1))

            pool.wait_ge(turned, PAIRS * UNITS * T_UNIT)
            pool.wait_ge(o_hi_ready, PAIRS * 8)
            pool.tensor_copy(silu_w[:, :, :], silu_c[:, :, None].broadcast_to([P, BATCH * KT, P]))\
                .then_inc(silu_w_ready, 1)
            pool.wait_ge(ints_ready, 64)
            for dst, src in ((f_gate, int_gate), (f_up, int_up)):
                pool.tensor_scalar(dst[:, 0:HM - 1, :], src[:, 0:HM - 1, :], -ZERO_POINT, None, ALU.add)
                pool.tensor_scalar(dst[0:HLAST, HM - 1, :], src[0:HLAST, HM - 1, :], -ZERO_POINT, None, ALU.add)\
                    .then_inc(wf_ready, 1)
            pool.wait_ge(down_ready, 32)
            pool.tensor_scalar(f_down[:, :, :], int_down[:, :, :], -ZERO_POINT, None, ALU.add).then_inc(wf_ready, 1)
            for n in range(GROUPS4):
                pool.wait_ge(h2_hi_ready, n + 1)
                part = (slice(None), n % KT, slice(n // KT * CH, n // KT * CH + CH))
                pool.tensor_tensor(hT_lo[part], h2_32[:, n % 2, :], hT_hi[part].bitcast(F32), ALU.subtract)\
                    .then_inc(h2_ready, 1)
            for n in range(NCH * HM):
                size = P if n % HM < HM - 1 else HLAST
                pool.wait_ge(gu_hi_ready, n + 1)
                pool.tensor_tensor(gu_lo[0:size, n % HM, :], gu[0:size, n % 2, :],
                                   gu_hi[0:size, n % HM, :].bitcast(F32), ALU.subtract).then_inc(gu_split, 1)

        @block.scalar
        def _(act):
            def w_high(j):
                raw, hi, _ = w_buffers[j]
                nc.scalar.activation(hi, raw, ACT.Copy).then_inc(w_hi_ready[j], 1)

            def qk_out(ps, piece):
                _, unit, which, _ = piece
                q = RANK[piece] % 2
                act.wait_ge(piece_made, ps.pieces(piece))
                if RANK[piece] >= 2:
                    act.wait_ge(qk_ready, ps.rank(piece, -1))
                act.nop(nofuse=True)
                head = ps.count(unit // UNITS * 2 + unit % 2, 2)
                bias = (bq_s if which == 0 else cols[:, ROW_BK:ROW_BK + HEADS])[:, bass.ds(head, 1)]
                nc.scalar.activation(straight[:, q, :], ps_r[:, ps.bank(piece), :], ACT.Identity, bias=bias,
                                     scale=SCALE if which == 0 else 1.0).then_inc(straight_ready, 1)

            def qk_high(ps, piece):
                _, unit, which, chunk = piece
                act.wait_ge(qk_sum, ps.rank(piece, 1))
                hi, _ = qk_at(unit % 2, which, chunk * CH, CH)
                nc.scalar.activation(hi, straight[:, RANK[piece] % 2, :], ACT.Copy).then_inc(qk_hi_ready, 1)

            def v_high(ps, piece):
                _, pb, j = piece
                act.wait_ge(piece_made, ps.pieces(piece))
                nc.scalar.activation(v_hi[:, pb % BATCH, 2 * j:2 * j + 2, :],
                                     ps_r[:, ps.bank(piece), :].rearrange("p (t n) -> p t n", t=2),
                                     ACT.Copy).then_inc(v_hi_ready, 1)

            def o_high(ps, piece):
                act.wait_ge(piece_made, ps.pieces(piece))
                nc.scalar.activation(o_hi[:, piece[2], :], ps_r[:, ps.bank(piece), :], ACT.Copy).then_inc(o_hi_ready, 1)

            act.wait_ge(cols_turned, 1)
            nc.scalar.activation(cols[:, :], ps_r[:, 0, 0:NROWS], ACT.Copy).then_inc(cols_ready, 1)
            act.wait_ge(cols_ready, 1)
            nc.scalar.activation(tanh_c[:, :], cols[:, ROW_C:ROW_SG], ACT.Tanh, scale=0.5).then_inc(tanh_ready, 1)
            for j in (WK, WQ, WV):
                act.wait_ge(raw_ready[j], 16)
                w_high(j)
            act.wait_ge(mod_made, 1)
            nc.scalar.activation(mod[:, :, :], ps_r[:, 1, 0:8 * BATCH].rearrange("p (j b) -> p j b", b=BATCH),
                                 ACT.Copy).then_inc(mod_ready, 1)
            act.wait_ge(var_ready, 1)
            nc.scalar.activation(root[:, :], var[:, :], ACT.Sqrt).then_inc(root_ready, 1)
            act.wait_ge(gain_ready, 2)
            for n in range(GROUPS4):
                k, b = n % KT, n // KT // 2
                act.wait_ge(xn_turned, n + 1)
                if n >= 2:
                    act.wait_ge(hT_ready, n - 1)
                src, shift, gain = ps_t[:, n % 2, :], mod[:, k, b:b + 1], mod[:, KT + k, b:b + 1]
                nc.scalar.activation(h32[:, n % 2, :], src, ACT.Identity, bias=shift, scale=gain).then_inc(h32_ready, 1)
                nc.scalar.activation(hT_hi[:, k, n // KT * CH:n // KT * CH + CH], src, ACT.Identity, bias=shift,
                                     scale=gain).then_inc(hhi_ready, 1)
            for n, piece in enumerate(FIRST_QK):
                qk_out(Span(0, 0), piece)
                if n:
                    qk_high(Span(0, 0), FIRST_QK[n - 1])
            qk_high(Span(0, 0), FIRST_QK[3])

            for piece in FIRST_V:
                v_high(Span(0, 0), piece)

            def turn_out(ps, u, step, j):
                k0, k1 = groups_of(ORDER[step])[j]
                act.wait_ge(turned, ps.groups(u, step, j + 1))
                nc.scalar.activation(
                    turned_at(ORDER[step], k0, k1)(pT_hi),
                    ps_t[:, (T_FIRST[step] + j) % 2, 0:(k1 - k0) * P].rearrange("p (k q) -> p k q", q=P),
                    ACT.Copy).then_inc(pT_hi_ready, 1)

            def exponentials(ps, u, step):
                t = ORDER[step]
                act.wait_ge(max_ready, ps.tiles(u, step + 1))
                if u * NQ + step >= 3:
                    act.wait_ge(turned, ps.groups(*divmod(u * NQ + step - 2, NQ)))
                nc.scalar.activation(probs[:, P_AT[step] * P:(P_AT[step] + t + 1) * P], ps_s[:, step % 2, 0:(t + 1) * P],
                                     ACT.Exp, bias=neg_max[:, t:t + 1],
                                     accum_out=row_sum[:, u % 2, t:t + 1]).then_inc(exp_ready, 1)

            def split_weights(ps, j, n):
                act.wait_ge(raw_ready[j], ps.count(n * 16 + 16, 16))
                used = {WO: ("wo", n * UNITS - 1, 1, 1), WV: ("v", 2 * n - 1, 3), WK: ("qk", n * UNITS - 1, 1, 1),
                        WQ: ("qk", n * UNITS - 1, 0, 1)}[j]
                if used in PIECE_AT:
                    act.wait_ge(piece_made, ps.pieces(used))
                w_high(j)

            def run(ps):
                for what, x, piece in ps.work(SCALAR_PLAN):
                    if what == "exp":
                        exponentials(ps, x, *piece)
                    elif what == "turn":
                        turn_out(ps, x, *piece)
                    elif what == "split":
                        split_weights(ps, x, piece)
                    elif what == "out":
                        qk_out(ps, piece)
                    else:
                        {"qk": qk_high, "v": v_high, "pv": o_high}[piece[0]](ps, piece)

            run(Span(0, 1))
            with act.Fori(0, LAST) as i:
                run(Span(1, 1 + UNITS, i))
            run(Span(1 + LAST * UNITS, ALL_UNITS + 1))

            for n in range(3 * HM):
                which, m = divmod(n, HM)
                size = P if m < HM - 1 else HLAST
                act.wait_ge(wf_turned, n + 1)
                if which < 2:
                    dst = wg_hi[:, which, :, m * P:m * P + size]
                    src = ps_t[:, n % 2, 0:KT * size].rearrange("p (k h) -> p k h", k=KT)
                else:
                    dst, src = wd_hi[0:size, m, :], ps_t[0:size, n % 2, 0:DIM]
                nc.scalar.activation(dst, src, ACT.Copy).then_inc(wf_hi_ready, 1)
            act.wait_ge(var2_ready, 1)
            nc.scalar.activation(root[:, :], var[:, :], ACT.Sqrt).then_inc(root2_ready, 1)
            for n in range(GROUPS4):
                k, b = n % KT, n // KT // 2
                act.wait_ge(xn2_turned, n + 1)
                if n >= 2:
                    act.wait_ge(h2_ready, n - 1)
                src, shift, gain = ps_t[:, n % 2, :], mod[:, 2 * KT + k, b:b + 1], mod[:, 3 * KT + k, b:b + 1]
                nc.scalar.activation(h2_32[:, n % 2, :], src, ACT.Identity, bias=shift, scale=gain)\
                    .then_inc(h2_32_ready, 1)
                nc.scalar.activation(hT_hi[:, k, n // KT * CH:n // KT * CH + CH], src, ACT.Identity, bias=shift,
                                     scale=gain).then_inc(h2_hi_ready, 1)

            def gu_high(n):
                m = n % HM
                size = P if m < HM - 1 else HLAST
                act.wait_ge(gu_ready, n + 1)
                if n >= HM:
                    act.wait_ge(down_made, n // HM * 2)
                nc.scalar.activation(gu_hi[0:size, m, :], gu[0:size, n % 2, :], ACT.Copy).then_inc(gu_hi_ready, 1)

            for n in range(NCH * HM):
                m = n % HM
                size = P if m < HM - 1 else HLAST
                act.wait_ge(gate_made, n + 1)
                if n >= 2:
                    act.wait_ge(gu_ready, n - 1)
                src = ps_s[0:size, n % 2, 0:CH]
                nc.scalar.activation(tanh_g[0:size, n % 2, :], src, ACT.Tanh, scale=half_sg[0:size, m:m + 1])\
                    .then_inc(tanh_g_ready, 1)
                nc.scalar.activation(lin_g[0:size, n % 2, :], src, ACT.Copy,
                                     scale=cols[0:size, ROW_SG + m:ROW_SG + m + 1]).then_inc(lin_ready, 1)
                if n >= 1:
                    gu_high(n - 1)
            gu_high(NCH * HM - 1)

        @block.vector
        def _(dve):
            linked = [0]

            def link(ins):
                linked[0] += 1
                ins.then_inc(dve_chain, 1)
                dve.wait_ge(dve_chain, linked[0])

            def norm(src, dst, tile_ready, var_sem, root_sem, done):
                for t in range(NTT):
                    if t % 4 == 0:
                        tile_ready(t // 4)
                    last = nc.vector.bn_stats(bn[:, t, :], src[:, t, :])
                link(last)
                for t in range(NTT):
                    last = nc.vector.bn_aggr(mv[:, t, :], bn[:, t, :])
                link(last)
                nc.vector.tensor_scalar(var[:, :], mv[:, :, 1], EPS, None, ALU.add).then_inc(var_sem, 1)
                dve.wait_ge(root_sem, 1)
                link(nc.vector.reciprocal(rstd[:, :], root[:, :]))
                link(nc.vector.tensor_tensor(newton[:, :], rstd[:, :], rstd[:, :], ALU.mult))
                link(nc.vector.tensor_tensor(newton[:, :], newton[:, :], var[:, :], ALU.mult))
                link(nc.vector.tensor_scalar(newton[:, :], newton[:, :], -0.5, 1.5, ALU.mult, ALU.add))
                link(nc.vector.tensor_tensor(rstd[:, :], rstd[:, :], newton[:, :], ALU.mult))
                for t in range(NTT):
                    ins = nc.vector.tensor_scalar(dst[:, t, :], src[:, t, :], mv[:, t, 0:1], rstd[:, t:t + 1],
                                                  ALU.subtract, ALU.mult)
                    if t % 4 == 3:
                        ins.then_inc(done, 1)

            dve.wait_ge(tanh_ready, 1)
            link(nc.vector.scalar_tensor_tensor(silu_c[:, :], tanh_c[:, :], 1.0, cols[:, ROW_C:ROW_SG], ALU.add, ALU.mult))
            nc.vector.tensor_scalar(silu_c[:, :], silu_c[:, :], 0.5, None, ALU.mult).then_inc(silu_ready, 1)
            nc.vector.tensor_scalar(bq_s[:, :], cols[:, ROW_BQ:ROW_BQ + HEADS], SCALE, None, ALU.mult)
            nc.vector.tensor_scalar(half_sg[:, :], cols[:, ROW_SG:ROW_SG + HM], 0.5, None, ALU.mult)
            nc.vector.tensor_scalar(half_su[:, :], cols[:, ROW_SU:ROW_SU + HM], 0.5, None, ALU.mult)
            dve.wait_ge(mod_ready, 1)
            for j in (1, 3):
                nc.vector.tensor_scalar(mod[:, KT * j:KT * j + KT, :], mod[:, KT * j:KT * j + KT, :], 1.0, None,
                                        ALU.add).then_inc(gain_ready, 1)
            norm(x_in, xn, lambda n: dve.wait_ge(x_ready[n], 16), var_ready, root_ready, xn_ready)
            dve.wait_ge(wo_all_ready, 32)
            dve.wait_ge(attn_bias_made, 1)
            nc.vector.tensor_tensor(attn_bias[:, :], ps_s[:, 0, 0:DIM], bo_wide[:, :], ALU.add)\
                .then_inc(attn_bias_ready, 1)

            def qk_add(ps, piece):
                q = RANK[piece] % 2
                dve.wait_ge(rotated, ps.rank(piece, 1))
                nc.vector.tensor_tensor(straight[:, q, :], straight[:, q, :], swapped[:, q, :], ALU.add)\
                    .then_inc(qk_sum, 1)

            def v_low(ps, piece):
                _, pb, j = piece
                dve.wait_ge(v_hi_ready, ps.rank(piece, 1))
                part = (slice(None), pb % BATCH, slice(2 * j, 2 * j + 2), slice(None))
                nc.vector.tensor_tensor(v_lo[part], ps_r[:, ps.bank(piece), :].rearrange("p (t n) -> p t n", t=2),
                                        v_hi[part].bitcast(F32), ALU.subtract).then_inc(v_ready, 1)

            def o_low(ps, piece):
                chunk = piece[2]
                dve.wait_ge(o_hi_ready, ps.rank(piece, 1))
                nc.vector.tensor_tensor(o_lo[:, chunk, :], ps_r[:, ps.bank(piece), :], o_hi[:, chunk, :].bitcast(F32),
                                        ALU.subtract).then_inc(o_ready, 1)

            for piece in FIRST_QK:
                qk_add(Span(0, 0), piece)
            for piece in FIRST_V:
                v_low(Span(0, 0), piece)

            def turn_low(ps, u, step, j):
                t = ORDER[step]
                k0, k1 = groups_of(t)[j]
                dve.wait_ge(pT_hi_ready, ps.groups(u, step, j + 1))
                nc.vector.tensor_tensor(
                    turned_at(t, k0, k1)(pT_lo),
                    ps_t[:, (T_FIRST[step] + j) % 2, 0:(k1 - k0) * P].rearrange("p (k q) -> p k q", q=P),
                    turned_at(t, k0, k1)(pT_hi).bitcast(F32), ALU.subtract).then_inc(pT_ready, 1)

            def wo_add(ps, piece):
                _, u, chunk, j = piece
                if j == 0:
                    nc.vector.reciprocal(inv_sum[:, u % 2, 4 * chunk:4 * chunk + 4],
                                         row_sum[:, u % 2, 4 * chunk:4 * chunk + 4]).then_inc(inv_ready, 1)
                    dve.wait_ge(inv_ready, ps.count(RANK[piece] // 2 + 1, PER_PASS["wo"] // 2))
                dve.wait_ge(piece_made, ps.pieces(piece))
                for s in range(2):
                    t = 4 * chunk + 2 * j + s
                    tt = unit_batch(u) * NQ + t
                    ins = nc.vector.scalar_tensor_tensor(
                        y[:, tt, :], ps_r[:, ps.bank(piece), s * DIM:s * DIM + DIM], inv_sum[:, u % 2, t:t + 1],
                        y[:, tt, :], ALU.mult, ALU.add)
                ins.then_inc(y_added, 1)

            def row_max(ps, u, step):
                t = ORDER[step]
                dve.wait_ge(scores_ready, ps.tiles(u, step + 1))
                nc.vector.tensor_reduce(neg_max[:, t:t + 1], ps_s[:, step % 2, 0:(t + 1) * P], AX, ALU.max,
                                        negate=True).then_inc(max_ready, 1)

            def run(ps):
                for what, x, piece in ps.work(VECTOR_PLAN):
                    if what == "max":
                        row_max(ps, x, *piece)
                    elif what == "turn":
                        turn_low(ps, x, *piece)
                    else:
                        {"qk": qk_add, "v": v_low, "pv": o_low, "wo": wo_add}[piece[0]](ps, piece)

            dve.wait_ge(y_added, 1)
            run(Span(0, 1))
            with dve.Fori(0, LAST) as i:
                run(Span(1, 1 + UNITS, i))
            run(Span(1 + LAST * UNITS, ALL_UNITS + 1))

            dve.wait_ge(down_ready, 32)
            for j in range(2):
                dve.wait_ge(g_made, j + 1)
                src = ps_r[:, j, :].rearrange("p (b n) -> p b n", b=BATCH)
                link(nc.vector.tensor_scalar(g_sign[:, :, :], src, 0.0, 2.0, ALU.is_ge, ALU.mult))
                link(nc.vector.tensor_scalar(g_row[:, j, :, :], src, -1.0, 0.25, ALU.mult, ALU.max))
                link(nc.vector.tensor_tensor(g_row[:, j, :, :], src, g_row[:, j, :, :], ALU.max))
                link(nc.vector.scalar_tensor_tensor(g_row[:, j, :, :], g_sign[:, :, :], -1.0, g_row[:, j, :, :],
                                                    ALU.add, ALU.mult))
            link(nc.vector.tensor_tensor(g_row[:, 1, :, :], g_row[:, 1, :, :],
                                         sd_wide[:, None, :].broadcast_to([P, BATCH, DIM]), ALU.mult))
            nc.vector.engine_nop().then_inc(g_ready, 1)
            dve.wait_ge(x2_in_ready, 16 * NCH)
            for n in range(NCH):
                part = (slice(None), slice(4 * n, 4 * n + 4), slice(None))
                link(nc.vector.tensor_tensor(y[part], y[part], attn_bias[:, None, :].broadcast_to([P, 4, DIM]), ALU.add))
                link(nc.vector.tensor_tensor(y[part], y[part],
                                             g_row[:, 0, n // 2, None, :].broadcast_to([P, 4, DIM]), ALU.mult))
                link(nc.vector.tensor_tensor(x2[part], x2[part], y[part], ALU.add))
            for n in range(3 * HM):
                which, m = divmod(n, HM)
                size = P if m < HM - 1 else HLAST
                dve.wait_ge(wf_hi_ready, n + 1)
                if which < 2:
                    part = (slice(None), which, slice(None), slice(m * P, m * P + size))
                    nc.vector.tensor_tensor(wg_lo[part], ps_t[:, n % 2, 0:KT * size].rearrange("p (k h) -> p k h", k=KT),
                                            wg_hi[part].bitcast(F32), ALU.subtract).then_inc(wf_lo_ready, 1)
                else:
                    nc.vector.tensor_tensor(wd_lo[0:size, m, :], ps_t[0:size, n % 2, 0:DIM],
                                            wd_hi[0:size, m, :].bitcast(F32), ALU.subtract).then_inc(wf_lo_ready, 1)

            norm(x2, xn2, lambda n: None, var2_ready, root2_ready, xn2_ready)

            def finish(n):
                dve.wait_ge(down_made, n + 1)
                part = (slice(None), slice(2 * n, 2 * n + 2), slice(None))
                link(nc.vector.tensor_tensor(y[part], ps_r[:, n % 2, :].rearrange("p (t n) -> p t n", t=2),
                                             g_row[:, 1, n // 4, None, :].broadcast_to([P, 2, DIM]), ALU.mult))
                nc.vector.tensor_tensor(y[part], y[part], x2[part], ALU.add).then_inc(out_ready, 1)

            for n in range(NCH * HM):
                m = n % HM
                size = P if m < HM - 1 else HLAST
                dve.wait_ge(lin_ready, n + 1)
                link(nc.vector.scalar_tensor_tensor(lin_g[0:size, n % 2, :], tanh_g[0:size, n % 2, :], 1.0,
                                                    lin_g[0:size, n % 2, :], ALU.add, ALU.mult))
                dve.wait_ge(up_made, n + 1)
                if n >= 2:
                    dve.wait_ge(gu_split, n - 1)
                nc.vector.scalar_tensor_tensor(gu[0:size, n % 2, :], ps_s[0:size, n % 2, CH:2 * CH],
                                               half_su[0:size, m:m + 1], lin_g[0:size, n % 2, :], ALU.mult, ALU.mult)\
                    .then_inc(gu_ready, 1)
                if n >= HM and m == 3:
                    for j in range(2):
                        finish(n // HM * 2 - 2 + j)
            for j in range(2):
                finish(NCH * 2 - 2 + j)

        @block.tensor
        def _(pe):
            def three(out, stationary, moving, first, last):
                (shi, slo), (mhi, mlo) = stationary, moving
                nc.tensor.matmul(out, shi, mhi, start=first, stop=False)
                nc.tensor.matmul(out, shi, mlo, start=False, stop=False)
                return nc.tensor.matmul(out, slo, mhi, start=False, stop=last)

            def wait_bank(ps, piece):
                old = ps.before(piece)
                if old is None:
                    return
                if old[0] == "qk":
                    pe.wait_ge(straight_ready, ps.rank(old, 1))
                elif old[0] == "v":
                    pe.wait_ge(v_ready, ps.rank(old, 1))
                elif old[0] == "pv":
                    pe.wait_ge(o_ready, ps.rank(old, 1))
                else:
                    pe.wait_ge(y_added, ps.rank(old, 2))

            def w_at(j, k, first, size):
                return w_hi[:, j, k, first:first + size], w_lo[:, j, k, first:first + size]

            def h_at(k, first, size):
                return hT_hi[:, k, first:first + size], hT_lo[:, k, first:first + size]

            def make(ps, piece):
                wait_bank(ps, piece)
                dst = ps_r[:, ps.bank(piece), :]
                if piece[0] == "qk":
                    _, u, which, chunk = piece
                    if u % UNITS == 0 and chunk == 0:
                        pe.wait_ge(w_ready[which], ps.passes(u // UNITS + 1))
                    for k in range(KT):
                        ins = three(dst, w_at(which, k, u % 2 * DH, DH),
                                    h_at(k, unit_batch(u) * SEQ + chunk * CH, CH), k == 0, k == KT - 1)
                elif piece[0] == "v":
                    _, pb, j = piece
                    if pb % BATCH == 0 and j == 0:
                        pe.wait_ge(w_ready[WV], ps.passes(pb // BATCH + 1))
                    for s in range(2):
                        for k in range(KT):
                            ins = three(dst[:, s * 2 * DH:s * 2 * DH + 2 * DH],
                                        h_at(k, pb % BATCH * SEQ + (2 * j + s) * P, P), w_at(WV, k, 0, 2 * DH),
                                        k == 0, k == KT - 1)
                elif piece[0] == "pv":
                    _, u, chunk = piece
                    b, d0 = unit_batch(u), u % 2 * DH
                    if u % 2 == 0 and chunk == 0:
                        pe.wait_ge(v_ready, ps.rank(("v", u // 2, 3), 1))
                    step = max(s for s in range(NQ) if ORDER[s] // 4 == chunk)
                    pe.wait_ge(pT_ready, ps.groups(u, step, T_GROUPS[step]))
                    n_keys = 4 * chunk + 4
                    for k in range(n_keys):
                        q0 = max(0, k - 4 * chunk) * P
                        slot, col = (k, 0) if chunk == 0 else (8 - k, q0)
                        ins = three(dst[:, q0:CH], (v_hi[:, b, k, d0:d0 + DH], v_lo[:, b, k, d0:d0 + DH]),
                                    (pT_hi[:, slot, col:col + CH - q0], pT_lo[:, slot, col:col + CH - q0]),
                                    k == 0, k == n_keys - 1)
                else:
                    _, u, chunk, j = piece
                    if j == 0:
                        pe.wait_ge(o_ready, ps.rank(("pv", u, chunk), 1))
                    if u % UNITS == 0 and j == 0 and chunk == 0:
                        pe.wait_ge(w_ready[WO], ps.passes(u // UNITS + 1))
                    for s in range(2):
                        q0 = (2 * j + s) * P
                        ins = three(dst[:, s * DIM:s * DIM + DIM],
                                    (o_hi[:, chunk, q0:q0 + P], o_lo[:, chunk, q0:q0 + P]),
                                    (wo_hi[:, u % 2, :], wo_lo[:, u % 2, :]), True, True)
                ins.then_inc(piece_made, 1)

            def scores(ps, u, step):
                t = ORDER[step]
                if u * NQ + step >= 2:
                    pe.wait_ge(exp_ready, ps.tiles(u, step - 1))
                if step < 2:
                    pe.wait_ge(qk_ready, ps.count(4 * u + (2 if t < 4 else 4), PER_PASS["qk"]))
                q = qk_at(u % 2, 0, t * P, P)
                for k0 in range(0, (t + 1) * P, CH):
                    size = min(CH, (t + 1) * P - k0)
                    diagonal = k0 + size == (t + 1) * P
                    three(ps_s[:, step % 2, k0:k0 + size], q, qk_at(u % 2, 1, k0, size), True, not diagonal)
                ins = nc.tensor.matmul(ps_s[:, step % 2, t * P:t * P + P], ident_b[:, :], mask_b[:, :],
                                       start=False, stop=True)
                ins.then_inc(scores_ready, 1)

            def turn(ps, u, step, j):
                t = ORDER[step]
                k0, k1 = groups_of(t)[j]
                if j == 0:
                    pe.wait_ge(exp_ready, ps.tiles(u, step + 1))
                bank = (T_FIRST[step] + j) % 2
                if u * T_UNIT + T_FIRST[step] + j >= 2:
                    pe.wait_ge(pT_ready, ps.groups(u, step, j - 1))
                for k in range(k0, k1):
                    at_ = (k if t < 4 else k0 + k1 - 1 - k) - k0
                    ins = nc.tensor.transpose(ps_t[:, bank, at_ * P:at_ * P + P],
                                              probs[:, (P_AT[step] + k) * P:(P_AT[step] + k) * P + P], ident[:, :])
                ins.then_inc(turned, 1)

            pe.wait_ge(consts_ready, 2)
            pe.wait_ge(rows_ready, 16 * 8)
            nc.tensor.transpose(ps_r[:, 0, 0:NROWS], rows[:, :], ident[0:NROWS, 0:NROWS]).then_inc(cols_turned, 1)
            pe.wait_ge(silu_ready, 1)
            pe.wait_ge(wmod_ready, 64)
            for j in range(4):
                for k in range(KT):
                    for kk in range(KT):
                        at_ = (KT * j + k) * BATCH
                        ins = nc.tensor.matmul(ps_r[:, 1, at_:at_ + BATCH], wmod_a[:, kk, j, k * P:k * P + P],
                                               silu_c[:, kk:BATCH * KT:KT], start=kk == 0, stop=kk == KT - 1)
            ins.then_inc(mod_made, 1)

            def turn_tokens(src, ready, n, done):
                k, chunk = n % KT, n // KT
                pe.wait_ge(ready, chunk + 1)
                for t in range(4):
                    ins = nc.tensor.transpose(ps_t[:, n % 2, t * P:t * P + P],
                                              src[:, 4 * chunk + t, k * P:k * P + P], ident[:, :])
                ins.then_inc(done, 1)

            for n in range(GROUPS4):
                if n >= 2:
                    pe.wait_ge(hhi_ready, n - 1)
                turn_tokens(xn, xn_ready, n, xn_turned)
            pe.wait_ge(bv_wide_ready, 1)
            pe.wait_ge(wo_all_ready, 32)
            for h in range(HEADS):
                ins = nc.tensor.matmul(ps_s[:, 0, 0:DIM], bv_wide[:, h, :], wo_all[:, h, :], start=h == 0,
                                       stop=h == HEADS - 1)
            ins.then_inc(attn_bias_made, 1)
            pe.wait_ge(cols_ready, 1)
            pe.wait_ge(mod_ready, 1)
            pe.wait_ge(hT_ready, GROUPS4)
            for piece in FIRST_QK + FIRST_V:
                make(Span(0, 0), piece)
            pe.wait_ge(attn_bias_ready, 1)

            def run(ps):
                for what, x, piece in ps.work(TENSOR_PLAN):
                    if what == "scores":
                        scores(ps, x, *piece)
                    elif what == "turn":
                        turn(ps, x, *piece)
                    else:
                        make(ps, piece)

            run(Span(0, 1))
            pe.wait_ge(v_ready, sum(piece[0] == "v" for piece in BEFORE_LOOP))
            pe.wait_ge(straight_ready, sum(piece[0] == "qk" for piece in BEFORE_LOOP))
            with pe.Fori(0, LAST) as i:
                run(Span(1, 1 + UNITS, i))
            run(Span(1 + LAST * UNITS, ALL_UNITS + 1))

            pe.wait_ge(y_added, PAIRS * 16 + 1)
            pe.wait_ge(silu_w_ready, 1)
            pe.wait_ge(wmod_g_ready, 32)
            for j in range(2):
                for b in range(BATCH):
                    for k in range(KT):
                        ins = nc.tensor.matmul(ps_r[:, j, b * DIM:b * DIM + DIM], silu_w[:, b * KT + k, :],
                                               wmod_g[:, k, j, :], start=k == 0, stop=k == KT - 1)
                ins.then_inc(g_made, 1)
            pe.wait_ge(pT_ready, PAIRS * UNITS * T_UNIT)
            for n in range(3 * HM):
                which, m = divmod(n, HM)
                size = P if m < HM - 1 else HLAST
                pe.wait_ge(wf_ready, which + 1)
                if n >= 2:
                    pe.wait_ge(wf_lo_ready, n - 1)
                for k in range(KT):
                    if which < 2:
                        src = (f_gate, f_up)[which][0:size, m, k * P:k * P + P]
                        ins = nc.tensor.transpose(ps_t[:, n % 2, k * size:k * size + size], src, ident[0:size, 0:size])
                    else:
                        ins = nc.tensor.transpose(ps_t[0:size, n % 2, k * P:k * P + P],
                                                  f_down[:, k, m * P:m * P + size], ident[:, :])
                ins.then_inc(wf_turned, 1)
            for n in range(GROUPS4):
                if n < 2:
                    pe.wait_ge(wf_lo_ready, 3 * HM - 1 + n)
                else:
                    pe.wait_ge(h2_hi_ready, n - 1)
                turn_tokens(xn2, xn2_ready, n, xn2_turned)
            pe.wait_ge(wf_lo_ready, 3 * HM)

            def down(n):
                pe.wait_ge(gu_split, n * HM + HM)
                for j in range(2):
                    if n == 0 and j == 0:
                        pe.wait_ge(g_ready, 1)
                    if n > 0:
                        pe.wait_ge(out_ready, 2 * n - 1 + j)
                    for s in range(2):
                        t = 2 * j + s
                        for m in range(HM):
                            size = P if m < HM - 1 else HLAST
                            ins = three(ps_r[:, j, s * DIM:s * DIM + DIM],
                                        (gu_hi[0:size, m, t * P:t * P + P], gu_lo[0:size, m, t * P:t * P + P]),
                                        (wd_hi[0:size, m, :], wd_lo[0:size, m, :]), m == 0, m == HM - 1)
                    ins.then_inc(down_made, 1)

            for n in range(NCH * HM):
                chunk, m = divmod(n, HM)
                size = P if m < HM - 1 else HLAST
                if m == 0:
                    pe.wait_ge(h2_ready, chunk * KT + KT)
                if n >= 2:
                    pe.wait_ge(gu_ready, n - 1)
                for which, done in enumerate((gate_made, up_made)):
                    for k in range(KT):
                        ins = three(ps_s[0:size, n % 2, which * CH:which * CH + CH],
                                    (wg_hi[:, which, k, m * P:m * P + size], wg_lo[:, which, k, m * P:m * P + size]),
                                    h_at(k, chunk * CH, CH), k == 0, k == KT - 1)
                    ins.then_inc(done, 1)
                if chunk > 0 and m == 1:
                    down(chunk - 1)
            down(NCH - 1)


def rotary_tables():
    inv_freq = np.float32(1.0) / (10000.0 ** (np.arange(0, DH, 2) / DH)).astype(np.float32)
    freqs = np.arange(SEQ, dtype=np.float32)[None, :] * inv_freq[:, None]
    cos = np.cos(freqs.astype(np.float64)).astype(np.float32)
    sin = np.sin(freqs.astype(np.float64)).astype(np.float32)
    return np.concatenate([cos, cos]), np.concatenate([-sin, sin])


INPUTS = ["L0_attn_x", "L0_attn_Wq", "L0_attn_bq", "L0_attn_Wk", "L0_attn_bk", "L0_attn_Wv", "L0_attn_bv",
          "L0_attn_Wo", "L0_attn_bo", "L0_ffn_wq_gate", "L0_ffn_s_gate", "L0_ffn_wq_up", "L0_ffn_s_up",
          "L0_ffn_wq_down", "L0_ffn_s_down", "L0_c", "L0_wmod"]


def kernel(**inputs):
    import concourse.bacc as bacc
    from concourse.bass_utils import run_bass_kernel_spmd

    nc = bacc.Bacc("TRN2", target_bir_lowering=False, num_devices=1)
    arrays, args = {}, []
    cos, sin = rotary_tables()
    for name, a in [(n, inputs[n]) for n in INPUTS] + [("rotary_cos", cos), ("rotary_sin", sin)]:
        a = np.ascontiguousarray(a)
        arrays[f"in_{name}"] = a
        args.append(nc.dram_tensor(f"in_{name}", a.shape, mybir.dt.from_np(a.dtype), kind="ExternalInput").ap())
    out = nc.dram_tensor("out_0", (BATCH, SEQ, DIM), F32, kind="ExternalOutput").ap()
    build(nc, *args, out)
    got = run_bass_kernel_spmd(nc, [arrays], core_ids=[0])
    return got.results[0]["out_0"]
```

```python
from contextlib import ExitStack

import numpy as np

import concourse.bass as bass
from concourse import mybir

F32 = mybir.dt.float32
F32R = mybir.dt.float32r
BF16 = mybir.dt.bfloat16
I32 = mybir.dt.int32
ALU = mybir.AluOpType
ACT = mybir.ActivationFunctionType
AX = mybir.AxisListType.X

P = 128
BATCH, SEQ, DIM = 2, 1024, 256
HEADS, DH = 16, 128
INNER = HEADS * DH
HID = 704
TOK = BATCH * SEQ
KT = DIM // P
NQ = SEQ // P
NTT = TOK // P
CH = 512
NCH = TOK // CH
HM = (HID + P - 1) // P
HLAST = HID - (HM - 1) * P
PAIRS = HEADS // 2
UNITS = 2 * BATCH
TILES = UNITS * NQ
EPS = 1e-5
SCALE = DH ** -0.5
WHOLE = 256.0
ZERO_POINT = 128.0
MASKED = -3.0e38

COL_BQ, COL_BK, COL_BV = 0, HEADS, 2 * HEADS
COL_C = 3 * HEADS
COL_SG = COL_C + BATCH * KT
COL_SU = COL_SG + HM
COL_SD = COL_SU + HM
NCOLS = COL_SD + KT
SROWS = NCOLS - COL_SG
MOD_SA, MOD_CA, MOD_SB, MOD_CB, MOD_GA, MOD_GB = (KT * j for j in range(6))

W_TILES = [(which, m) for m in range(HM) for which in range(2)] + [(2, m) for m in range(HM)]
W_EARLY = 4
BESIDE = {n: [("w", W_EARLY + 2 * n), ("w", W_EARLY + 2 * n + 1)] for n in range((len(W_TILES) - W_EARLY) // 2)}
BESIDE |= {7: [("h", 4), ("h", 5)], 8: [("h", 6), ("h", 7)]}
NORM_AT = 2
GU = 8
OUT_TILES = [(2 * n, 2) for n in range(NTT // 2 - 2)] + [(n, 1) for n in range(NTT - 4, NTT)]
LATE_TURNS = [("w", n) for n in range(W_EARLY)] + [("h", n) for n in range(4)] \
    + [x for n in sorted(BESIDE) for x in BESIDE[n]]

ORDER = [0, 7, 1, 6, 2, 5, 3, 4]
P_AT = [0, 1, 9, 11, 0, 3, 9, 13]
P_BLOCKS = 18

T_GROUPS = [(t + 4) // 4 for t in ORDER]
T_FIRST = [sum(T_GROUPS[:s]) for s in range(NQ)]
T_UNIT = sum(T_GROUPS)

ALL_UNITS = PAIRS * UNITS
WQ, WK, WV, WO = range(4)


TENSOR_PLAN = """make:K0+ make:Q0+ scores:0 turn:6.0- turn:7.0- scores:1 scores:2 turn:7.1- make:P0- turn:0.0
        make:P1- scores:3 turn:1.0 make:W00- make:K1+ scores:4 turn:1.1 make:W01- turn:2.0 make:Q1+
        make:W10- scores:5 turn:3.0 make:W11- turn:3.1 make:V0 turn:4.0 scores:6 make:V1 turn:5.0 scores:7
        turn:5.1"""
SCALAR_PLAN = """out:K0+ exp:7- turn:6.0- exp:0 split:V out:Q0+ turn:7.0- turn:7.1- high:P0- turn:0.0 exp:1 exp:2
        high:P1- high:K0+ high:Q0+ turn:1.0 out:K1+ turn:1.1 split:K exp:3 turn:2.0 exp:4 out:Q1+ turn:3.0
        split:Q exp:5 turn:3.1 turn:4.0 high:V0 high:K1+ high:V1 turn:5.0 exp:6 split:O turn:5.1 high:Q1+"""
VECTOR_PLAN = """max:0 turn:6.0- turn:7.0- turn:7.1- max:1 low:P0- add:K0+ max:2 turn:0.0 add:Q0+ low:P1- max:3
        sum:W00- turn:1.0 max:4 sum:W01- turn:1.1 turn:2.0 sum:W10- max:5 turn:3.0 sum:W11- add:K1+ turn:3.1
        turn:4.0 max:6 low:V0 add:Q1+ low:V1 max:7 turn:5.0 turn:5.1"""
POOL_PLAN = """rotate:K0+ split:V rotate:Q0+ low:K0+ low:Q0+ rotate:K1+ split:K split:Q rotate:Q1+ low:K1+ low:Q1+
        split:O"""


def unit_plan(plan, u):
    out = []
    for token in plan.split():
        what, name = token.rstrip("+-").split(":")
        v = u + {"+": 1, "-": -1}.get(token[-1], 0)
        if what == "split":
            which = "QKVO".index(name)
            n = v // UNITS + (which != WO)
            if v % UNITS == (0 if which == WO else 2) and n < PAIRS and v < ALL_UNITS:
                out.append((what, which, n))
        elif name[0] in "KQ":
            if 1 <= v < ALL_UNITS:
                out.append((what, v, ("qk", v, int(name[0] == "K"), int(name[1]))))
            elif v == ALL_UNITS and what in ("make", "out") and name[1] == "0":
                out.append((what, v, ("gate", "KQ".index(name[0]))))
        elif name[0] == "V":
            piece = ("v", 2 * (v // UNITS) + 1 + v % UNITS // 2, v % 2 * 2 + int(name[1]))
            if v >= 0 and piece[1] < 2 * PAIRS:
                out.append((what, v, piece))
        elif v == -1 and name[0] == "P":
            out.append((what, v, ("v", 0, 2 + int(name[1]))))
        elif 0 <= v < ALL_UNITS:
            if name[0] == "P":
                out.append((what, v, ("pv", v, int(name[1]))))
            elif name[0] == "W":
                out.append((what, v, ("wo", v, int(name[1]), int(name[2]))))
            else:
                out.append((what, v, tuple(int(x) for x in name.split("."))))
    return out


FIRST_QK = [("qk", 0, 1, 0), ("qk", 0, 0, 0), ("qk", 0, 1, 1), ("qk", 0, 0, 1)]
FIRST_V = [("v", 0, 0), ("v", 0, 1)]
BEFORE_LOOP = FIRST_QK + FIRST_V + [piece for what, _, piece in unit_plan(TENSOR_PLAN, 0) if what == "make"]
PIECES = FIRST_QK + FIRST_V + [piece for u in range(ALL_UNITS + 1) for what, _, piece in unit_plan(TENSOR_PLAN, u)
                               if what == "make"]
PIECE_AT = {piece: n for n, piece in enumerate(PIECES)}
RANK = {piece: sum(other[0] == piece[0] for other in PIECES[:n]) for piece, n in PIECE_AT.items()}
PER_PASS = {"qk": 4 * UNITS, "v": 2 * UNITS, "pv": 2 * UNITS, "wo": 4 * UNITS, "gate": 0}
PIECES_PER_PASS = sum(PER_PASS.values())


class Span:

    def __init__(self, first, last, i=None):
        self.i = i
        self.units = range(first, last) if i is None else range(first + UNITS, last + UNITS)

    def work(self, plan):
        return [x for u in self.units for x in unit_plan(plan, u)]

    def count(self, n, per_round):
        return n if self.i is None else self.i * per_round + (n - per_round)

    def pieces(self, piece):
        return self.count(PIECE_AT[piece] + 1, PIECES_PER_PASS)

    def rank(self, piece, more=0):
        return self.count(RANK[piece] + more, PER_PASS[piece[0]])

    def bank(self, piece):
        return PIECE_AT[piece] % 2

    def before(self, piece):
        n = PIECE_AT[piece]
        return PIECES[n - 2] if n >= 2 else None

    def tiles(self, u, step):
        return self.count(u * NQ + step, TILES)

    def passes(self, n):
        return self.count(n, 1)

    def groups(self, u, step, more=0):
        return self.count(u * T_UNIT + T_FIRST[step] + more, UNITS * T_UNIT)


def unit_batch(u):
    return u // 2 % BATCH


def build(nc, x, wq, bq, wk, bk, wv, bv, wo, bo, wq_gate, s_gate, wq_up, s_up, wq_down, s_down, c, wmod,
          cos, sin, out):
    with ExitStack() as ctx:
        def sem(name):
            return ctx.enter_context(nc.semaphore(name))

        base = (nc.sbuf_base + 31) // 32 * 32
        KB = 1024
        A_HTH, A_HTL, A_Y = 0, 16 * KB, 32 * KB
        A_QK, A_V, A_PT = 48 * KB, 80 * KB, 112 * KB
        A_W, A_ROPE, A_RAW, A_P, A_SMALL = 148 * KB, 172 * KB, 188 * KB, 194 * KB, 194 * KB + 512 * P_BLOCKS
        A_WO, A_O = A_W + 12 * KB, A_W + 16 * KB
        small_at = [A_SMALL]

        def at(name, offset, shape, dt):
            return nc.alloc_sbuf_tensor_at(name, shape, dt, offset=base + offset)

        def small(name, shape, dt):
            size = int(np.prod(shape[1:])) * (2 if dt == BF16 else 4)
            t = at(name, small_at[0], shape, dt)
            small_at[0] += (size + 31) // 32 * 32
            return t

        hT_hi = at("hT_hi", A_HTH, [P, KT, TOK], F32R)
        hT_lo = at("hT_lo", A_HTL, [P, KT, TOK], F32R)
        y = at("y", A_Y, [P, NTT, DIM], F32)
        qk_hi = at("qk_hi", A_QK, [P, 2, 2, SEQ], F32R)
        qk_lo = at("qk_lo", A_QK + 16 * KB, [P, 2, 2, SEQ], F32R)
        v_hi = at("v_hi", A_V, [P, BATCH, NQ, 2 * DH], F32R)
        v_lo = at("v_lo", A_V + 16 * KB, [P, BATCH, NQ, 2 * DH], F32R)
        pT_hi = at("pT_hi", A_PT, [P, NQ + 1, CH], F32R)
        pT_lo = at("pT_lo", A_PT + 18 * KB, [P, NQ + 1, CH], F32R)
        w_hi = at("w_hi", A_W, [P, 3, KT, 2 * DH], F32R)
        w_lo = at("w_lo", A_W + 6 * KB, [P, 3, KT, 2 * DH], F32R)
        wo_hi = at("wo_hi", A_WO, [P, 2, DIM], F32R)
        wo_lo = at("wo_lo", A_WO + 2 * KB, [P, 2, DIM], F32R)
        o_hi = at("o_hi", A_O, [P, 2, CH], F32R)
        o_lo = at("o_lo", A_O + 4 * KB, [P, 2, CH], F32R)
        cos_sb = at("cos_sb", A_ROPE, [P, SEQ], F32)
        sin_sb = at("sin_sb", A_ROPE + 4 * KB, [P, SEQ], F32)
        straight = at("straight", A_ROPE + 8 * KB, [P, 2, CH], F32)
        swapped = at("swapped", A_ROPE + 12 * KB, [P, 2, CH], F32)
        w_raw = at("w_raw", A_RAW, [P, 3, KT, 2 * DH], F32)
        wo_raw = at("wo_raw", A_RAW + 4 * KB, [P, 2, DIM], F32)
        probs = at("probs", A_P, [P, P_BLOCKS * P], F32)
        ident = small("ident", [P, P], F32)
        ident_b = small("ident_b", [P, P], BF16)
        mask_b = small("mask_b", [P, P], BF16)
        attn_bias = small("attn_bias", [P, DIM], F32)
        cols = small("cols", [P, NCOLS], F32)
        bq_s = small("bq_s", [P, HEADS], F32)
        tanh_c = small("tanh_c", [P, BATCH * KT], F32)
        silu_c = small("silu_c", [P, BATCH * KT], F32)
        mod = small("mod", [P, 6 * KT, BATCH], F32)
        sign = small("sign", [P, 2 * KT, BATCH], F32)
        magnitude = small("magnitude", [P, 2 * KT, BATCH], F32)
        bn = small("bn", [P, NTT, 6], F32)
        mv = small("mv", [P, NTT, 2], F32)
        var = small("var", [P, NTT], F32)
        root = small("root", [P, NTT], F32)
        rstd = small("rstd", [P, NTT], F32)
        newton = small("newton", [P, NTT], F32)
        neg_max = small("neg_max", [P, NQ], F32)
        row_sum = small("row_sum", [P, 2, NQ], F32)
        inv_sum = small("inv_sum", [P, 2, NQ], F32)
        assert base + small_at[0] <= nc.sbuf_usable_end, (base + small_at[0], nc.sbuf_usable_end)

        x_in = at("x_in", A_QK, [P, NTT, DIM], F32)
        wmod_a = at("wmod_a", A_QK + 24 * KB, [P, KT, 4, DIM], F32)
        xn = at("xn", A_PT, [P, NTT, DIM], F32)
        h32 = at("h32", A_PT + 28 * KB, [P, 4, CH], F32)
        wmod_g = at("wmod_g", A_V + 8 * KB, [P, KT, 2, DIM], F32)
        wo_all = at("wo_all", A_Y, [P, HEADS, DIM], F32)
        straight_b = at("straight_b", A_V + 24 * KB, [P, 2, CH], F32)
        swapped_b = at("swapped_b", A_V + 28 * KB, [P, 2, CH], F32)
        b_rows = at("b_rows", A_P, [3 * HEADS, P], F32)
        c_rows = at("c_rows", A_P + 512, [BATCH * KT, P], F32)
        s_rows = at("s_rows", A_P + 1024, [SROWS, P], F32)
        bo_wide = at("bo_wide", A_P + 1536, [P, DIM], F32)
        x2 = at("x2", A_QK, [P, NTT, DIM], F32)
        int_gate = at("int_gate", A_W, [P, HM, DIM], I32)
        int_up = at("int_up", A_W + 6 * KB, [P, HM, DIM], I32)
        int_down = at("int_down", A_RAW, [P, KT, HID], I32)
        f_gate = at("f_gate", A_W, [P, HM, DIM], F32)
        f_up = at("f_up", A_W + 6 * KB, [P, HM, DIM], F32)
        f_down = at("f_down", A_RAW, [P, KT, HID], F32)
        wg_hi = [at("gate_hi", A_V, [P, KT, HID], F32R), at("up_hi", A_QK + 16 * KB, [P, KT, HID], F32R)]
        wg_lo = [at("gate_lo", A_V + 16 * KB, [P, KT, HID], F32R), at("up_lo", A_ROPE, [P, KT, HID], F32R)]
        wd_hi = at("wd_hi", A_ROPE + 6 * KB, [P, HM, DIM], F32R)
        wd_lo = at("wd_lo", A_W, [P, HM, DIM], F32R)
        h2_32 = at("h2_32", A_V + 8 * KB, [P, 4, CH], F32)
        g_row = [at("ga_row", A_V + 6 * KB, [P, BATCH, DIM], F32), at("gb_row", A_V + 22 * KB, [P, BATCH, DIM], F32)]
        xn2 = [at("xn2_0", A_QK + 24 * KB, [P, NQ, DIM], F32), at("xn2_1", A_V + 24 * KB, [P, NQ, DIM], F32)]
        gu = at("gu", A_QK + 24 * KB, [P, 2, CH], F32)
        gu_hi = at("gu_hi", A_PT, [P, GU, CH], F32R)
        gu_lo = at("gu_lo", A_PT + 2 * KB * GU, [P, GU, CH], F32R)
        w_full = at("w_full", A_PT + 4 * KB * GU, [P, 4, KT * P], F32)
        tanh_g = at("tanh_g", A_P, [P, 2, CH], F32)
        silu_g = at("silu_g", A_P + 4 * KB, [P, 2, CH], F32)
        half_sgu = small("half_sgu", [P, HM], F32)
        half_sg = small("half_sg", [P, HM], F32)
        largest = small("largest", [P, 5], F32)
        largest_of = small("largest_of", [P, 1], F32)
        largest_all = small("largest_all", [1, 1], F32)
        wide = small("wide", [1, 1], I32)
        assert base + small_at[0] <= nc.sbuf_usable_end, (base + small_at[0], nc.sbuf_usable_end)

        ps_s = ctx.enter_context(nc.psum_tensor("ps_s", [P, 2, SEQ], F32))
        ps_t = ctx.enter_context(nc.psum_tensor("ps_t", [P, 2, CH], F32))
        ps_r = ctx.enter_context(nc.psum_tensor("ps_r", [P, 2, CH], F32))

        zeroed = sem("zeroed")
        bq_ready = sem("bq_ready")
        consts_ready = sem("consts_ready")
        c_ready = sem("c_ready")
        b_rows_ready = sem("b_rows_ready")
        s_rows_ready = sem("s_rows_ready")
        x_ready = [sem(f"x_ready{n}") for n in range(NCH)]
        wmod_a_ready = sem("wmod_a_ready")
        wmod_b_ready = sem("wmod_b_ready")
        tables_ready = sem("tables_ready")
        raw_ready = [sem(f"raw_{x}_ready") for x in ("wq", "wk", "wv", "wo")]
        wo_all_ready = sem("wo_all_ready")
        cols_turned = sem("cols_turned")
        cols_ready = sem("cols_ready")
        tanh_ready = sem("tanh_ready")
        silu_ready = sem("silu_ready")
        mod_made = sem("mod_made")
        mod_ready = sem("mod_ready")
        var_ready = sem("var_ready")
        root_ready = sem("root_ready")
        xn_ready = sem("xn_ready")
        xn_turned = sem("xn_turned")
        hhi_ready = sem("hhi_ready")
        hT_ready = sem("hT_ready")
        attn_bias_made = sem("attn_bias_made")
        attn_bias_ready = sem("attn_bias_ready")
        pool_chain = sem("pool_chain")
        dve_chain = sem("dve_chain")
        gain_ready = sem("gain_ready")

        w_hi_ready = [sem(f"{x}_hi_ready") for x in ("wq", "wk", "wv", "wo")]
        w_ready = [sem(f"{x}_ready") for x in ("wq", "wk", "wv", "wo")]
        scores_ready = sem("scores_ready")
        max_ready = sem("max_ready")
        exp_ready = sem("exp_ready")
        turned = sem("turned")
        pT_hi_ready = sem("pT_hi_ready")
        pT_ready = sem("pT_ready")
        piece_made = sem("piece_made")
        y_added = sem("y_added")
        straight_ready = sem("straight_ready")
        swapped_ready = [sem(f"swapped_ready{n}") for n in range(2)]
        first_swapped = [sem(f"first_swapped{n}") for n in range(4)]
        rotated = sem("rotated")
        qk_sum = sem("qk_sum")
        qk_hi_ready = sem("qk_hi_ready")
        qk_ready = sem("qk_ready")
        v_hi_ready = sem("v_hi_ready")
        v_ready = sem("v_ready")
        o_hi_ready = sem("o_hi_ready")
        o_ready = sem("o_ready")
        inv_ready = sem("inv_ready")

        gates_ready = sem("gates_ready")
        g_ready = sem("g_ready")
        ints_ready = [sem(f"int_{x}_ready") for x in ("gate", "up", "down")]
        x2_in_ready = [sem(f"x2_in_ready{n}") for n in range(NCH)]
        x2_ready = sem("x2_ready")
        xn2_ready = sem("xn2_ready")
        xn2_turned = sem("xn2_turned")
        h2_hi_ready = sem("h2_hi_ready")
        h2_ready = sem("h2_ready")
        wf_ready = [sem(f"f_{x}_ready") for x in ("gate", "up", "down")]
        wf_turned = sem("wf_turned")
        wf_hi_ready = sem("wf_hi_ready")
        wf_lo_ready = sem("wf_lo_ready")
        wf_late_ready = sem("wf_late_ready")
        gate_made = sem("gate_made")
        up_made = sem("up_made")
        tanh_g_ready = sem("tanh_g_ready")
        gu_ready = sem("gu_ready")
        gu_hi_ready = sem("gu_hi_ready")
        gu_split = sem("gu_split")
        down_made = sem("down_made")
        largest_ready = sem("largest_ready")
        largest_turned = sem("largest_turned")
        wide_ready = sem("wide_ready")
        out_ready = sem("out_ready")
        stored = sem("stored")

        block = ctx.enter_context(nc.Block())

        x_t = x.rearrange("b (t p) d -> p (b t) d", p=P)
        out_t = out.rearrange("b (t p) d -> p (b t) d", p=P)
        wmod_t = wmod.rearrange("(k p) (j d) -> p k j d", p=P, d=DIM)
        w_t = [w.rearrange("(k p) n -> p k n", p=P) for w in (wq, wk, wv)]
        wo_t = wo.rearrange("(h p) n -> p h n", p=P)
        LAST = PAIRS - 1
        COLS_BANK = (0, CH, 2 * BATCH * KT)
        GROUPS4 = TOK // CH * KT

        w_buffers = [(w_raw[:, j, :, :], w_hi[:, j, :, :], w_lo[:, j, :, :]) for j in range(3)]
        w_buffers.append((wo_raw[:, :, :], wo_hi[:, :, :], wo_lo[:, :, :]))

        def w_full_at(n):
            which, m = W_TILES[n]
            size = P if m < HM - 1 else HLAST
            if which < 2:
                return w_full[:, n % 4, 0:KT * size].rearrange("p (k h) -> p k h", k=KT)
            return w_full[0:size, n % 4, :]

        def rope_buffers(piece):
            return (straight_b, swapped_b) if piece in FIRST_QK[2:] else (straight, swapped)

        def turned_at(t, k0, k1):
            if t < 4:
                return lambda pT: pT.rearrange("p s q -> p (s q)")[:, t * P:t * P + (t + 1) * 3 * P]\
                    .rearrange("p (k q) -> p k q", q=3 * P)[:, :, 0:P]
            return lambda pT: pT[:, 9 - k1:9 - k0, (t - 4) * P:(t - 4) * P + P]

        def groups_of(t):
            return [(k0, min(k0 + 4, t + 1)) for k0 in range(0, t + 1, 4)]

        def qk_at(parity, which, first, size):
            return (qk_hi[:, parity, which, first:first + size], qk_lo[:, parity, which, first:first + size])

        @block.sync
        def _(sp):
            def load_w(j, n):
                if j == WO:
                    src = wo_t[:, bass.ds(n * 2, 2), :]
                else:
                    src = w_t[j][:, :, bass.ds(n * 2 * DH, 2 * DH)]
                sp.dma_start(w_buffers[j][0], src).then_inc(raw_ready[j], 16)

            def load_x(n):
                sp.dma_start(x_in[:, 4 * n:4 * n + 4, :], x_t[:, 4 * n:4 * n + 4, :]).then_inc(x_ready[n], 16)

            def load_mod(j, part, done):
                sp.dma_start(wmod_a[:, :, j, :], wmod_t[:, :, part, :]).then_inc(done, 16)

            sp.dma_start(c_rows[:, :], c.rearrange("b (k p) -> (b k) p", p=P)).then_inc(c_ready, 16)
            load_x(0)
            load_x(1)
            load_mod(0, 0, wmod_a_ready)
            load_mod(1, 1, wmod_a_ready)
            for n, src in enumerate((bq, bk, bv)):
                sp.dma_start(b_rows[n * HEADS:n * HEADS + HEADS, :], src.rearrange("(h d) -> h d", d=DH))\
                    .then_inc(b_rows_ready, 16)
            load_w(WK, 0)
            load_w(WQ, 0)
            load_x(2)
            load_x(3)
            sp.dma_start(cos_sb[:, :], cos).then_inc(tables_ready, 16)
            sp.dma_start(sin_sb[:, :], sin).then_inc(tables_ready, 16)
            load_w(WV, 0)

            def swap_halves(ps, piece):
                q = RANK[piece] % 2
                src, dst = rope_buffers(piece)
                sp.wait_ge(straight_ready, ps.rank(piece, 1))
                half = DH // 2
                for a, b in ((0, half), (half, 0)):
                    sp.dma_start(dst[a:a + half, q, :], src[b:b + half, q, :])\
                        .then_inc(first_swapped[RANK[piece]] if piece in FIRST_QK else swapped_ready[q], 16)

            def run(ps):
                for u in ps.units:
                    n = u // UNITS + 1
                    qk = [piece for what, _, piece in unit_plan(TENSOR_PLAN, u) if what == "make" and piece[0] == "qk"]
                    for piece in qk:
                        swap_halves(ps, piece)
                    if n < PAIRS and u % UNITS == 1:
                        for j, shared in ((WK, WK), (WQ, WQ), (WV, WO)):
                            sp.wait_ge(w_ready[shared], ps.passes(n))
                            load_w(j, ps.passes(n))
                    if n < PAIRS and u % UNITS == 2:
                        sp.wait_ge(w_ready[WV], ps.passes(n + 1))
                        load_w(WO, ps.passes(n))

            sp.wait_ge(zeroed, 1)
            for src, r0 in ((s_gate, 0), (s_up, HM)):
                sp.dma_start(s_rows[r0:r0 + HM - 1, :], src[0:(HM - 1) * P].rearrange("(m p) -> m p", p=P))\
                    .then_inc(s_rows_ready, 16)
                sp.dma_start(s_rows[r0 + HM - 1:r0 + HM, 0:HLAST],
                             src[(HM - 1) * P:HID].rearrange("(a p) -> a p", a=1)).then_inc(s_rows_ready, 16)
            sp.dma_start(s_rows[2 * HM:SROWS, :], s_down.rearrange("(k p) -> k p", p=P)).then_inc(s_rows_ready, 16)
            sp.dma_start(wo_all[:, :, :], wo_t).then_inc(wo_all_ready, 16)
            sp.dma_start(bo_wide[:, :], bo.rearrange("(a n) -> a n", a=1).broadcast_to([P, DIM]))\
                .then_inc(wo_all_ready, 16)
            for piece in FIRST_QK:
                swap_halves(Span(0, 0), piece)
            load_mod(2, 3, wmod_b_ready)
            load_mod(3, 4, wmod_b_ready)
            for j, part in enumerate((2, 5)):
                sp.dma_start(wmod_g[:, :, j, :], wmod_t[:, :, part, :]).then_inc(wmod_b_ready, 16)
            sp.wait_ge(w_ready[WV], 1)
            load_w(WO, 0)
            run(Span(0, 1))
            with sp.Fori(0, LAST) as i:
                run(Span(1, 1 + UNITS, i))
            run(Span(1 + LAST * UNITS, ALL_UNITS - 1))

            def load_x2(n):
                sp.dma_start(x2[:, 4 * n:4 * n + 4, :], x_t[:, 4 * n:4 * n + 4, :]).then_inc(x2_in_ready[n], 16)

            for j in range(4):
                sp.wait_ge(w_ready[j], PAIRS)
            sp.dma_start(int_down[:, :, :], wq_down.rearrange("(k p) h -> p k h", p=P)).then_inc(ints_ready[2], 16)
            sp.wait_ge(scores_ready, (ALL_UNITS - 1) * NQ)
            load_x2(0)
            load_x2(1)
            sp.wait_ge(piece_made, PIECE_AT[("qk", ALL_UNITS - 1, 0, 1)] + 1)
            for n, (dst, src) in enumerate(((int_gate, wq_gate), (int_up, wq_up))):
                sp.dma_start(dst[:, 0:HM - 1, :], src[0:(HM - 1) * P, :].rearrange("(m p) d -> p m d", p=P))\
                    .then_inc(ints_ready[n], 16)
                sp.dma_start(dst[0:HLAST, HM - 1, :], src[(HM - 1) * P:HID, :]).then_inc(ints_ready[n], 16)
            sp.wait_ge(scores_ready, ALL_UNITS * NQ)
            load_x2(2)
            load_x2(3)
            for first, size in OUT_TILES:
                sp.wait_ge(out_ready, first + size)
                sp.dma_start(out_t[:, first:first + size, :], y[:, first:first + size, :]).then_inc(stored, 16)
            sp.wait_ge(stored, 16 * len(OUT_TILES))

        @block.gpsimd
        def _(pool):
            pool.memset(s_rows[:, :], 0.0).then_inc(zeroed, 1)
            pool.memset(ident[:, :], 0.0).then_inc(pool_chain, 1)
            pool.memset(mask_b[:, :], 0.0).then_inc(pool_chain, 1)
            pool.wait_ge(pool_chain, 2)
            pool.affine_select(out=ident[:, :], in_=ident[:, :], compare_op=ALU.not_equal, fill=1.0, base=0,
                               pattern=[[-1, P]], channel_multiplier=1).then_inc(pool_chain, 1)
            pool.affine_select(out=mask_b[:, :], in_=mask_b[:, :], compare_op=ALU.is_ge, fill=MASKED, base=0,
                               pattern=[[-1, P]], channel_multiplier=1).then_inc(consts_ready, 1)
            pool.wait_ge(pool_chain, 3)
            pool.tensor_copy(ident_b[:, :], ident[:, :]).then_inc(consts_ready, 1)

            def w_low(j, n):
                raw, hi, lo = w_buffers[j]
                pool.wait_ge(w_hi_ready[j], n + 1)
                pool.tensor_tensor(lo, raw, hi.bitcast(F32), ALU.subtract).then_inc(w_ready[j], 1)

            def rotate(ps, piece):
                q, chunk = RANK[piece] % 2, piece[3]
                pool.wait_ge(swapped_ready[q], ps.count((RANK[piece] - 4) // 2 * 32 + 32, PER_PASS["qk"] // 2 * 32))
                cs = slice(chunk * CH, chunk * CH + CH)
                pool.tensor_tensor(swapped[:, q, :], swapped[:, q, :], sin_sb[:, cs], ALU.mult)
                pool.tensor_tensor(straight[:, q, :], straight[:, q, :], cos_sb[:, cs], ALU.mult).then_inc(rotated, 1)

            def qk_low(ps, piece):
                _, unit, which, chunk = piece
                pool.wait_ge(qk_hi_ready, ps.rank(piece, 1))
                hi, lo = qk_at(unit % 2, which, chunk * CH, CH)
                pool.tensor_tensor(lo, rope_buffers(piece)[0][:, RANK[piece] % 2, :], hi.bitcast(F32), ALU.subtract)\
                    .then_inc(qk_ready, 1)

            w_low(WK, 0)
            w_low(WQ, 0)
            w_low(WV, 0)
            pool.wait_ge(tables_ready, 32)
            for n, piece in enumerate(FIRST_QK):
                buf = rope_buffers(piece)[1][:, n % 2, :]
                pool.wait_ge(first_swapped[n], 32)
                pool.tensor_tensor(buf, buf, sin_sb[:, piece[3] * CH:piece[3] * CH + CH], ALU.mult).then_inc(rotated, 1)

            def run(ps):
                for what, x, piece in ps.work(POOL_PLAN):
                    if what == "rotate":
                        rotate(ps, piece)
                    elif what == "low":
                        qk_low(ps, piece)
                    else:
                        w_low(x, ps.passes(piece))

            run(Span(0, 1))
            with pool.Fori(0, LAST) as i:
                run(Span(1, 1 + UNITS, i))
            run(Span(1 + LAST * UNITS, ALL_UNITS + 1))

            def residual(n):
                part = (slice(None), slice(4 * n, 4 * n + 4), slice(None))
                pool.wait_ge(x2_in_ready[n], 16)
                pool.tensor_tensor(y[part], y[part], g_row[0][:, n // 2, None, :].broadcast_to([P, 4, DIM]), ALU.mult)\
                    .then_inc(pool_chain, 1)
                pool.wait_ge(pool_chain, 4 + n)
                pool.tensor_tensor(x2[part], x2[part], y[part], ALU.add).then_inc(x2_ready, 1)

            pool.wait_ge(g_ready, 1)
            pool.wait_ge(y_added, 1 + 4 * (ALL_UNITS - 2))
            residual(0)
            residual(1)

            def to_float(which):
                dst, src = ((f_gate, int_gate), (f_up, int_up), (f_down, int_down))[which]
                if which == 2:
                    pool.wait_ge(ints_ready[2], 16)
                    pool.tensor_scalar(dst[:, :, :], src[:, :, :], -ZERO_POINT, None, ALU.add).then_inc(wf_ready[2], 1)
                    return
                pool.wait_ge(ints_ready[which], 32)
                pool.tensor_scalar(dst[:, 0:HM - 1, :], src[:, 0:HM - 1, :], -ZERO_POINT, None, ALU.add)
                pool.tensor_scalar(dst[0:HLAST, HM - 1, :], src[0:HLAST, HM - 1, :], -ZERO_POINT, None, ALU.add)\
                    .then_inc(wf_ready[which], 1)

            pool.memset(largest[:, :], 0.0).then_inc(largest_ready, 1)
            for which in range(3):
                to_float(which)

            def h2_low(n):
                pool.wait_ge(h2_hi_ready, n + 1)
                part = (slice(None), n % KT, slice(n // KT * CH, n // KT * CH + CH))
                pool.tensor_tensor(hT_lo[part], h2_32[:, n % 4, :], hT_hi[part].bitcast(F32), ALU.subtract)\
                    .then_inc(h2_ready, 1)

            def w_part_low(n):
                which, m = W_TILES[n]
                size = P if m < HM - 1 else HLAST
                pool.wait_ge(wf_hi_ready, n + 1)
                if which < 2:
                    part = (slice(None), slice(None), slice(m * P, m * P + size))
                    hi, lo = wg_hi[which][part], wg_lo[which][part]
                else:
                    hi, lo = wd_hi[0:size, m, :], wd_lo[0:size, m, :]
                pool.tensor_tensor(lo, w_full_at(n), hi.bitcast(F32), ALU.subtract).then_inc(wf_late_ready, 1)

            for n in range(GROUPS4 // 2):
                h2_low(n)
            for n in range(NCH * HM):
                size = P if n % HM < HM - 1 else HLAST
                for what, j in BESIDE.get(n, []):
                    {"w": w_part_low, "h": h2_low}[what](j)
                pool.wait_ge(gu_hi_ready, n + 1)
                pool.tensor_tensor(gu_lo[0:size, n % GU, :], gu[0:size, n % 2, :],
                                   gu_hi[0:size, n % GU, :].bitcast(F32), ALU.subtract).then_inc(gu_split, 1)

        @block.scalar
        def _(act):
            def w_high(j):
                raw, hi, _ = w_buffers[j]
                nc.scalar.activation(hi, raw, ACT.Copy).then_inc(w_hi_ready[j], 1)

            def qk_out(ps, piece):
                _, unit, which, _ = piece
                q = RANK[piece] % 2
                act.wait_ge(piece_made, ps.pieces(piece))
                if RANK[piece] >= 4:
                    act.wait_ge(qk_ready, ps.rank(piece, -1))
                act.nop(nofuse=True)
                head = ps.count(unit // UNITS * 2 + unit % 2, 2)
                bias = (bq_s if which == 0 else cols[:, COL_BK:COL_BK + HEADS])[:, bass.ds(head, 1)]
                nc.scalar.activation(rope_buffers(piece)[0][:, q, :], ps_r[:, ps.bank(piece), :], ACT.Identity, bias=bias,
                                     scale=SCALE if which == 0 else 1.0).then_inc(straight_ready, 1)

            def gate_out(ps, piece):
                act.wait_ge(piece_made, ps.pieces(piece))
                nc.scalar.activation(g_row[piece[1]][:, :, :],
                                     ps_r[:, ps.bank(piece), :].rearrange("p (b n) -> p b n", b=BATCH), ACT.Copy)\
                    .then_inc(g_ready, 1)

            def qk_high(ps, piece):
                _, unit, which, chunk = piece
                act.wait_ge(qk_sum, ps.rank(piece, 1))
                hi, _ = qk_at(unit % 2, which, chunk * CH, CH)
                nc.scalar.activation(hi, rope_buffers(piece)[0][:, RANK[piece] % 2, :], ACT.Copy).then_inc(qk_hi_ready, 1)

            def v_high(ps, piece):
                _, pb, j = piece
                act.wait_ge(piece_made, ps.pieces(piece))
                nc.scalar.activation(v_hi[:, pb % BATCH, 2 * j:2 * j + 2, :],
                                     ps_r[:, ps.bank(piece), :].rearrange("p (t n) -> p t n", t=2),
                                     ACT.Copy).then_inc(v_hi_ready, 1)

            def o_high(ps, piece):
                act.wait_ge(piece_made, ps.pieces(piece))
                nc.scalar.activation(o_hi[:, piece[2], :], ps_r[:, ps.bank(piece), :], ACT.Copy).then_inc(o_hi_ready, 1)

            def col_out(first, size, n):
                act.wait_ge(cols_turned, n)
                nc.scalar.activation(cols[:, first:first + size], ps_s[:, 0, COLS_BANK[n - 1]:COLS_BANK[n - 1] + size],
                                     ACT.Copy).then_inc(cols_ready, 1)

            def mod_out(n):
                act.wait_ge(mod_made, n + 1)
                first, last = ((MOD_SA, MOD_SB), (MOD_SB, MOD_GB + KT))[n]
                nc.scalar.activation(mod[:, first:last, :],
                                     ps_s[:, 1, CH * n:CH * n + (last - first) * BATCH].rearrange("p (j b) -> p j b", b=BATCH),
                                     ACT.Copy).then_inc(mod_ready, 1)

            def roots(n, tiles):
                act.wait_ge(var_ready, n)
                nc.scalar.activation(root[:, tiles], var[:, tiles], ACT.Sqrt).then_inc(root_ready, 1)

            def h_out(n):
                k, b = n % KT, n // KT // 2
                act.wait_ge(xn_turned, n + 1)
                if n >= 4:
                    act.wait_ge(hT_ready, n - 3)
                src, shift, gain = ps_t[:, n % 2, :], mod[:, k, b:b + 1], mod[:, KT + k, b:b + 1]
                nc.scalar.activation(h32[:, n % 4, :], src, ACT.Identity, bias=shift, scale=gain)
                nc.scalar.activation(hT_hi[:, k, n // KT * CH:n // KT * CH + CH], src, ACT.Identity, bias=shift,
                                     scale=gain).then_inc(hhi_ready, 1)

            col_out(COL_C, BATCH * KT, 1)
            act.wait_ge(cols_ready, 1)
            nc.scalar.activation(tanh_c[:, :], cols[:, COL_C:COL_SG], ACT.Tanh, scale=0.5).then_inc(tanh_ready, 1)
            roots(1, slice(0, NTT // 2))
            mod_out(0)
            col_out(0, COL_C, 2)
            for j in (WK, WQ):
                act.wait_ge(raw_ready[j], 16)
                w_high(j)
            act.wait_ge(gain_ready, 1)
            for n in range(GROUPS4 // 2):
                h_out(n)
            act.wait_ge(bq_ready, 1)
            act.wait_ge(raw_ready[WV], 16)
            w_high(WV)
            for n, piece in enumerate(FIRST_QK):
                qk_out(Span(0, 0), piece)
                if n == 2:
                    roots(2, slice(NTT // 2, NTT))
            for piece in FIRST_V:
                v_high(Span(0, 0), piece)
            for n, piece in enumerate(FIRST_QK):
                if n in (1, 2):
                    h_out(GROUPS4 // 2 + n - 1)
                qk_high(Span(0, 0), piece)
            col_out(COL_SG, SROWS, 3)
            for n in range(GROUPS4 // 2 + 2, GROUPS4):
                h_out(n)
            mod_out(1)

            def turn_out(ps, u, step, j):
                k0, k1 = groups_of(ORDER[step])[j]
                act.wait_ge(turned, ps.groups(u, step, j + 1))
                nc.scalar.activation(
                    turned_at(ORDER[step], k0, k1)(pT_hi),
                    ps_t[:, (T_FIRST[step] + j) % 2, 0:(k1 - k0) * P].rearrange("p (k q) -> p k q", q=P),
                    ACT.Copy).then_inc(pT_hi_ready, 1)

            def exponentials(ps, u, step):
                t = ORDER[step]
                act.wait_ge(max_ready, ps.tiles(u, step + 1))
                if u * NQ + step >= 3:
                    act.wait_ge(turned, ps.groups(*divmod(u * NQ + step - 2, NQ)))
                nc.scalar.activation(probs[:, P_AT[step] * P:(P_AT[step] + t + 1) * P], ps_s[:, step % 2, 0:(t + 1) * P],
                                     ACT.Exp, bias=neg_max[:, t:t + 1],
                                     accum_out=row_sum[:, u % 2, t:t + 1]).then_inc(exp_ready, 1)

            def split_weights(ps, j, n):
                act.wait_ge(raw_ready[j], ps.count(n * 16 + 16, 16))
                used = {WO: ("wo", n * UNITS - 1, 1, 1), WV: ("v", 2 * n - 1, 3), WK: ("qk", n * UNITS - 1, 1, 1),
                        WQ: ("qk", n * UNITS - 1, 0, 1)}[j]
                if used in PIECE_AT:
                    act.wait_ge(piece_made, ps.pieces(used))
                w_high(j)

            def do(ps, what, x, piece):
                if what == "exp":
                    exponentials(ps, x, *piece)
                elif what == "turn":
                    turn_out(ps, x, *piece)
                elif what == "split":
                    split_weights(ps, x, piece)
                elif what == "out":
                    {"qk": qk_out, "gate": gate_out}[piece[0]](ps, piece)
                else:
                    {"qk": qk_high, "v": v_high, "pv": o_high}[piece[0]](ps, piece)

            def run(ps):
                for work in ps.work(SCALAR_PLAN):
                    do(ps, *work)

            run(Span(0, 1))
            with act.Fori(0, LAST) as i:
                run(Span(1, 1 + UNITS, i))
            run(Span(1 + LAST * UNITS, ALL_UNITS))

            def w_out(n):
                which, m = W_TILES[n]
                size = P if m < HM - 1 else HLAST
                bank = LATE_TURNS.index(("w", n)) % 2
                act.wait_ge(wf_turned, n + 1)
                if which < 2:
                    dst = wg_hi[which][:, :, m * P:m * P + size]
                    src = ps_t[:, bank, 0:KT * size].rearrange("p (k h) -> p k h", k=KT)
                else:
                    dst, src = wd_hi[0:size, m, :], ps_t[0:size, bank, 0:DIM]
                if n >= W_EARLY:
                    if n >= W_EARLY + 4:
                        act.wait_ge(wf_late_ready, n - W_EARLY - 3)
                    nc.scalar.activation(w_full_at(n), src, ACT.Copy)
                nc.scalar.activation(dst, src, ACT.Copy).then_inc(wf_hi_ready, 1)

            def h2_out(n):
                k, b = n % KT, n // KT // 2
                act.wait_ge(xn2_turned, n + 1)
                if n >= 4:
                    act.wait_ge(h2_ready, n - 3)
                src = ps_t[:, LATE_TURNS.index(("h", n)) % 2, :]
                shift, gain = mod[:, MOD_SB + k, b:b + 1], mod[:, MOD_CB + k, b:b + 1]
                nc.scalar.activation(h2_32[:, n % 4, :], src, ACT.Identity, bias=shift, scale=gain)
                nc.scalar.activation(hT_hi[:, k, n // KT * CH:n // KT * CH + CH], src, ACT.Identity, bias=shift,
                                     scale=gain).then_inc(h2_hi_ready, 1)

            ending = Span(ALL_UNITS, ALL_UNITS + 1)
            work = ending.work(SCALAR_PLAN)
            for x in work:
                if x[0] != "high":
                    do(ending, *x)
            for n in range(W_EARLY):
                w_out(n)
            roots(3, slice(0, NTT // 2))
            for x in work:
                if x[0] == "high":
                    do(ending, *x)
            for n in range(GROUPS4 // 2):
                h2_out(n)

            def gu_high(n):
                m = n % HM
                size = P if m < HM - 1 else HLAST
                act.wait_ge(gu_ready, n + 1)
                if n >= GU:
                    act.wait_ge(down_made, (n - GU) // HM * 2 + 2)
                nc.scalar.activation(gu_hi[0:size, n % GU, :], gu[0:size, n % 2, :], ACT.Copy).then_inc(gu_hi_ready, 1)

            for n in range(NCH * HM):
                m = n % HM
                size = P if m < HM - 1 else HLAST
                act.wait_ge(gate_made, n + 1)
                if n >= 2:
                    act.wait_ge(gu_ready, n - 1)
                nc.scalar.activation(tanh_g[0:size, n % 2, :], ps_s[0:size, n % 2, 0:CH], ACT.Tanh,
                                     scale=half_sg[0:size, m:m + 1])\
                    .then_inc(tanh_g_ready, 1)
                if n >= 1:
                    gu_high(n - 1)
                for what, j in BESIDE.get(n, []):
                    {"w": w_out, "h": h2_out}[what](j)
                if n == NORM_AT + 2:
                    roots(5, slice(NTT // 2, NTT))
            gu_high(NCH * HM - 1)

        @block.vector
        def _(dve):
            linked = [0]

            def link(ins):
                linked[0] += 1
                ins.then_inc(dve_chain, 1)
                dve.wait_ge(dve_chain, linked[0])

            norms = [0]

            def norm(src, dst, tiles, tile_ready, done):
                moments(src, tiles, tile_ready)
                reciprocal_roots(tiles)
                normalise(src, dst, tiles, done)

            def moments(src, tiles, tile_ready):
                for t in tiles:
                    if t % 4 == 0:
                        tile_ready(t // 4)
                    last = nc.vector.bn_stats(bn[:, t, :], src[:, t, :])
                link(last)
                for t in tiles:
                    last = nc.vector.bn_aggr(mv[:, t, :], bn[:, t, :])
                link(last)
                part = slice(tiles[0], tiles[-1] + 1)
                nc.vector.tensor_scalar(var[:, part], mv[:, part, 1], EPS, None, ALU.add).then_inc(var_ready, 1)

            def reciprocal_roots(tiles):
                part = slice(tiles[0], tiles[-1] + 1)
                norms[0] += 1
                dve.wait_ge(root_ready, norms[0])
                link(nc.vector.reciprocal(rstd[:, part], root[:, part]))
                link(nc.vector.tensor_tensor(newton[:, part], rstd[:, part], rstd[:, part], ALU.mult))
                link(nc.vector.tensor_tensor(newton[:, part], newton[:, part], var[:, part], ALU.mult))
                link(nc.vector.tensor_scalar(newton[:, part], newton[:, part], -0.5, 1.5, ALU.mult, ALU.add))
                link(nc.vector.tensor_tensor(rstd[:, part], rstd[:, part], newton[:, part], ALU.mult))

            def normalise(src, dst, tiles, done):
                for t in tiles:
                    ins = nc.vector.tensor_scalar(dst(t), src[:, t, :], mv[:, t, 0:1], rstd[:, t:t + 1],
                                                  ALU.subtract, ALU.mult)
                    if t % 4 == 3:
                        ins.then_inc(done, 1)

            dve.wait_ge(tanh_ready, 1)
            link(nc.vector.scalar_tensor_tensor(silu_c[:, :], tanh_c[:, :], 1.0, cols[:, COL_C:COL_SG], ALU.add, ALU.mult))
            nc.vector.tensor_scalar(silu_c[:, :], silu_c[:, :], 0.5, None, ALU.mult).then_inc(silu_ready, 1)
            norm(x_in, lambda t: xn[:, t, :], range(NTT // 2), lambda n: dve.wait_ge(x_ready[n], 16), xn_ready)

            def gains(n):
                part = (slice(None), slice((MOD_CA, MOD_CB)[n], (MOD_CA, MOD_CB)[n] + KT), slice(None))
                dve.wait_ge(mod_ready, n + 1)
                nc.vector.tensor_scalar(mod[part], mod[part], 1.0, None, ALU.add).then_inc(gain_ready, 1)

            gains(0)
            dve.wait_ge(cols_ready, 2)
            nc.vector.tensor_scalar(bq_s[:, :], cols[:, COL_BQ:COL_BQ + HEADS], SCALE, None, ALU.mult).then_inc(bq_ready, 1)
            def h_low(n):
                dve.wait_ge(hhi_ready, n + 1)
                part = (slice(None), n % KT, slice(n // KT * CH, n // KT * CH + CH))
                nc.vector.tensor_tensor(hT_lo[part], h32[:, n % 4, :], hT_hi[part].bitcast(F32), ALU.subtract)\
                    .then_inc(hT_ready, 1)

            for n in range(GROUPS4 // 2):
                h_low(n)
            norm(x_in, lambda t: xn[:, t, :], range(NTT // 2, NTT), lambda n: dve.wait_ge(x_ready[n], 16), xn_ready)

            def qk_add(ps, piece):
                q = RANK[piece] % 2
                here, there = rope_buffers(piece)
                dve.wait_ge(rotated, ps.rank(piece, 1))
                nc.vector.tensor_tensor(here[:, q, :], here[:, q, :], there[:, q, :], ALU.add).then_inc(qk_sum, 1)

            def v_low(ps, piece):
                _, pb, j = piece
                dve.wait_ge(v_hi_ready, ps.rank(piece, 1))
                part = (slice(None), pb % BATCH, slice(2 * j, 2 * j + 2), slice(None))
                nc.vector.tensor_tensor(v_lo[part], ps_r[:, ps.bank(piece), :].rearrange("p (t n) -> p t n", t=2),
                                        v_hi[part].bitcast(F32), ALU.subtract).then_inc(v_ready, 1)

            def o_low(ps, piece):
                chunk = piece[2]
                dve.wait_ge(o_hi_ready, ps.rank(piece, 1))
                nc.vector.tensor_tensor(o_lo[:, chunk, :], ps_r[:, ps.bank(piece), :], o_hi[:, chunk, :].bitcast(F32),
                                        ALU.subtract).then_inc(o_ready, 1)

            def cosine(n):
                buf = rope_buffers(FIRST_QK[n])[0][:, n % 2, :]
                dve.wait_ge(first_swapped[n], 32)
                link(nc.vector.tensor_tensor(buf, buf, cos_sb[:, FIRST_QK[n][3] * CH:FIRST_QK[n][3] * CH + CH], ALU.mult))

            def first_low(n):
                _, unit, which, chunk = FIRST_QK[n]
                dve.wait_ge(qk_hi_ready, n + 1)
                hi, lo = qk_at(unit % 2, which, chunk * CH, CH)
                nc.vector.tensor_tensor(lo, rope_buffers(FIRST_QK[n])[0][:, n % 2, :], hi.bitcast(F32), ALU.subtract)\
                    .then_inc(qk_ready, 1)

            dve.wait_ge(tables_ready, 32)
            cosine(0)
            cosine(1)
            qk_add(Span(0, 0), FIRST_QK[0])
            for piece in FIRST_V:
                v_low(Span(0, 0), piece)
            cosine(2)
            qk_add(Span(0, 0), FIRST_QK[1])
            first_low(0)
            cosine(3)
            qk_add(Span(0, 0), FIRST_QK[2])
            first_low(1)
            dve.wait_ge(wo_all_ready, 32)
            dve.wait_ge(attn_bias_made, 1)
            nc.vector.tensor_tensor(attn_bias[:, :], ps_s[:, 0, CH:CH + DIM], bo_wide[:, :], ALU.add)\
                .then_inc(attn_bias_ready, 1)
            h_low(GROUPS4 // 2)
            qk_add(Span(0, 0), FIRST_QK[3])
            first_low(2)
            h_low(GROUPS4 // 2 + 1)
            first_low(3)
            for n in range(GROUPS4 // 2 + 2, GROUPS4):
                h_low(n)
            dve.wait_ge(attn_bias_ready, 1)
            nc.vector.tensor_copy(y[:, :, :], attn_bias[:, None, :].broadcast_to([P, NTT, DIM])).then_inc(y_added, 1)
            gains(1)
            dve.wait_ge(cols_ready, 3)
            nc.vector.tensor_scalar(half_sg[:, :], cols[:, COL_SG:COL_SG + HM], 0.5, None, ALU.mult)
            nc.vector.scalar_tensor_tensor(half_sgu[:, :], cols[:, COL_SU:COL_SU + HM], 0.5, cols[:, COL_SG:COL_SG + HM],
                                           ALU.mult, ALU.mult)
            gates, scaled = mod[:, MOD_GA:MOD_GB + KT, :], mod[:, MOD_GB:MOD_GB + KT, :]
            nc.vector.tensor_scalar(sign[:, :, :], gates, 0.0, 2.0, ALU.is_ge, ALU.mult)
            link(nc.vector.scalar_tensor_tensor(magnitude[:, :, :], gates, -1.0, gates, ALU.mult, ALU.max))
            link(nc.vector.tensor_scalar(magnitude[:, :, :], magnitude[:, :, :], 0.25, None, ALU.max))
            link(nc.vector.scalar_tensor_tensor(gates, sign[:, :, :], -1.0, magnitude[:, :, :], ALU.add, ALU.mult))
            nc.vector.tensor_tensor(scaled, scaled, cols[:, COL_SD:COL_SD + KT, None].broadcast_to([P, KT, BATCH]),
                                    ALU.mult).then_inc(gates_ready, 1)

            def turn_low(ps, u, step, j):
                t = ORDER[step]
                k0, k1 = groups_of(t)[j]
                dve.wait_ge(pT_hi_ready, ps.groups(u, step, j + 1))
                nc.vector.tensor_tensor(
                    turned_at(t, k0, k1)(pT_lo),
                    ps_t[:, (T_FIRST[step] + j) % 2, 0:(k1 - k0) * P].rearrange("p (k q) -> p k q", q=P),
                    turned_at(t, k0, k1)(pT_hi).bitcast(F32), ALU.subtract).then_inc(pT_ready, 1)

            def wo_add(ps, piece):
                _, u, chunk, j = piece
                if j == 0:
                    nc.vector.reciprocal(inv_sum[:, u % 2, 4 * chunk:4 * chunk + 4],
                                         row_sum[:, u % 2, 4 * chunk:4 * chunk + 4]).then_inc(inv_ready, 1)
                    dve.wait_ge(inv_ready, ps.count(RANK[piece] // 2 + 1, PER_PASS["wo"] // 2))
                dve.wait_ge(piece_made, ps.pieces(piece))
                for s in range(2):
                    t = 4 * chunk + 2 * j + s
                    tt = unit_batch(u) * NQ + t
                    ins = nc.vector.scalar_tensor_tensor(
                        y[:, tt, :], ps_r[:, ps.bank(piece), s * DIM:s * DIM + DIM], inv_sum[:, u % 2, t:t + 1],
                        y[:, tt, :], ALU.mult, ALU.add)
                ins.then_inc(y_added, 1)

            def row_max(ps, u, step):
                t = ORDER[step]
                dve.wait_ge(scores_ready, ps.tiles(u, step + 1))
                nc.vector.tensor_reduce(neg_max[:, t:t + 1], ps_s[:, step % 2, 0:(t + 1) * P], AX, ALU.max,
                                        negate=True).then_inc(max_ready, 1)

            def do(ps, what, x, piece):
                if what == "max":
                    row_max(ps, x, *piece)
                elif what == "turn":
                    turn_low(ps, x, *piece)
                else:
                    {"qk": qk_add, "v": v_low, "pv": o_low, "wo": wo_add}[piece[0]](ps, piece)

            def run(ps):
                for work in ps.work(VECTOR_PLAN):
                    do(ps, *work)

            run(Span(0, 1))
            with dve.Fori(0, LAST) as i:
                run(Span(1, 1 + UNITS, i))
            run(Span(1 + LAST * UNITS, ALL_UNITS))

            def w_part_low(n):
                which, m = W_TILES[n]
                size = P if m < HM - 1 else HLAST
                bank = LATE_TURNS.index(("w", n)) % 2
                dve.wait_ge(wf_hi_ready, n + 1)
                part = (slice(None), slice(None), slice(m * P, m * P + size))
                nc.vector.tensor_tensor(wg_lo[which][part], ps_t[:, bank, 0:KT * size].rearrange("p (k h) -> p k h", k=KT),
                                        wg_hi[which][part].bitcast(F32), ALU.subtract).then_inc(wf_lo_ready, 1)

            def four(n):
                return range(4 * n, 4 * n + 4)

            def x2_arrived(n):
                dve.wait_ge(x2_ready, n + 1)

            ending = Span(ALL_UNITS, ALL_UNITS + 1)
            work = ending.work(VECTOR_PLAN)
            for x in work:
                if x[0] == "turn":
                    do(ending, *x)
            for n in range(W_EARLY):
                w_part_low(n)
            norm(x2, lambda t: xn2[0][:, t, :], range(NQ), x2_arrived, xn2_ready)
            for x in work:
                if x[0] != "turn":
                    do(ending, *x)

            dve.wait_ge(largest_ready, 1)
            for which, w in enumerate((f_gate, f_up)):
                dve.wait_ge(wf_ready[which], 1)
                nc.vector.tensor_reduce(largest[:, 2 * which:2 * which + 1], w[:, 0:HM - 1, :].rearrange("p m d -> p (m d)"), AX,
                                        ALU.max, apply_absolute_value=True)
                nc.vector.tensor_reduce(largest[0:HLAST, 2 * which + 1:2 * which + 2], w[0:HLAST, HM - 1, :], AX, ALU.max,
                                        apply_absolute_value=True)
            dve.wait_ge(wf_ready[2], 1)
            link(nc.vector.tensor_reduce(largest[:, 4:5], f_down[:, :, :].rearrange("p k h -> p (k h)"), AX, ALU.max,
                                         apply_absolute_value=True))
            nc.vector.tensor_reduce(largest_of[:, :], largest[:, :], AX, ALU.max).then_inc(largest_ready, 1)

            def weights_width():
                dve.wait_ge(largest_turned, 1)
                link(nc.vector.tensor_reduce(largest_all[:, :], ps_r[0:1, 1, 0:P], AX, ALU.max))
                nc.vector.tensor_scalar(wide[:, :], largest_all[:, :], WHOLE, None, ALU.is_gt).then_inc(wide_ready, 1)

            def residual(n):
                part = (slice(None), slice(4 * n, 4 * n + 4), slice(None))
                dve.wait_ge(x2_in_ready[n], 16)
                link(nc.vector.tensor_tensor(y[part], y[part], g_row[0][:, n // 2, None, :].broadcast_to([P, 4, DIM]),
                                             ALU.mult))
                nc.vector.tensor_tensor(x2[part], x2[part], y[part], ALU.add).then_inc(x2_ready, 1)

            def finish(first, size, src):
                part = (slice(None), slice(first, first + size), slice(None))
                link(nc.vector.tensor_tensor(y[part], src, g_row[1][:, first // NQ, None, :].broadcast_to([P, size, DIM]),
                                             ALU.mult))
                ins = nc.vector.tensor_tensor(y[part], y[part], x2[part], ALU.add)
                ins.then_inc(out_ready, size)

            for n in range(NCH * HM):
                m = n % HM
                size = P if m < HM - 1 else HLAST
                dve.wait_ge(tanh_g_ready, n + 1)
                link(nc.vector.scalar_tensor_tensor(silu_g[0:size, n % 2, :], tanh_g[0:size, n % 2, :], 1.0,
                                                    ps_s[0:size, n % 2, 0:CH], ALU.add, ALU.mult))
                dve.wait_ge(up_made, n + 1)
                if n >= 2:
                    dve.wait_ge(gu_split, n - 1)
                nc.vector.scalar_tensor_tensor(gu[0:size, n % 2, :], ps_s[0:size, n % 2, CH:2 * CH],
                                               half_sgu[0:size, m:m + 1], silu_g[0:size, n % 2, :], ALU.mult, ALU.mult)\
                    .then_inc(gu_ready, 1)
                if n < 2:
                    dve.wait_ge(g_ready, 1)
                    residual(2 + n)
                elif n in (NORM_AT, NORM_AT + 1):
                    moments(x2, four(NCH // 2 + n - NORM_AT), x2_arrived)
                elif n in (NORM_AT + 3, NORM_AT + 4):
                    if n == NORM_AT + 3:
                        reciprocal_roots(range(NQ, NTT))
                    normalise(x2, lambda t: xn2[1][:, t % NQ, :], four(NCH // 2 + n - NORM_AT - 3), xn2_ready)
                if n == 4:
                    weights_width()
                if n >= HM and m in (1, 2):
                    j = n // HM * 2 - 2 + m - 1
                    dve.wait_ge(g_ready, 2)
                    dve.wait_ge(down_made, j + 1)
                    finish(2 * j, 2, ps_r[:, j % 2, :].rearrange("p (t n) -> p t n", t=2))
            for j in range(4):
                dve.wait_ge(down_made, (NCH - 1) * 2 + j + 1)
                finish(NTT - 4 + j, 1, (ps_r, ps_t)[j // 2][:, j % 2, None, 0:DIM])

        @block.tensor
        def _(pe):
            def three(out, stationary, moving, first, last):
                (shi, slo), (mhi, mlo) = stationary, moving
                nc.tensor.matmul(out, shi, mhi, start=first, stop=False)
                nc.tensor.matmul(out, shi, mlo, start=False, stop=False)
                return nc.tensor.matmul(out, slo, mhi, start=False, stop=last)

            def two(out, stationary, moving, first, last):
                (shi, slo), (mhi, mlo) = stationary, moving
                nc.tensor.matmul(out, shi, mhi, start=first, stop=False)
                if mlo is None:
                    return nc.tensor.matmul(out, slo, mhi, start=False, stop=last)
                return nc.tensor.matmul(out, shi, mlo, start=False, stop=last)

            def wait_bank(ps, piece):
                old = ps.before(piece)
                if old is None:
                    return
                if old[0] == "qk":
                    pe.wait_ge(straight_ready, ps.rank(old, 1))
                elif old[0] == "v":
                    pe.wait_ge(v_ready, ps.rank(old, 1))
                elif old[0] == "pv":
                    pe.wait_ge(o_ready, ps.rank(old, 1))
                elif old[0] == "gate":
                    pe.wait_ge(g_ready, ps.rank(old, 1))
                else:
                    pe.wait_ge(y_added, ps.rank(old, 2))

            def w_at(j, k, first, size):
                return w_hi[:, j, k, first:first + size], w_lo[:, j, k, first:first + size]

            def h_at(k, first, size):
                return hT_hi[:, k, first:first + size], hT_lo[:, k, first:first + size]

            def make(ps, piece):
                wait_bank(ps, piece)
                dst = ps_r[:, ps.bank(piece), :]
                if piece[0] == "qk":
                    _, u, which, chunk = piece
                    if u % UNITS == 0 and chunk == 0:
                        pe.wait_ge(w_ready[which], ps.passes(u // UNITS + 1))
                    for k in range(KT):
                        ins = three(dst, w_at(which, k, u % 2 * DH, DH),
                                    h_at(k, unit_batch(u) * SEQ + chunk * CH, CH), k == 0, k == KT - 1)
                elif piece[0] == "v":
                    _, pb, j = piece
                    if pb % BATCH == 0 and j == 0:
                        pe.wait_ge(w_ready[WV], ps.passes(pb // BATCH + 1))
                    for s in range(2):
                        for k in range(KT):
                            ins = three(dst[:, s * 2 * DH:s * 2 * DH + 2 * DH],
                                        h_at(k, pb % BATCH * SEQ + (2 * j + s) * P, P), w_at(WV, k, 0, 2 * DH),
                                        k == 0, k == KT - 1)
                elif piece[0] == "pv":
                    _, u, chunk = piece
                    b, d0 = unit_batch(u), u % 2 * DH
                    if u % 2 == 0 and chunk == 0:
                        pe.wait_ge(v_ready, ps.rank(("v", u // 2, 3), 1))
                    step = max(s for s in range(NQ) if ORDER[s] // 4 == chunk)
                    pe.wait_ge(pT_ready, ps.groups(u, step, T_GROUPS[step]))
                    n_keys = 4 * chunk + 4
                    for k in range(n_keys):
                        q0 = max(0, k - 4 * chunk) * P
                        slot, col = (k, 0) if chunk == 0 else (8 - k, q0)
                        ins = three(dst[:, q0:CH], (v_hi[:, b, k, d0:d0 + DH], v_lo[:, b, k, d0:d0 + DH]),
                                    (pT_hi[:, slot, col:col + CH - q0], pT_lo[:, slot, col:col + CH - q0]),
                                    k == 0, k == n_keys - 1)
                elif piece[0] == "gate":
                    pe.wait_ge(gates_ready, 1)
                    for b in range(BATCH):
                        for k in range(KT):
                            column = mod[:, (MOD_GA, MOD_GB)[piece[1]] + k, b:b + 1]
                            ins = nc.tensor.matmul(dst[:, b * DIM + k * P:b * DIM + k * P + P],
                                                   column.broadcast_to([P, P]), ident[:, :], start=True, stop=True)
                else:
                    _, u, chunk, j = piece
                    if j == 0:
                        pe.wait_ge(o_ready, ps.rank(("pv", u, chunk), 1))
                    if u % UNITS == 0 and j == 0 and chunk == 0:
                        pe.wait_ge(w_ready[WO], ps.passes(u // UNITS + 1))
                    for s in range(2):
                        q0 = (2 * j + s) * P
                        ins = three(dst[:, s * DIM:s * DIM + DIM],
                                    (o_hi[:, chunk, q0:q0 + P], o_lo[:, chunk, q0:q0 + P]),
                                    (wo_hi[:, u % 2, :], wo_lo[:, u % 2, :]), True, True)
                ins.then_inc(piece_made, 1)

            def scores(ps, u, step):
                t = ORDER[step]
                if u * NQ + step == 0:
                    pe.wait_ge(cols_ready, 3)
                    pe.wait_ge(attn_bias_ready, 1)
                elif u * NQ + step == 1:
                    pe.wait_ge(mod_ready, 2)
                else:
                    pe.wait_ge(exp_ready, ps.tiles(u, step - 1))
                if step < 2:
                    pe.wait_ge(qk_ready, ps.count(4 * u + (2 if t < 4 else 4), PER_PASS["qk"]))
                q = qk_at(u % 2, 0, t * P, P)
                for k0 in range(0, (t + 1) * P, CH):
                    size = min(CH, (t + 1) * P - k0)
                    diagonal = k0 + size == (t + 1) * P
                    three(ps_s[:, step % 2, k0:k0 + size], q, qk_at(u % 2, 1, k0, size), True, not diagonal)
                ins = nc.tensor.matmul(ps_s[:, step % 2, t * P:t * P + P], ident_b[:, :], mask_b[:, :],
                                       start=False, stop=True)
                ins.then_inc(scores_ready, 1)

            def turn(ps, u, step, j):
                t = ORDER[step]
                k0, k1 = groups_of(t)[j]
                if j == 0:
                    pe.wait_ge(exp_ready, ps.tiles(u, step + 1))
                bank = (T_FIRST[step] + j) % 2
                if u * T_UNIT + T_FIRST[step] + j >= 2:
                    pe.wait_ge(pT_ready, ps.groups(u, step, j - 1))
                for k in range(k0, k1):
                    at_ = (k if t < 4 else k0 + k1 - 1 - k) - k0
                    ins = nc.tensor.transpose(ps_t[:, bank, at_ * P:at_ * P + P],
                                              probs[:, (P_AT[step] + k) * P:(P_AT[step] + k) * P + P], ident[:, :])
                ins.then_inc(turned, 1)

            pe.wait_ge(consts_ready, 2)
            def turn_rows(src, size, n):
                nc.tensor.transpose(ps_s[:, 0, COLS_BANK[n]:COLS_BANK[n] + size], src[:, :], ident[0:size, 0:size])\
                    .then_inc(cols_turned, 1)

            def modulation(n):
                for j in ((0, 1), (2, 3, 4, 5))[n]:
                    for k in range(KT):
                        for kk in range(KT):
                            at_ = CH * n + (KT * (j - 2 * n) + k) * BATCH
                            src = wmod_a[:, kk, j, k * P:k * P + P] if j < 4 else wmod_g[:, kk, j - 4, k * P:k * P + P]
                            ins = nc.tensor.matmul(ps_s[:, 1, at_:at_ + BATCH], src,
                                                   silu_c[:, kk:BATCH * KT:KT], start=kk == 0, stop=kk == KT - 1)
                ins.then_inc(mod_made, 1)

            pe.wait_ge(c_ready, 16)
            turn_rows(c_rows, BATCH * KT, 0)
            pe.wait_ge(silu_ready, 1)
            pe.wait_ge(wmod_a_ready, 32)
            modulation(0)
            pe.wait_ge(b_rows_ready, 48)
            turn_rows(b_rows, 3 * HEADS, 1)

            def turn_tokens(tile, bank, ready, n, done):
                k, chunk = n % KT, n // KT
                pe.wait_ge(ready, chunk + 1)
                for t in range(4):
                    ins = nc.tensor.transpose(ps_t[:, bank, t * P:t * P + P], tile(4 * chunk + t)[:, k * P:k * P + P],
                                              ident[:, :])
                ins.then_inc(done, 1)

            def turn_xn(n):
                if n >= 2:
                    pe.wait_ge(hhi_ready, n - 1)
                turn_tokens(lambda t: xn[:, t, :], n % 2, xn_ready, n, xn_turned)

            for n in range(GROUPS4 // 2):
                turn_xn(n)
            pe.wait_ge(w_ready[WK], 1)
            for n, piece in enumerate(FIRST_QK):
                pe.wait_ge(hT_ready, KT * (n // 2) + KT)
                make(Span(0, 0), piece)
            pe.wait_ge(w_ready[WV], 1)
            for piece in FIRST_V:
                make(Span(0, 0), piece)
            turn_xn(GROUPS4 // 2)
            turn_xn(GROUPS4 // 2 + 1)
            pe.wait_ge(cols_ready, 2)
            pe.wait_ge(wo_all_ready, 32)
            for h in range(HEADS):
                ins = nc.tensor.matmul(ps_s[:, 0, CH:CH + DIM], cols[:, COL_BV + h:COL_BV + h + 1].broadcast_to([P, P]),
                                       wo_all[:, h, :], start=h == 0, stop=h == HEADS - 1)
            ins.then_inc(attn_bias_made, 1)
            for n in range(GROUPS4 // 2 + 2, GROUPS4):
                turn_xn(n)
            pe.wait_ge(s_rows_ready, 80)
            turn_rows(s_rows, SROWS, 2)
            pe.wait_ge(wmod_b_ready, 64)
            modulation(1)

            def do(ps, what, x, piece):
                if what == "scores":
                    scores(ps, x, *piece)
                elif what == "turn":
                    turn(ps, x, *piece)
                else:
                    make(ps, piece)

            def run(ps):
                for work in ps.work(TENSOR_PLAN):
                    do(ps, *work)

            run(Span(0, 1))
            pe.wait_ge(hT_ready, GROUPS4)
            pe.wait_ge(v_ready, sum(piece[0] == "v" for piece in BEFORE_LOOP))
            pe.wait_ge(straight_ready, sum(piece[0] == "qk" for piece in BEFORE_LOOP))
            with pe.Fori(0, LAST) as i:
                run(Span(1, 1 + UNITS, i))
            run(Span(1 + LAST * UNITS, ALL_UNITS))

            def wait_late(x):
                at_ = LATE_TURNS.index(x)
                if at_ < 2:
                    pe.wait_ge(pT_ready, ALL_UNITS * T_UNIT)
                    return at_
                what, n = LATE_TURNS[at_ - 2]
                if what == "w":
                    pe.wait_ge(wf_lo_ready if n < W_EARLY else wf_hi_ready, n + 1)
                else:
                    pe.wait_ge(h2_hi_ready, n + 1)
                return at_ % 2

            def turn_w(n):
                which, m = W_TILES[n]
                size = P if m < HM - 1 else HLAST
                bank = wait_late(("w", n))
                pe.wait_ge(wf_ready[which], 1)
                for k in range(KT):
                    if which < 2:
                        src = (f_gate, f_up)[which][0:size, m, k * P:k * P + P]
                        ins = nc.tensor.transpose(ps_t[:, bank, k * size:k * size + size], src, ident[0:size, 0:size])
                    else:
                        ins = nc.tensor.transpose(ps_t[0:size, bank, k * P:k * P + P], f_down[:, k, m * P:m * P + size],
                                                  ident[:, :])
                ins.then_inc(wf_turned, 1)

            def turn_xn2(n):
                bank = wait_late(("h", n))
                turn_tokens(lambda t: xn2[t // NQ][:, t % NQ, :], bank, xn2_ready, n, xn2_turned)

            ending = Span(ALL_UNITS, ALL_UNITS + 1)
            work = ending.work(TENSOR_PLAN)
            for x in work:
                if x[0] == "turn":
                    do(ending, *x)
            for n in range(W_EARLY):
                turn_w(n)
            rest = [x for x in work if x[0] != "turn"]
            for x in rest[0:2]:
                do(ending, *x)
            for n in range(GROUPS4 // 2):
                turn_xn2(n)
                do(ending, *rest[2 + n])

            def down(n, j, wide_weights):
                pe.wait_ge(gu_split, n * HM + HM)
                if n == 0:
                    pe.wait_ge(y_added, 1 + 4 * ALL_UNITS)
                else:
                    pe.wait_ge(out_ready, 4 * n - 2 + 2 * j)
                for s in range(2):
                    for m in range(HM):
                        ins = down_part(ps_r[:, j, s * DIM:s * DIM + DIM], 2 * j + s, n, m, wide_weights)
                ins.then_inc(down_made, 1)

            def down_part(out, t, chunk, m, wide_weights):
                size = P if m < HM - 1 else HLAST
                slot = (chunk * HM + m) % GU
                hidden = gu_hi[0:size, slot, t * P:t * P + P], gu_lo[0:size, slot, t * P:t * P + P]
                if wide_weights:
                    return three(out, hidden, (wd_hi[0:size, m, :], wd_lo[0:size, m, :]), m == 0, m == HM - 1)
                return two(out, hidden, (wd_hi[0:size, m, :], None), m == 0, m == HM - 1)

            def gate_up(n, wide_weights):
                chunk, m = divmod(n, HM)
                size = P if m < HM - 1 else HLAST
                if n >= 2:
                    pe.wait_ge(gu_ready, n - 1)
                for which, done in enumerate((gate_made, up_made)):
                    for k in range(KT):
                        dst = ps_s[0:size, n % 2, which * CH:which * CH + CH]
                        hi, lo = wg_hi[which][:, k, m * P:m * P + size], wg_lo[which][:, k, m * P:m * P + size]
                        if wide_weights:
                            ins = three(dst, (hi, lo), h_at(k, chunk * CH, CH), k == 0, k == KT - 1)
                        else:
                            ins = two(dst, (hi, None), h_at(k, chunk * CH, CH), k == 0, k == KT - 1)
                    ins.then_inc(done, 1)

            def beside(n):
                for what, j in BESIDE.get(n, []):
                    {"w": turn_w, "h": turn_xn2}[what](j)

            pe.wait_ge(h2_ready, KT)
            for n in range(HM):
                if 2 * n < W_EARLY:
                    pe.wait_ge(wf_lo_ready, 2 * n + 2)
                else:
                    pe.wait_ge(wf_late_ready, 2 * n + 2 - W_EARLY)
                gate_up(n, True)
                beside(n)
                if n == 2:
                    pe.wait_ge(y_added, 1 + 4 * ALL_UNITS)
                    pe.wait_ge(largest_ready, 2)
                    nc.tensor.transpose(ps_r[0:1, 1, 0:P], largest_of[:, :], ident[:, :]).then_inc(largest_turned, 1)

            def chunks(wide_weights):
                for n in range(HM, NCH * HM):
                    chunk, m = divmod(n, HM)
                    if m == 0:
                        pe.wait_ge(h2_ready, chunk * KT + KT)
                    gate_up(n, wide_weights)
                    beside(n)
                    if m in (1, 2):
                        if chunk == 1 and m == 1:
                            if wide_weights:
                                pe.wait_ge(wf_late_ready, len(W_TILES) - W_EARLY)
                            else:
                                pe.wait_ge(wf_hi_ready, len(W_TILES))
                        down(chunk - 1, m - 1, wide_weights)
                pe.wait_ge(out_ready, NTT - 4)
                pe.wait_ge(h2_hi_ready, GROUPS4)
                outs = [ps[:, j, 0:DIM] for ps in (ps_r, ps_t) for j in range(2)]
                for m in range(HM):
                    pe.wait_ge(gu_split, (NCH - 1) * HM + m + 1)
                    for t in range(4):
                        ins = down_part(outs[t], t, NCH - 1, m, wide_weights)
                        if m == HM - 1:
                            ins.then_inc(down_made, 1)

            pe.wait_ge(wide_ready, 1)
            some_wide = pe.value_load(wide[0:1, 0:1], min_val=0, max_val=1)
            with pe.If(some_wide == 1):
                chunks(True)
            with pe.Else():
                chunks(False)


def rotary_tables():
    inv_freq = np.float32(1.0) / (10000.0 ** (np.arange(0, DH, 2) / DH)).astype(np.float32)
    freqs = np.arange(SEQ, dtype=np.float32)[None, :] * inv_freq[:, None]
    cos = np.cos(freqs.astype(np.float64)).astype(np.float32)
    sin = np.sin(freqs.astype(np.float64)).astype(np.float32)
    return np.concatenate([cos, cos]), np.concatenate([-sin, sin])


INPUTS = ["L0_attn_x", "L0_attn_Wq", "L0_attn_bq", "L0_attn_Wk", "L0_attn_bk", "L0_attn_Wv", "L0_attn_bv",
          "L0_attn_Wo", "L0_attn_bo", "L0_ffn_wq_gate", "L0_ffn_s_gate", "L0_ffn_wq_up", "L0_ffn_s_up",
          "L0_ffn_wq_down", "L0_ffn_s_down", "L0_c", "L0_wmod"]


def kernel(**inputs):
    import concourse.bacc as bacc
    from concourse.bass_utils import run_bass_kernel_spmd

    nc = bacc.Bacc("TRN2", target_bir_lowering=False, num_devices=1)
    arrays, args = {}, []
    cos, sin = rotary_tables()
    for name, a in [(n, inputs[n]) for n in INPUTS] + [("rotary_cos", cos), ("rotary_sin", sin)]:
        a = np.ascontiguousarray(a)
        arrays[f"in_{name}"] = a
        args.append(nc.dram_tensor(f"in_{name}", a.shape, mybir.dt.from_np(a.dtype), kind="ExternalInput").ap())
    out = nc.dram_tensor("out_0", (BATCH, SEQ, DIM), F32, kind="ExternalOutput").ap()
    build(nc, *args, out)
    got = run_bass_kernel_spmd(nc, [arrays], core_ids=[0])
    return got.results[0]["out_0"]
```
